# Optimizing a Trainium2 kernel written in Bass

```python
import numpy as np
import jax
import jax.numpy as jnp

def _softmax(x, axis=-1):
    return jax.nn.softmax(x, axis=axis)

def _gelu(x):
    return jax.nn.gelu(x, approximate=True)

def _silu(x):
    return jax.nn.silu(x)

def _sigmoid(x):
    return jax.nn.sigmoid(x)

def _layernorm(x, axis=-1, eps=1e-05):
    m = jnp.mean(x, axis=axis, keepdims=True)
    v = jnp.var(x, axis=axis, keepdims=True)
    return (x - m) / jnp.sqrt(v + eps)

def _scatter_add(tgt, idx, src, axis=0):
    return tgt.at[idx].add(src)

def _segment_sum(src, seg, n):
    return jax.ops.segment_sum(src, seg, n)
kernel_name = 'mk_hybrid_d1_jaxref_r8_85aea2'

def setup_inputs(seed: int=0):
    np.random.seed(seed)
    _w = jnp.asarray

    def _L0_attn_a_setup():
        import jax, jax.numpy as jnp
        import numpy as np
        B, S, E, H = (2, 256, 256, 16)
        D = E // H
        NEG = -1e+30

        def alibi_slopes(n_heads):
            return jnp.asarray(2.0 ** (-8.0 * np.arange(1, n_heads + 1) / n_heads), dtype=jnp.float32)
        key = jax.random.key(seed)
        ks = jax.random.split(key, 5)
        sc = 0.02
        return {'x': jax.random.normal(ks[0], (B, S, E), dtype=jnp.float32), 'Wq': jax.random.normal(ks[1], (E, E), dtype=jnp.float32) * sc, 'Wk': jax.random.normal(ks[2], (E, E), dtype=jnp.float32) * sc, 'Wv': jax.random.normal(ks[3], (E, E), dtype=jnp.float32) * sc, 'Wo': jax.random.normal(ks[4], (E, E), dtype=jnp.float32) * sc, 'bo': jnp.zeros((E,), dtype=jnp.float32)}
    _L0_attn_a_in = _L0_attn_a_setup()

    def _L0_attn_b_setup():
        import jax, jax.numpy as jnp
        import numpy as np
        B, S, D_IN = (2, 256, 256)
        D_OUT, DL, H = (256, 64, 16)
        DH = D_OUT // H
        key = jax.random.key(seed)
        ks = jax.random.split(key, 20)
        g = lambda k, shp: jax.random.normal(k, shp, dtype=jnp.float32) * 0.02
        return {'x': jax.random.normal(ks[0], (B, S, D_IN), dtype=jnp.float32), 'wq_w': g(ks[1], (D_IN, D_OUT)), 'wq_b': g(ks[2], (D_OUT,)), 'wk_w': g(ks[3], (D_IN, D_OUT)), 'wk_b': g(ks[4], (D_OUT,)), 'wkl_w': g(ks[5], (D_OUT, DL)), 'wkl_b': g(ks[6], (DL,)), 'wv_w': g(ks[7], (D_IN, D_OUT)), 'wv_b': g(ks[8], (D_OUT,)), 'wvl_w': g(ks[9], (D_OUT, DL)), 'wvl_b': g(ks[10], (DL,)), 'upk_w': g(ks[11], (H, DL, DH)), 'upk_b': g(ks[12], (H, DH)), 'upv_w': g(ks[13], (H, DL, DH)), 'upv_b': g(ks[14], (H, DH)), 'wo_w': g(ks[15], (D_OUT, D_OUT)), 'wo_b': g(ks[16], (D_OUT,))}
    _L0_attn_b_in = _L0_attn_b_setup()

    def _L0_ffn_setup():
        import jax, jax.numpy as jnp
        import numpy as np
        H = 256
        E = 64
        I = 64
        SI = 64
        TOP_K = 8
        B, T = (2, 64)
        key = jax.random.key(seed)
        ks = jax.random.split(key, 8)
        s = 0.02
        return {'h': jax.random.normal(ks[0], (B, T, H), jnp.float32), 'gate_w': jax.random.normal(ks[1], (E, H), jnp.float32) * s, 'gu_w': jax.random.normal(ks[2], (E, 2 * I, H), jnp.float32) * s, 'dp_w': jax.random.normal(ks[3], (E, H, I), jnp.float32) * s, 'sh_gate_w': jax.random.normal(ks[4], (SI, H), jnp.float32) * s, 'sh_up_w': jax.random.normal(ks[5], (SI, H), jnp.float32) * s, 'sh_down_w': jax.random.normal(ks[6], (H, SI), jnp.float32) * s, 'sh_gate1_w': jax.random.normal(ks[7], (1, H), jnp.float32) * s}
    _L0_ffn_in = _L0_ffn_setup()
    _d = {'L0_attn_a_x': _L0_attn_a_in['x'], 'L0_attn_a_Wq': _L0_attn_a_in['Wq'], 'L0_attn_a_Wk': _L0_attn_a_in['Wk'], 'L0_attn_a_Wv': _L0_attn_a_in['Wv'], 'L0_attn_a_Wo': _L0_attn_a_in['Wo'], 'L0_attn_a_bo': _L0_attn_a_in['bo'], 'L0_attn_b_wq_w': _L0_attn_b_in['wq_w'], 'L0_attn_b_wq_b': _L0_attn_b_in['wq_b'], 'L0_attn_b_wk_w': _L0_attn_b_in['wk_w'], 'L0_attn_b_wk_b': _L0_attn_b_in['wk_b'], 'L0_attn_b_wkl_w': _L0_attn_b_in['wkl_w'], 'L0_attn_b_wkl_b': _L0_attn_b_in['wkl_b'], 'L0_attn_b_wv_w': _L0_attn_b_in['wv_w'], 'L0_attn_b_wv_b': _L0_attn_b_in['wv_b'], 'L0_attn_b_wvl_w': _L0_attn_b_in['wvl_w'], 'L0_attn_b_wvl_b': _L0_attn_b_in['wvl_b'], 'L0_attn_b_upk_w': _L0_attn_b_in['upk_w'], 'L0_attn_b_upk_b': _L0_attn_b_in['upk_b'], 'L0_attn_b_upv_w': _L0_attn_b_in['upv_w'], 'L0_attn_b_upv_b': _L0_attn_b_in['upv_b'], 'L0_attn_b_wo_w': _L0_attn_b_in['wo_w'], 'L0_attn_b_wo_b': _L0_attn_b_in['wo_b'], 'L0_ffn_gate_w': _L0_ffn_in['gate_w'], 'L0_ffn_gu_w': _L0_ffn_in['gu_w'], 'L0_ffn_dp_w': _L0_ffn_in['dp_w'], 'L0_ffn_sh_gate_w': _L0_ffn_in['sh_gate_w'], 'L0_ffn_sh_up_w': _L0_ffn_in['sh_up_w'], 'L0_ffn_sh_down_w': _L0_ffn_in['sh_down_w'], 'L0_ffn_sh_gate1_w': _L0_ffn_in['sh_gate1_w']}
    _x0 = _d['L0_attn_a_x']
    _d['L0_attn_a_x'] = jax.random.normal(jax.random.fold_in(jax.random.key(seed), 1), (1, 2048, 256), dtype=_x0.dtype)
    del _x0
    return _d

def reference(L0_attn_a_x, L0_attn_a_Wq, L0_attn_a_Wk, L0_attn_a_Wv, L0_attn_a_Wo, L0_attn_a_bo, L0_attn_b_wq_w, L0_attn_b_wq_b, L0_attn_b_wk_w, L0_attn_b_wk_b, L0_attn_b_wkl_w, L0_attn_b_wkl_b, L0_attn_b_wv_w, L0_attn_b_wv_b, L0_attn_b_wvl_w, L0_attn_b_wvl_b, L0_attn_b_upk_w, L0_attn_b_upk_b, L0_attn_b_upv_w, L0_attn_b_upv_b, L0_attn_b_wo_w, L0_attn_b_wo_b, L0_ffn_gate_w, L0_ffn_gu_w, L0_ffn_dp_w, L0_ffn_sh_gate_w, L0_ffn_sh_up_w, L0_ffn_sh_down_w, L0_ffn_sh_gate1_w):

    def _L0_attn_a_ref(x, Wq, Wk, Wv, Wo, bo):
        import jax, jax.numpy as jnp
        import numpy as np
        B, S, E, H = (2, 256, 256, 16)
        D = E // H
        NEG = -1e+30

        def alibi_slopes(n_heads):
            return jnp.asarray(2.0 ** (-8.0 * np.arange(1, n_heads + 1) / n_heads), dtype=jnp.float32)
        b, s, e = x.shape
        q = (x @ Wq).reshape(b, s, H, D).transpose(0, 2, 1, 3)
        k = (x @ Wk).reshape(b, s, H, D).transpose(0, 2, 1, 3)
        v = (x @ Wv).reshape(b, s, H, D).transpose(0, 2, 1, 3)
        scores = jnp.einsum('bhqd,bhkd->bhqk', q, k)
        i = jnp.arange(s)[:, None]
        j = jnp.arange(s)[None, :]
        causal = j <= i
        scores = jnp.where(causal[None, None], scores, NEG)
        bias = alibi_slopes(H)[:, None, None] * (j - i).astype(jnp.float32)
        scores = scores + bias[None]
        scores = scores / jnp.sqrt(jnp.float32(D))
        w = jax.nn.softmax(scores, axis=-1)
        ctx = jnp.einsum('bhqk,bhkd->bqhd', w, v).reshape(b, s, e)
        return ctx @ Wo + bo

    def _L0_attn_b_ref(x, wq_w, wq_b, wk_w, wk_b, wkl_w, wkl_b, wv_w, wv_b, wvl_w, wvl_b, upk_w, upk_b, upv_w, upv_b, wo_w, wo_b):
        import jax, jax.numpy as jnp
        import numpy as np
        B, S, D_IN = (2, 256, 256)
        D_OUT, DL, H = (256, 64, 16)
        DH = D_OUT // H
        b, s, _ = x.shape
        k_lat = (x @ wk_w + wk_b) @ wkl_w + wkl_b
        v_lat = (x @ wv_w + wv_b) @ wvl_w + wvl_b
        q = (x @ wq_w + wq_b).reshape(b, s, H, DH).transpose(0, 2, 1, 3)
        k = jnp.einsum('bsl,hld->bhsd', k_lat, upk_w) + upk_b[None, :, None, :]
        v = jnp.einsum('bsl,hld->bhsd', v_lat, upv_w) + upv_b[None, :, None, :]
        scores = jnp.einsum('bhqd,bhkd->bhqk', q, k) / jnp.sqrt(jnp.float32(DH))
        causal = jnp.tril(jnp.ones((s, s), dtype=bool))
        scores = jnp.where(causal[None, None], scores, -jnp.inf)
        attn = jax.nn.softmax(scores, axis=-1)
        out = jnp.einsum('bhqk,bhkd->bhqd', attn, v)
        out = out.transpose(0, 2, 1, 3).reshape(b, s, D_OUT)
        return out @ wo_w + wo_b

    def _L0_ffn_ref(h, gate_w, gu_w, dp_w, sh_gate_w, sh_up_w, sh_down_w, sh_gate1_w):
        import jax, jax.numpy as jnp
        import numpy as np
        H = 256
        E = 64
        I = 64
        SI = 64
        TOP_K = 8
        B, T = (2, 64)
        Bb, Tt, Hh = h.shape
        x = h.reshape(Bb * Tt, Hh)
        N = x.shape[0]
        logits = x @ gate_w.T
        topv, topi = jax.lax.top_k(logits, TOP_K)
        rw = jax.nn.softmax(topv.astype(jnp.float32), axis=-1).astype(x.dtype)
        W = jnp.zeros((N, E), x.dtype).at[jnp.arange(N)[:, None], topi].set(rw)
        gu = jnp.einsum('nh,eih->nei', x, gu_w)
        gate, up = (gu[..., :I], gu[..., I:])
        inter = jax.nn.silu(gate) * up
        inter_w = inter * W[:, :, None]
        out = jnp.einsum('nei,ehi->nh', inter_w, dp_w)
        sh_inter = jax.nn.silu(x @ sh_gate_w.T) * (x @ sh_up_w.T)
        sh_out = sh_inter @ sh_down_w.T
        sh_g = jax.nn.sigmoid(x @ sh_gate1_w.T)
        out = out + sh_g * sh_out
        return out.reshape(Bb, Tt, Hh)
    x = L0_attn_a_x
    x = x + _L0_attn_a_ref(_layernorm(x, axis=-1), L0_attn_a_Wq, L0_attn_a_Wk, L0_attn_a_Wv, L0_attn_a_Wo, L0_attn_a_bo)
    x = x + _L0_ffn_ref(_layernorm(x, axis=-1), L0_ffn_gate_w, L0_ffn_gu_w, L0_ffn_dp_w, L0_ffn_sh_gate_w, L0_ffn_sh_up_w, L0_ffn_sh_down_w, L0_ffn_sh_gate1_w)
    x = x + _L0_attn_b_ref(_layernorm(x, axis=-1), L0_attn_b_wq_w, L0_attn_b_wq_b, L0_attn_b_wk_w, L0_attn_b_wk_b, L0_attn_b_wkl_w, L0_attn_b_wkl_b, L0_attn_b_wv_w, L0_attn_b_wv_b, L0_attn_b_wvl_w, L0_attn_b_wvl_b, L0_attn_b_upk_w, L0_attn_b_upk_b, L0_attn_b_upv_w, L0_attn_b_upv_b, L0_attn_b_wo_w, L0_attn_b_wo_b)
    x = x + _L0_ffn_ref(_layernorm(x, axis=-1), L0_ffn_gate_w, L0_ffn_gu_w, L0_ffn_dp_w, L0_ffn_sh_gate_w, L0_ffn_sh_up_w, L0_ffn_sh_down_w, L0_ffn_sh_gate1_w)
    return x

_drawn_inputs = setup_inputs


def setup_inputs(seed=0):
    import zlib

    import numpy as np

    out = dict(_drawn_inputs(seed))
    spreads = {'L0_attn_a_bo': (0.0, 0.1)}
    factors = {'L0_attn_a_Wq': 8.0,
     'L0_attn_a_Wk': 8.0,
     'L0_attn_a_Wv': 3.762,
     'L0_attn_a_Wo': 3.757,
     'L0_attn_b_wq_w': 8.0,
     'L0_attn_b_wq_b': 8.0,
     'L0_attn_b_wk_w': 8.0,
     'L0_attn_b_wk_b': 64.0,
     'L0_attn_b_wkl_w': 8.0,
     'L0_attn_b_wkl_b': 64.0,
     'L0_attn_b_wv_w': 8.0,
     'L0_attn_b_wv_b': 8.0,
     'L0_attn_b_wvl_w': 8.0,
     'L0_attn_b_wvl_b': 8.0,
     'L0_attn_b_upk_w': 8.0,
     'L0_attn_b_upk_b': 64.0,
     'L0_attn_b_upv_w': 8.0,
     'L0_attn_b_upv_b': 22.576,
     'L0_attn_b_wo_w': 8.0,
     'L0_attn_b_wo_b': 22.024,
     'L0_ffn_gate_w': 8.0,
     'L0_ffn_gu_w': 8.0,
     'L0_ffn_dp_w': 8.0,
     'L0_ffn_sh_gate_w': 6.824,
     'L0_ffn_sh_up_w': 6.871,
     'L0_ffn_sh_down_w': 6.846,
     'L0_ffn_sh_gate1_w': 8.0}
    for name, (base, spread) in spreads.items():
        noise = np.random.default_rng([zlib.crc32(name.encode()), seed]).standard_normal(out[name].shape)
        drawn = base * np.exp(spread * noise) if base else spread * noise
        out[name] = jnp.asarray(drawn.astype(out[name].dtype))
    for name, factor in factors.items():
        out[name] = (out[name] * factor).astype(out[name].dtype)
    return out
```

```python
from contextlib import ExitStack

import numpy as np

import concourse.bass as bass
from concourse import mybir

F32 = mybir.dt.float32
F32R = mybir.dt.float32r
BF16 = mybir.dt.bfloat16
ALU = mybir.AluOpType
ACT = mybir.ActivationFunctionType
AX = mybir.AxisListType

P = 128
S = 2048
E = 256
T = S // P
KC = E // P
QB = 512
NB = S // QB
TPB = QB // P
H = 16
D = E // H
DL = 64
EPS = 1e-5
NEG = -1e30
VLOW = -3e38

ROWS_HEAD = 3 * D
ROW_BIAS = 2 * ROWS_HEAD
ROW_MAX = ROW_BIAS + 2
ROWS = ROW_MAX + 4
GH = 4
G = H // GH
NP = 3
NMAX, NPV = 3, 1

NEXP = 64
EI = 64
TOPK = 8
GC = NEXP + 2
PAIRS = NEXP // 2
ROUTE_STEPS = T + 10
EW = KC * 2 * P + E
FB = 1024
NFB = S // FB


W_COLS = {"q": E, "k": E, "v": E, "kl": DL, "vl": DL, "upk": E, "upv": E}
W_CHUNKS = {"q": KC, "k": KC, "v": KC, "kl": KC, "vl": KC, "upk": 1, "upv": 1}
W_OFF, NWB = {}, 0
for _name in W_COLS:
    W_OFF[_name] = NWB
    NWB += W_COLS[_name] * W_CHUNKS[_name]
NWA = W_OFF["kl"]
W_ORDER = [["q", "k", "v"], ["q", "k", "kl", "upk", "v", "vl", "upv"]]


def core_plan():
    SIGNAL, ROWS_BACK, LOAD = 250, 3600, 12000

    maxima = []
    for g in range(G):
        for b in range(NB):
            if (g, b) != (0, 0):
                pending = ("turn", *divmod(g * NB + b - 1, NB))
            else:
                pending = None
            for t in range(b * TPB, (b + 1) * TPB):
                for h in range(GH):
                    for c in range(t // TPB + 1):
                        maxima.append(("max", g, h, t, c))
                        if pending and len(maxima) and (h, t, c) == (1, b * TPB, 0):
                            maxima.append(pending)
    maxima.append(("turn", G - 1, NB - 1))
    units = [(g, b, j) for g in range(G) for b in range(NB) for j in range(TPB * (b + 1))]
    scores = [("qk", g, b, j, p, e) for e, (g, b, j) in enumerate(units) for p in range(2)]
    sums = [("pv", g, b, j, e) for e, (g, b, j) in enumerate(units)]
    contexts = [("ctx", g, b) for g in range(G) for b in range(NB)]
    streams = [contexts, maxima, scores, sums]
    at = [0] * 4

    plan = []
    pe = dve = act = 0.0
    max_bank_free = [0.0] * NMAX
    exp_bank_free = [0.0] * 2
    uses = 0
    reduced, turned, loaded = {}, {}, {0: 0.0, 1: 0.0}
    exps, products, scored, summed = {}, {}, {}, {}

    def width(b, j):
        return QB - P * max(0, j - TPB * b)

    def ready(item):
        kind, g = item[0], item[1]
        if kind in ("max", "turn", "ctx"):
            bank = max_bank_free[uses % NMAX]
            if kind == "max":
                return max(bank, loaded[g]) if g in loaded else None
            if kind == "turn":
                return max(bank, reduced[item[1:]]) if item[1:] in reduced else None
            return max(bank, summed[item[1:]]) if item[1:] in summed else None
        if kind == "qk":
            return max(exp_bank_free[item[4]], turned[item[1:3]]) if item[1:3] in turned and \
                (item[5] < NP or item[5] - NP in products) else None
        n = item[1] * NB + item[2]
        if item[3] == TPB * (item[2] + 1) - 1 and n - 2 >= at[0]:
            return None
        return exps.get((item[4], 1))

    while any(at[k] < len(s) for k, s in enumerate(streams)):
        best = None
        for k, s in enumerate(streams):
            if at[k] < len(s):
                when = ready(s[at[k]])
                if when is not None:
                    when = max(when, pe)
                    if best is None or when < best[0]:
                        best = (when, k)
        start, k = best
        item = streams[k][at[k]]
        at[k] += 1
        plan.append(item)
        kind, g = item[0], item[1]
        if kind == "max":
            _, g, h, t, c = item
            n = min(QB, P * (t + 1) - QB * c)
            pe = start + n / 2.4 + 3
            dve = max(dve, pe + SIGNAL) + n / 0.96 + 75
            max_bank_free[uses % NMAX] = dve + 50
            uses += 1
            if h == GH - 1 and t % TPB == TPB - 1 and c == t // TPB:
                dve += 250
                reduced[g, t // TPB] = dve + 50
        elif kind == "turn":
            pe = start + 110
            dve = max(dve, pe + SIGNAL) + 600
            max_bank_free[uses % NMAX] = dve + 50
            uses += 1
            turned[item[1:]] = dve + ROWS_BACK
        elif kind == "ctx":
            pe = start + 450
            dve = max(dve, pe + SIGNAL) + 550
            max_bank_free[uses % NMAX] = dve + 50
            uses += 1
        elif kind == "qk":
            _, g, b, j, p, e = item
            n = width(b, j)
            pe = start + 2 * (n / 2.4 + 3) + (120 if j >= TPB * b else 0)
            free = products[e - NP] if e >= NP else 0
            act = max(act, pe + SIGNAL, free) + 2 * n / 1.2 + 60
            exp_bank_free[p] = act + 50
            exps[e, p] = act + 50
            if j == T - 1 and p == 1 and g + 2 < G:
                loaded[g + 2] = max(pe, turned[g + 1, NB - 2] if (g + 1, NB - 2) in turned else pe) + LOAD
        elif kind == "pv":
            _, g, b, j, e = item
            n = width(b, j)
            pe = start + 4 * (n / 2.4 + 3) + 100
            products[e] = pe + SIGNAL
            if j == TPB * (b + 1) - 1:
                act = max(act, pe + SIGNAL) + 600
                summed[g, b] = act + 50
                plan.append(("out", g, b))
    return plan


def build(nc, A, parts="afbf"):
    plan = core_plan()
    ctx = ExitStack()
    with ctx:
        def sem(name):
            return ctx.enter_context(nc.semaphore(name))

        def tile(name, shape, dt=F32, stack=ctx):
            return stack.enter_context(nc.sbuf_tensor(f"{name}_t", shape, dt))

        exp_banks = [ctx.enter_context(nc.psum_tensor(f"exp_banks{i}", [P, 2, QB], F32)) for i in range(2)]
        max_banks = [ctx.enter_context(nc.psum_tensor(f"max_bank{i}", [P, QB], F32)) for i in range(NMAX)]
        pv_banks = [ctx.enter_context(nc.psum_tensor(f"pv_bank{i}", [P, QB], F32)) for i in range(NPV)]
        BANK = [exp_banks[0][:, 0, :], exp_banks[0][:, 1, :], exp_banks[1][:, 0, :], exp_banks[1][:, 1, :],
                *(bank[:, :] for bank in max_banks + pv_banks)]
        NBANK = len(BANK)

        x = tile("x_sb", [P, T, E])
        ident = tile("ident", [P, P])
        ones = tile("ones", [P, 1])
        diag_mask = tile("diag_mask", [P, QB])
        ident16 = tile("ident16", [P, P], BF16)
        cut16 = tile("cut16", [P, P], BF16)
        values = tile("values", [P, T, H, 2 * D])
        w_post_raw = tile("w_post_raw", [P, KC * E])
        w_post = tile("w_post", [P, 2, KC, E], F32R)
        bias_cols = tile("bias_cols", [P, 10])
        bias_rows = tile("bias_rows", [P, 3, E])
        stats = tile("stats", [P, T, 6])
        mean_var = tile("mean_var", [P, T, 2])
        var_eps = tile("var_eps", [P, T])
        std = tile("std", [P, T])
        rstd = tile("rstd", [P, T])

        outer = ExitStack()
        xT = tile("xT", [P, 2, KC, S], F32R, outer)
        xn = tile("xn", [P, T, E], F32, outer)
        pre = ExitStack()
        mid = tile("mid", [P, 2, KC, S], F32R, pre)
        lat = tile("lat", [DL, 2, S], F32R, pre)
        part_hi = [tile(f"part_hi{i}", [P, QB], F32R, pre) for i in range(2)]
        part_lo = [tile(f"part_lo{i}", [P, QB], F32R, pre) for i in range(2)]
        w_raw = tile("w_raw", [P, NWB], F32, pre)
        w_hi = tile("w_hi", [P, NWB], F32R, pre)
        w_lo = tile("w_lo", [P, NWB], F32R, pre)
        slope_raw = tile("slope_raw", [P, S * H // P], F32, pre)
        slope_hi = tile("slope_hi", [P, S * H // P], F32R, pre)
        slope_lo = tile("slope_lo", [P, S * H // P], F32R, pre)
        fill = tile("fill", [ROWS_HEAD, 2, QB], F32R, pre)
        pre.close()
        moe = ExitStack()
        g_raw = tile("g_raw", [P, KC * GC], F32, moe)
        g_hi = tile("g_hi", [P, KC * GC], F32R, moe)
        g_lo = tile("g_lo", [P, KC * GC], F32R, moe)
        logits = tile("logits", [P, T, GC], F32, moe)
        top = tile("top", [P, T, TOPK], F32, moe)
        route = tile("route", [P, T, GC], F32, moe)
        chosen = tile("chosen", [P, T, NEXP], F32, moe)
        route_sum = tile("route_sum", [P, T], F32, moe)
        route_inv = tile("route_inv", [P, T], F32, moe)
        route_rows_sb = tile("route_rows_sb", [GC, S], F32, moe)
        e_raw = [tile(f"e_raw{i}", [P, EW], F32, moe) for i in range(3)]
        e_hi = [tile(f"e_hi{i}", [P, EW], F32R, moe) for i in range(3)]
        e_lo = [tile(f"e_lo{i}", [P, EW], F32R, moe) for i in range(3)]
        wide = [tile(f"wide{i}", [P, FB], F32, moe) for i in range(2)]
        silu = [tile(f"silu{i}", [P, QB], F32, moe) for i in range(2)]
        inter = [tile(f"inter{i}", [P, QB], F32, moe) for i in range(2)]
        i_hi = [tile(f"i_hi{i}", [P, QB], F32R, moe) for i in range(2)]
        i_lo = [tile(f"i_lo{i}", [P, QB], F32R, moe) for i in range(2)]
        moe_out = tile("moe_out", [P, KC, FB], F32, moe)
        moe.close()
        outer.close()

        core = ExitStack()
        Qp = [tile(f"Qp{s}", [P, 2, S], F32R, core) for s in range(2)]
        Kp = [tile(f"Kp{s}", [P, 2, 2, S], F32R, core) for s in range(2)]
        probs = tile("probs", [P, NP, GH, QB], F32, core)
        context = tile("context", [P, T, E], F32, core)
        masked = [tile(f"masked{i}", [P, QB], F32, core) for i in range(2)]
        chunk_max = tile("chunk_max", [P, 2, GH, TPB, NB], F32, core)
        neg_max = tile("neg_max", [P, 2, GH, TPB], F32, core)
        neg_hi = tile("neg_hi", [GH * TPB, 2, P], F32R, core)
        neg_lo = tile("neg_lo", [GH * TPB, 2, P], F32R, core)
        sums = tile("sums", [P, 2, QB], F32, core)
        inv_den = tile("inv_den", [P, 2, TPB * GH], F32, core)
        core.close()

        q_parts = nc.dram_tensor("q_parts", [H, ROWS_HEAD, S], F32).ap()
        k_parts = nc.dram_tensor("k_parts", [H, ROWS_HEAD, S], F32).ap()
        slope_parts = nc.dram_tensor("slope_parts", [H, 2, S], F32).ap()
        const_rows = nc.dram_tensor("const_rows", [2, ROWS_HEAD, S], F32).ap()
        route_rows = [nc.dram_tensor(f"route_rows{f}", [GC, S], F32).ap() for f in range(2)]

        x_in = sem("x_in")
        consts_in = sem("consts_in")
        w_in = sem("w_in")
        wpost_in = sem("wpost_in")
        set_zero = sem("set_zero")
        ident_ready = sem("ident_ready")
        fill_ready = sem("fill_ready")
        w_high = sem("w_high")
        w_split = sem("w_split")
        wpost_split = sem("wpost_split")
        const_out = sem("const_out")
        slopes_ready = sem("slopes_ready")
        stats_done = sem("stats_done")
        aggr_done = sem("aggr_done")
        eps_done = sem("eps_done")
        std_done = sem("std_done")
        rstd_done = sem("rstd_done")
        xn_done = sem("xn_done")
        product = sem("product")
        hi_done = sem("hi_done")
        bank_free = sem("bank_free")
        part_out = [sem(f"part_out{i}") for i in range(2)]
        ops_in = [sem(f"ops_in{i}") for i in range(2)]
        max_product = sem("max_product")
        max_free = sem("max_free")
        neg_done = sem("neg_done")
        neg_high = sem("neg_high")
        neg_in = sem("neg_in")
        qk_product = sem("qk_product")
        exp_done = sem("exp_done")
        pv_done = sem("pv_done")
        sums_out = sem("sums_out")
        inv_done = sem("inv_done")
        bias_added = sem("bias_added")
        g_in = sem("g_in")
        g_split = sem("g_split")
        top_done = sem("top_done")
        route_step = sem("route_step")
        route_exp = sem("route_exp")
        rows_out = sem("rows_out")
        raw_in = [sem(f"raw_in{i}") for i in range(3)]
        wide_in = [sem(f"wide_in{i}") for i in range(2)]
        gu_high = sem("gu_high")
        gu_split = sem("gu_split")
        dn_high = sem("dn_high")
        dn_split = sem("dn_split")
        gu_product = sem("gu_product")
        silu_done = sem("silu_done")
        gated = sem("gated")
        weighted = sem("weighted")
        i_high = sem("i_high")
        i_split = sem("i_split")
        down_done = sem("down_done")
        moe_sums = sem("moe_sums")
        x_out = sem("x_out")

        STAGES = {("a", 0): [("T", 8), ("Q", 8), ("K", 8), ("V", 8), ("C", 8), ("O", 8)],
                  ("b", 1): [("T", 8), ("Q", 8), ("K1", 8), ("KL", 4), ("K", 8), ("V1", 8), ("VL", 4), ("V", 8),
                             ("C", 8), ("O", 8)],
                  "f": [("T", 8), ("R", 4), ("W", 4), ("F0", 4), ("F1", 4)]}
        WITH_HI = {"T", "Q", "K", "K1", "KL", "V1", "VL", "C"}
        first_unit, first_hi, norm_of, phases = {}, {}, {}, []
        u = hi = 0
        for i, kind in enumerate(parts):
            n = parts[:i].count("f") if kind == "f" else "ab".index(kind)
            phases.append((kind, n))
            norm_of[kind, n] = i
            for name, count in STAGES["f"] if kind == "f" else STAGES[kind, n]:
                first_unit[kind, n, name], first_hi[kind, n, name] = u, hi
                u += count
                hi += count * (name in WITH_HI)
        total_units = u
        LAYER = ["a", "b"]
        bias_of_col = {"q": 0, "k": 2, "v": 4, "upk": 6, "kl": 8, "vl": 9}

        def w_ready(layer, name):
            return sum(len(W_ORDER[i]) for i in range(layer)) + W_ORDER[layer].index(name) + 1

        def weight(part, name, k, cols, rows=P):
            at = W_OFF[name] + k * W_COLS[name]
            return part[0:rows, at + cols.start:at + cols.stop]

        e_of = {}
        n = 0
        for layer in range(2):
            for g in range(G):
                for b in range(NB):
                    for j in range(TPB * (b + 1)):
                        e_of[layer, g, b, j] = n
                        n += 1
        mu_of = {}
        for item in plan:
            if item[0] in ("max", "turn", "ctx"):
                mu_of[item] = len(mu_of)
        MU = len(mu_of)

        def block_no(layer, g, b):
            return (layer * G + g) * NB + b

        FRESH_LOADS, GROUP_LOADS = 2 * (3 + 8), 2 * 5
        HU = 2 * (PAIRS + 1)

        def split_base(f, fb):
            return f * (1 + NFB * PAIRS) + 1 + fb * PAIRS

        def unit_base(f, fb):
            return (f * NFB + fb) * HU

        def in_block(t, part):
            return lambda i: t[:, part, i // NB, (i % NB) * QB:(i % NB + 1) * QB]

        def in_lat(part):
            return lambda i: lat[:, part, i * QB:(i + 1) * QB]

        def staged(layer, name, tiles):
            return lambda i: tiles[(layer * 4 * NB + (name == "K") * 2 * NB + i) % 2][:, :]

        def bias_col(name, rows=P):
            return lambda i: bias_cols[0:rows, bias_of_col[name] + i // NB:bias_of_col[name] + i // NB + 1]

        block = ctx.enter_context(nc.Block())

        def experts_dma(sp, f):
            sp.wait_ge(product, first_unit["f", f, "T"] - 8)
            sp.dma_start(g_raw[:, :], A["router"]).then_inc(g_in, 16)
            sp.dma_start(e_raw[2][:, :], A["experts"][PAIRS]).then_inc(raw_in[2], 16)

            def load_raw(fb, q, k, first=False):
                if not first:
                    sp.wait_ge(dn_split, split_base(f, fb) + q - 1)
                sp.dma_start(e_raw[k][:, :], A["experts"][q]).then_inc(raw_in[k], 16)

            def load_wide(fb, q, k, value):
                if value is not None:
                    sp.wait_ge(weighted, value)
                rows = route_rows[f][bass.ds(2 * q, 2), fb * FB:(fb + 1) * FB]
                sp.dma_start(wide[k][:, :],
                             rows.rearrange("e (o c) -> e o c", o=1).broadcast_to([2, EI, FB])).then_inc(wide_in[k], 16)

            for fb in range(NFB):
                at = unit_base(f, fb)
                for k in range(2):
                    load_raw(fb, k, k, first=(f == 0 and fb == 0 and k == 0))
                if fb == 0:
                    sp.wait_ge(bank_free, first_unit["f", f, "F0"])
                    sp.dma_start(route_rows[f][:, :], route_rows_sb[:, :]).then_inc(rows_out, 16)
                    sp.wait_ge(rows_out, 16 * (f + 1))
                for k in range(2):
                    load_wide(fb, k, k, at - 2 * k if at else None)
                with sp.Fori(1, PAIRS // 2) as i:
                    for k in range(2):
                        load_raw(fb, 2 * i + k, k)
                        load_wide(fb, 2 * i + k, k, at + 4 * i + 2 * k - 2)
                load_wide(fb, PAIRS, 0, at + 2 * PAIRS - 2)

        @block.sync
        def _(sp):
            for t in range(T):
                sp.dma_start(x[:, t, :], A["x"][t * P:(t + 1) * P, :]).then_inc(x_in, 16)
            sp.dma_start(w_raw[:, 0:NWA], A["w_a"]).then_inc(w_in, 16)
            sp.dma_start(bias_cols[:, :], A["bias_cols"]).then_inc(consts_in, 16)
            sp.dma_start(bias_rows[:, :, :], A["bias_rows"].rearrange("(a r) e -> a r e", a=1)
                         .broadcast_to([P, 3, E])).then_inc(consts_in, 16)
            sp.dma_start(slope_raw[:, :], A["slopes"]).then_inc(consts_in, 16)
            sp.dma_start(w_post_raw[:, :], A["w_a_post"]).then_inc(wpost_in, 16)
            sp.wait_ge(slopes_ready, 2)
            for i, part in enumerate((slope_hi, slope_lo)):
                sp.dma_start(slope_parts[:, i, :].rearrange("h (k c) -> h k c", k=P // H),
                             part[:, :].bitcast(F32)).then_inc(const_out, 16)
            sp.wait_ge(fill_ready, 3)
            for i in range(2):
                for c in range(NB):
                    sp.dma_start(const_rows[i, :, c * QB:(c + 1) * QB], fill[:, i, :].bitcast(F32)).then_inc(const_out, 16)

            def attention(kind, layer):
                if layer == 1:
                    sp.wait_ge(product, first_unit[kind, layer, "T"])
                    sp.dma_start(w_raw[:, :], A["w_b"]).then_inc(w_in, 16)
                    sp.dma_start(w_post_raw[:, :], A["w_b_post"]).then_inc(wpost_in, 16)
                for s, (name, dst) in enumerate((("Q", q_parts), ("K", k_parts))):
                    for i in range(2 * NB):
                        m, b = i // NB, i % NB
                        n = layer * 4 * NB + s * 2 * NB + i
                        sp.wait_ge(bank_free, first_unit[kind, layer, name] + i + 1)
                        out = dst[m * 8:(m + 1) * 8, :, b * QB:(b + 1) * QB]
                        order = (part_hi, part_hi, part_lo) if name == "Q" else (part_hi, part_lo, part_hi)
                        for r, part in enumerate(order):
                            sp.dma_start(out[:, r * D:(r + 1) * D, :], part[n % 2][:, :].bitcast(F32)).then_inc(part_out[n % 2], 16)

                def load_fresh(s):
                    for p in range(2):
                        sp.dma_start(Qp[s][ROW_BIAS:ROW_MAX, p, :].bitcast(F32), const_rows[1, 0:2, :]).then_inc(ops_in[s], 16)
                        sp.dma_start(Kp[s][ROWS_HEAD:2 * ROWS_HEAD, p, 0, :].bitcast(F32), const_rows[0, :, :]).then_inc(ops_in[s], 16)
                        sp.dma_start(Kp[s][0:ROWS_HEAD, p, 1, :].bitcast(F32), const_rows[0, :, :]).then_inc(ops_in[s], 16)
                        for hh in range(2):
                            for r in (ROW_MAX, ROW_MAX + 2):
                                sp.dma_start(Kp[s][r + hh:r + hh + 1, p, hh, :].bitcast(F32), const_rows[1, 0:1, :]).then_inc(ops_in[s], 16)
                                sp.dma_start(Kp[s][r + 1 - hh:r + 2 - hh, p, hh, :].bitcast(F32), const_rows[0, 0:1, :]).then_inc(ops_in[s], 16)

                def load_group(g):
                    s = g % 2
                    for p in range(2):
                        h0 = GH * g + 2 * p
                        sp.dma_start(Qp[s][0:2 * ROWS_HEAD, p, :].bitcast(F32),
                                     q_parts[h0:h0 + 2, :, :].rearrange("h r s -> (h r) s")).then_inc(ops_in[s], 16)
                        for hh in range(2):
                            sp.dma_start(Kp[s][hh * ROWS_HEAD:(hh + 1) * ROWS_HEAD, p, hh, :].bitcast(F32),
                                         k_parts[h0 + hh, :, :]).then_inc(ops_in[s], 16)
                            bias = slope_parts[h0 + hh, :, :] if layer == 0 else const_rows[0, 0:2, :]
                            sp.dma_start(Kp[s][ROW_BIAS:ROW_MAX, p, hh, :].bitcast(F32), bias).then_inc(ops_in[s], 16)

                if layer == 0:
                    sp.wait_ge(const_out, 16 * (2 + 2 * NB))
                sp.wait_ge(product, first_unit[kind, layer, "V"] + 8)
                sp.wait_ge(bank_free, first_unit[kind, layer, "V"] + 8)
                for i in range(2):
                    sp.wait_ge(part_out[i], 16 * 3 * 2 * NB * (layer + 1))
                for s in range(2):
                    load_fresh(s)
                    load_group(s)
                for g in range(G):
                    for b in range(NB):
                        n = block_no(layer, g, b)
                        s = g % 2
                        sp.wait_ge(max_free, layer * MU + mu_of["turn", g, b] + 1)
                        for p in range(2):
                            for r, rows in ((ROW_MAX, neg_hi), (ROW_MAX + 2, neg_lo)):
                                sp.dma_start(Qp[s][r:r + 2, p, b * QB:(b + 1) * QB].bitcast(F32),
                                             rows[8 * p:8 * p + 8, n % 2, :].bitcast(F32)).then_inc(neg_in, 16)
                        sp.wait_ge(neg_in, 64 * (n + 1))
                        if b == NB - 2 and 1 <= g < G - 1:
                            sp.wait_ge(qk_product, 2 * (e_of[layer, g - 1, NB - 1, T - 1] + 1))
                            load_group(g + 1)

            for kind, n in phases:
                if kind != "f":
                    attention(kind, n)
                else:
                    experts_dma(sp, n)
            sp.wait_ge(bank_free, total_units)
            for t in range(T):
                sp.dma_start(A["out"][t * P:(t + 1) * P, :], x[:, t, :]).then_inc(x_out, 16)
            sp.wait_ge(x_out, 16 * T)

        def experts_pool(pool, f):
            pool.wait_ge(g_in, 16 * (f + 1))
            pool.tensor_copy(g_hi[:, :], g_raw[:, :]).then_inc(g_split, 1)
            pool.wait_ge(g_split, 2 * f + 1)
            pool.tensor_tensor(g_lo[:, :], g_raw[:, :], g_hi[:, :].bitcast(F32), ALU.subtract).then_inc(g_split, 1)

            def split(k, cols, high, low, value):
                pool.tensor_tensor(e_hi[k][:, cols], e_raw[k][:, cols], ones[:, :].broadcast_to([P, cols.stop - cols.start]),
                                   ALU.mult).then_inc(high, 1)
                pool.wait_ge(high, value)
                pool.tensor_tensor(e_lo[k][:, cols], e_raw[k][:, cols], e_hi[k][:, cols].bitcast(F32), ALU.subtract)\
                    .then_inc(low, 1)

            GU, DN = slice(0, EW - E), slice(EW - E, EW)
            pool.wait_ge(raw_in[2], 16 * (f + 1))
            split(2, GU, gu_high, gu_split, split_base(f, 0))
            split(2, DN, dn_high, dn_split, split_base(f, 0))
            for fb in range(NFB):
                at, sb = unit_base(f, fb), split_base(f, fb)
                loads = (f * NFB + fb) * PAIRS // 2

                def pair(i, k, used):
                    pool.wait_ge(raw_in[k], 16 * (loads + 1 + i))
                    if used is not None:
                        pool.wait_ge(gu_product, used)
                    split(k, GU, gu_high, gu_split, sb + 2 * i + k + 1)
                    if used is not None:
                        pool.wait_ge(down_done, used)
                    split(k, DN, dn_high, dn_split, sb + 2 * i + k + 1)

                for k in range(2):
                    pair(0, k, at - 4 + 2 * k if at else None)
                with pool.Fori(1, PAIRS // 2) as i:
                    for k in range(2):
                        pair(i, k, at + 4 * i + 2 * k - 2)

        @block.gpsimd
        def _(pool):
            pool.memset(ident[:, :], 0.0).then_inc(set_zero, 1)
            pool.memset(diag_mask[:, :], 0.0).then_inc(set_zero, 1)
            pool.memset(cut16[:, :], 0.0).then_inc(set_zero, 1)
            pool.wait_ge(set_zero, 3)
            pool.affine_select(out=ident[:, :], in_=ident[:, :], compare_op=ALU.not_equal, fill=1.0, base=0,
                               pattern=[[-1, P]], channel_multiplier=1).then_inc(ident_ready, 1)
            pool.affine_select(out=diag_mask[:, QB - P:QB], in_=diag_mask[:, QB - P:QB], compare_op=ALU.is_ge,
                               fill=NEG, base=0, pattern=[[-1, P]], channel_multiplier=1).then_inc(ident_ready, 1)
            pool.affine_select(out=cut16[:, :], in_=cut16[:, :], compare_op=ALU.is_ge, fill=NEG, base=0,
                               pattern=[[1, P]], channel_multiplier=-1).then_inc(ident_ready, 1)
            pool.wait_ge(ident_ready, 1)
            pool.tensor_copy(ident16[:, :], ident[:, :]).then_inc(ident_ready, 1)
            pool.memset(ones[:, :], 1.0).then_inc(fill_ready, 1)
            pool.memset(fill[:, 0, :].bitcast(F32), 0.0).then_inc(fill_ready, 1)
            pool.memset(fill[:, 1, :].bitcast(F32), 1.0).then_inc(fill_ready, 1)

            def attention(kind, layer):
                pool.wait_ge(fill_ready, 1)
                pool.wait_ge(w_in, 16 * (layer + 1))
                for name in W_ORDER[layer]:
                    cols = slice(W_OFF[name], W_OFF[name] + W_CHUNKS[name] * W_COLS[name])
                    pool.tensor_tensor(w_hi[:, cols], w_raw[:, cols], ones[:, :].broadcast_to([P, cols.stop - cols.start]),
                                       ALU.mult).then_inc(w_high, 1)
                    pool.wait_ge(w_high, w_ready(layer, name))
                    pool.tensor_tensor(w_lo[:, cols], w_raw[:, cols], w_hi[:, cols].bitcast(F32), ALU.subtract)\
                        .then_inc(w_split, 1)
                if layer == 0:
                    pool.memset(values[:, :, :, D:2 * D], 0.0).then_inc(set_zero, 1)
                    pool.wait_ge(set_zero, 4)
                    pool.memset(values[:, :, :, D:D + 1], 1.0).then_inc(ident_ready, 1)
                pool.wait_ge(wpost_in, 16 * (layer + 1))
                wp = w_post_raw[:, :].rearrange("p (k e) -> p k e", k=KC)
                pool.tensor_copy(w_post[:, 0, :, :], wp).then_inc(wpost_split, 1)
                pool.wait_ge(wpost_split, 2 * layer + 1)
                pool.tensor_tensor(w_post[:, 1, :, :], wp, w_post[:, 0, :, :].bitcast(F32), ALU.subtract)\
                    .then_inc(wpost_split, 1)
                pool.wait_ge(consts_in, 48)
                pool.wait_ge(xn_done, T * (norm_of[kind, layer] + 1))
                pool.tensor_tensor(x[:, :, :], x[:, :, :], bias_rows[:, layer:layer + 1, :].broadcast_to([P, T, E]),
                                   ALU.add).then_inc(bias_added, 1)

            for kind, n in phases:
                if kind != "f":
                    attention(kind, n)
                else:
                    experts_pool(pool, n)

        def experts_act(act, f, norm, high_parts):
            phase = ("f", f)
            norm(phase)
            high_parts(phase, "T", 2 * NB, in_block(xT, 0))
            act.wait_ge(route_step, ROUTE_STEPS * f + 2)
            act.activation(route[:, :, :], route[:, :, :], ACT.Exp).then_inc(route_exp, 1)
            for fb in range(NFB):
                at = unit_base(f, fb)

                def unit(v, s, first=False):
                    act.wait_ge(gu_product, at + v + 1)
                    if not first:
                        act.wait_ge(gated, at + v - 1)
                    act.activation(silu[s][:, :], BANK[2 * s], ACT.Silu).then_inc(silu_done, 1)
                    act.wait_ge(weighted, at + v + 1)
                    if not first:
                        act.wait_ge(down_done, at + v - 1)
                    act.activation(i_hi[s][:, :], inter[s][:, :], ACT.Copy).then_inc(i_high, 1)

                for v in range(4):
                    unit(v, v % 2, first=(at == 0 and v < 2))
                with act.Fori(1, PAIRS // 2) as i:
                    for r in range(4):
                        unit(4 * i + r, r % 2)
                for v in range(2 * PAIRS, HU):
                    unit(v, v % 2)
                act.wait_ge(down_done, at + HU)
                if fb:
                    act.wait_ge(product, first_unit["f", f, "F0"] + 4)
                for n in range(2 * KC):
                    act.activation(moe_out[:, n // 2, (n % 2) * QB:(n % 2 + 1) * QB], BANK[4 + n], ACT.Copy)\
                        .then_inc(moe_sums, 1)

        @block.scalar
        def _(act):
            def high_parts(phase, name, count, dst, bias=None, rows=P):
                for i in range(count):
                    u = first_unit[(*phase, name)] + i
                    act.wait_ge(product, u + 1)
                    if name in ("Q", "K"):
                        n = phase[1] * 4 * NB + (name == "K") * 2 * NB + i
                        if n >= 2:
                            act.wait_ge(part_out[n % 2], 48 * (n // 2))
                    bank = BANK[u % NBANK][0:rows, :]
                    if bias is None:
                        act.activation(dst(i), bank, ACT.Copy).then_inc(hi_done, 1)
                    else:
                        act.activation(dst(i), bank, ACT.Identity, bias=bias(i)).then_inc(hi_done, 1)

            def norm(phase):
                act.wait_ge(eps_done, norm_of[phase] + 1)
                act.activation(std[:, :], var_eps[:, :], ACT.Sqrt).then_inc(std_done, 1)

            def attention(kind, layer):
                phase = (kind, layer)
                norm(phase)
                high_parts(phase, "T", 2 * NB, in_block(xT, 0))
                if layer == 0:
                    high_parts(phase, "Q", 2 * NB, staged(layer, "Q", part_hi))
                    high_parts(phase, "K", 2 * NB, staged(layer, "K", part_hi))
                else:
                    high_parts(phase, "Q", 2 * NB, staged(layer, "Q", part_hi), bias_col("q"))
                    high_parts(phase, "K1", 2 * NB, in_block(mid, 0), bias_col("k"))
                    high_parts(phase, "KL", NB, in_lat(0), bias_col("kl", DL), DL)
                    high_parts(phase, "K", 2 * NB, staged(layer, "K", part_hi), bias_col("upk"))
                    high_parts(phase, "V1", 2 * NB, in_block(mid, 0), bias_col("v"))
                    high_parts(phase, "VL", NB, in_lat(0), bias_col("vl", DL), DL)
                act.wait_ge(product, first_unit[kind, layer, "V"] + 8)
                act.wait_ge(bank_free, first_unit[kind, layer, "V"] + 8)
                for item in plan:
                    if item[0] == "qk":
                        _, g, b, j, p, _ = item
                        e = e_of[layer, g, b, j]
                        off = P * max(0, j - TPB * b)
                        act.wait_ge(qk_product, 2 * e + p + 1)
                        if e >= NP:
                            act.wait_ge(pv_done, e - NP + 1)
                        act.activation(probs[:, e % NP, 2 * p:2 * p + 2, off:QB], exp_banks[p][:, :, off:QB],
                                       ACT.Exp, scale=D ** -0.5).then_inc(exp_done, 1)
                    elif item[0] == "out":
                        _, g, b = item
                        n = block_no(layer, g, b)
                        act.wait_ge(pv_done, e_of[layer, g, b, TPB * (b + 1) - 1] + 1)
                        if n % (G * NB) >= 2:
                            before = (g * NB + b - 2) // NB, (g * NB + b - 2) % NB
                            act.wait_ge(max_product, layer * MU + mu_of["ctx", before[0], before[1]] + 1)
                        act.activation(sums[:, n % 2, :], pv_banks[n % NPV][:, :], ACT.Copy).then_inc(sums_out, 1)
                high_parts(phase, "C", 2 * NB, in_block(xT, 0))

            act.wait_ge(consts_in, 48)
            act.activation(slope_hi[:, :], slope_raw[:, :], ACT.Copy).then_inc(slopes_ready, 1)
            for kind, n in phases:
                if kind != "f":
                    attention(kind, n)
                else:
                    experts_act(act, n, norm, high_parts)

        def experts_pe(pe, f, turn, bank_of, three_passes):
            phase = ("f", f)
            turn(phase, "T", xn, lambda b: pe.wait_ge(xn_done, T * norm_of[phase] + (b + 1) * TPB))
            pe.wait_ge(bank_free, first_unit["f", f, "T"] + 2 * NB)
            pe.wait_ge(g_split, 2 * (f + 1))
            for i in range(NB):
                bank = bank_of(first_unit["f", f, "R"] + i)
                for t in range(TPB):
                    cols = slice((i * TPB + t) * P, (i * TPB + t + 1) * P)
                    last = three_passes(bank[:, t * P:t * P + GC], lambda a, k: xT[:, a, k, cols],
                                        lambda c, k: (g_hi, g_lo)[c][:, k * GC:(k + 1) * GC], KC)
                last.then_inc(product, 1)
            pe.wait_ge(route_step, ROUTE_STEPS * (f + 1))
            for i in range(NB):
                bank = bank_of(first_unit["f", f, "W"] + i)
                for t in range(TPB):
                    last = pe.transpose(bank[0:GC, t * P:(t + 1) * P], route[:, i * TPB + t, :], ident[:, :])
                last.then_inc(product, 1)
            for fb in range(NFB):
                at, sb = unit_base(f, fb), split_base(f, fb)
                pe.wait_ge(bank_free, first_unit["f", f, f"F{fb}"])

                def gate_up(v, k, s, new_pair, split_value, first=False):
                    if new_pair:
                        pe.wait_ge(gu_split, split_value)
                    if not first:
                        pe.wait_ge(gated, at + v - 1)
                    tokens = slice(fb * FB + s * QB, fb * FB + (s + 1) * QB)
                    for n in range(2):
                        last = three_passes(BANK[2 * s + n],
                                            lambda a, c: (e_hi, e_lo)[a][k][:, (2 * c + n) * P:(2 * c + n + 1) * P],
                                            lambda a, c: xT[:, a, c, tokens], KC)
                    last.then_inc(gu_product, 1)

                def down(v, k, s, new_pair, split_value, start=False, stop=False):
                    if new_pair:
                        pe.wait_ge(dn_split, split_value)
                    pe.wait_ge(i_split, at + v + 1)
                    for m in range(KC):
                        cols = slice(EW - E + m * P, EW - E + (m + 1) * P)
                        last = three_passes(BANK[4 + 2 * m + s], lambda a, c: (e_hi, e_lo)[a][k][:, cols],
                                            lambda a, c: (i_hi, i_lo)[a][s][:, :], 1, start, stop)
                    last.then_inc(down_done, 1)

                def four(i, first=False, last=False):
                    for r in range(4):
                        k, pair = (1, 2 * i + 1) if r < 2 else (0, 2 * i + 2)
                        if last and r >= 2:
                            gate_up(4 * i + r + 2, 2, r % 2, False, None)
                        else:
                            gate_up(4 * i + r + 2, k, r % 2, r % 2 == 0, sb + pair + 1)
                        down(4 * i + r, r // 2, r % 2, r % 2 == 0, sb + 2 * i + r // 2 + 1, start=first and r < 2)

                for v in range(2):
                    gate_up(v, 0, v, v == 0, sb + 1, first=True)
                four(0, first=True)
                with pe.Fori(1, PAIRS // 2 - 1) as i:
                    four(i)
                four(PAIRS // 2 - 1, last=True)
                for v in range(2 * PAIRS, HU):
                    down(v, 2, v % 2, False, None, stop=True)
                pe.wait_ge(moe_sums, 4 * (f * NFB + fb + 1))
                for i in range(FB // P // 2):
                    bank = bank_of(first_unit["f", f, f"F{fb}"] + i)
                    for n in range(2 * KC):
                        t, m = 2 * i + n // 2, n % 2
                        last = pe.transpose(bank[:, n * P:(n + 1) * P], moe_out[:, m, t * P:(t + 1) * P], ident[:, :])
                    last.then_inc(product, 1)

        @block.tensor
        def _(pe):
            def bank_of(u):
                if u >= NBANK:
                    pe.wait_ge(bank_free, u - NBANK + 1)
                return BANK[u % NBANK]

            def three_passes(out, stationary, moving, chunks, start=True, stop=True):
                order = [(k, a, c) for k in range(chunks) for a, c in ((0, 0), (0, 1), (1, 0))]
                for n, (k, a, c) in enumerate(order):
                    last = pe.matmul(out, stationary(a, k), moving(c, k), start=start and n == 0,
                                     stop=stop and n == len(order) - 1, skip_group_check=not (start and stop))
                return last

            def turn(phase, name, src, wait):
                for i in range(2 * NB):
                    k, b = i // NB, i % NB
                    wait(b)
                    bank = bank_of(first_unit[(*phase, name)] + i)
                    for t in range(TPB):
                        last = pe.transpose(bank[:, t * P:(t + 1) * P], src[:, b * TPB + t, k * P:(k + 1) * P], ident[:, :])
                    last.then_inc(product, 1)

            def features(phase, name, w, src, chunks=KC, rows=P):
                pe.wait_ge(w_split, w_ready(phase[1], w))
                for i in range(2 * NB):
                    m, b = i // NB, i % NB
                    bank = bank_of(first_unit[(*phase, name)] + i)
                    three_passes(bank, lambda a, k: weight((w_hi, w_lo)[a], w, k, slice(m * P, (m + 1) * P), rows),
                                 lambda c, k: src(c, k, slice(b * QB, (b + 1) * QB)), chunks).then_inc(product, 1)

            def latent(phase, name, w, since):
                pe.wait_ge(w_split, w_ready(phase[1], w))
                pe.wait_ge(bank_free, first_unit[(*phase, since)] + 2 * NB)
                for b in range(NB):
                    bank = bank_of(first_unit[(*phase, name)] + b)
                    three_passes(bank[0:DL, :], lambda a, k: weight((w_hi, w_lo)[a], w, k, slice(0, DL)),
                                 lambda c, k: mid[:, c, k, b * QB:(b + 1) * QB], KC).then_inc(product, 1)

            def tokens_out(phase, name, stationary, moving, chunks):
                for i in range(T // 2):
                    bank = bank_of(first_unit[(*phase, name)] + i)
                    for t in range(2):
                        last = three_passes(bank[:, t * E:(t + 1) * E], lambda a, k: stationary(a, k, 2 * i + t),
                                            moving, chunks)
                    last.then_inc(product, 1)

            def from_xT(c, k, cols):
                return xT[:, c, k, cols]

            def max_bank(n):
                if n >= NMAX:
                    pe.wait_ge(max_free, n - NMAX + 1)
                return max_banks[n % NMAX]

            def attention(kind, layer):
                phase = (kind, layer)
                turn(phase, "T", xn, lambda b: pe.wait_ge(xn_done, T * norm_of[phase] + (b + 1) * TPB))
                pe.wait_ge(bank_free, first_unit[kind, layer, "T"] + 2 * NB)
                features(phase, "Q", "q", from_xT)
                if layer == 0:
                    features(phase, "K", "k", from_xT)
                    pe.wait_ge(w_split, w_ready(layer, "v"))
                    tokens_out(phase, "V", lambda a, k, t: xT[:, a, k, t * P:(t + 1) * P],
                               lambda c, k: weight((w_hi, w_lo)[c], "v", k, slice(0, E)), KC)
                else:
                    features(phase, "K1", "k", from_xT)
                    latent(phase, "KL", "kl", "K1")
                    pe.wait_ge(bank_free, first_unit[kind, layer, "KL"] + NB)
                    features(phase, "K", "upk", lambda c, k, cols: lat[:, c, cols], 1, DL)
                    features(phase, "V1", "v", from_xT)
                    latent(phase, "VL", "vl", "V1")
                    pe.wait_ge(w_split, w_ready(layer, "upv"))
                    pe.wait_ge(bank_free, first_unit[kind, layer, "VL"] + NB)
                    tokens_out(phase, "V", lambda a, k, t: lat[:, a, t * P:(t + 1) * P],
                               lambda c, k: weight((w_hi, w_lo)[c], "upv", 0, slice(0, E), DL), 1)
                pe.wait_ge(bank_free, first_unit[kind, layer, "V"] + 8)
                pe.wait_ge(ident_ready, 5)
                loads = [0, 0]
                for s in range(2):
                    loads[s] = 16 * layer * (FRESH_LOADS + G // 2 * GROUP_LOADS)
                loaded = set()
                for item in plan:
                    if item[0] == "max":
                        _, g, h, t, c = item
                        s, p, hh = g % 2, h // 2, h % 2
                        if g not in loaded:
                            loaded.add(g)
                            loads[s] += 16 * (GROUP_LOADS + (FRESH_LOADS if g < 2 else 0))
                            pe.wait_ge(ops_in[s], loads[s])
                        n = min(QB, P * (t + 1) - QB * c)
                        bank = max_bank(layer * MU + mu_of[item])
                        pe.matmul(bank[:, 0:n], Qp[s][0:ROW_MAX, p, t * P:(t + 1) * P],
                                  Kp[s][0:ROW_MAX, p, hh, c * QB:c * QB + n], start=True, stop=True)\
                            .then_inc(max_product, 1)
                    elif item[0] == "turn":
                        _, g, b = item
                        n = block_no(layer, g, b)
                        bank = max_bank(layer * MU + mu_of[item])
                        pe.wait_ge(neg_done, n + 1)
                        pe.transpose(bank[0:GH * TPB, 0:P], neg_max[:, n % 2, :, :].rearrange("p h t -> p (h t)"),
                                     ident[:, :]).then_inc(max_product, 1)
                    elif item[0] == "qk":
                        _, g, b, j, p, _ = item
                        e = e_of[layer, g, b, j]
                        s = g % 2
                        off = P * max(0, j - TPB * b)
                        if j == 0 and p == 0:
                            pe.wait_ge(neg_in, 64 * (block_no(layer, g, b) + 1))
                        if e >= 1:
                            pe.wait_ge(exp_done, 2 * (e - 1) + p + 1)
                        for hh in range(2):
                            last = pe.matmul(exp_banks[p][:, hh, off:QB], Kp[s][0:ROWS, p, hh, j * P:(j + 1) * P],
                                             Qp[s][0:ROWS, p, b * QB + off:(b + 1) * QB], start=True,
                                             stop=j < TPB * b)
                            if j >= TPB * b:
                                last = pe.matmul(exp_banks[p][:, hh, off:off + P], ident16[:, :], cut16[:, :],
                                                 start=False, stop=True)
                        last.then_inc(qk_product, 1)
                    elif item[0] == "pv":
                        _, g, b, j, _ = item
                        e = e_of[layer, g, b, j]
                        off = P * max(0, j - TPB * b)
                        n = block_no(layer, g, b)
                        if j == 0 and n >= NPV:
                            pe.wait_ge(sums_out, n - NPV + 1)
                        pe.wait_ge(exp_done, 2 * (e + 1))
                        for h in range(GH):
                            last = pe.matmul(pv_banks[n % NPV][32 * h:32 * h + 32, off:QB],
                                             values[:, j, GH * g + h, :], probs[:, e % NP, h, off:QB],
                                             start=(j == 0), stop=(j == TPB * (b + 1) - 1))
                        last.then_inc(pv_done, 1)
                    elif item[0] == "ctx":
                        _, g, b = item
                        n = block_no(layer, g, b)
                        bank = max_bank(layer * MU + mu_of[item])
                        pe.wait_ge(sums_out, n + 1)
                        for t in range(TPB):
                            last = pe.transpose(bank[:, t * P:(t + 1) * P], sums[:, n % 2, t * P:(t + 1) * P], ident[:, :])
                        last.then_inc(max_product, 1)
                pe.wait_ge(max_free, (layer + 1) * MU)
                turn(phase, "C", context, lambda b: None)
                pe.wait_ge(bank_free, first_unit[kind, layer, "C"] + 2 * NB)
                pe.wait_ge(wpost_split, 2 * (layer + 1))
                tokens_out(phase, "O", lambda a, k, t: xT[:, a, k, t * P:(t + 1) * P],
                           lambda c, k: w_post[:, c, k, :], KC)

            pe.wait_ge(ident_ready, 1)
            for kind, n in phases:
                if kind != "f":
                    attention(kind, n)
                else:
                    experts_pe(pe, n, turn, bank_of, three_passes)

        def experts_dve(dve, f, norm, low_parts):
            phase = ("f", f)
            norm(phase)
            low_parts(phase, "T", 2 * NB, in_block(xT, 0), in_block(xT, 1))
            for i in range(NB):
                u = first_unit["f", f, "R"] + i
                dve.wait_ge(product, u + 1)
                dve.tensor_copy(logits[:, i * TPB:(i + 1) * TPB, :],
                                BANK[u % NBANK].rearrange("p (t c) -> p t c", t=TPB)[:, :, 0:GC]).then_inc(bank_free, 1)
            dve.wait_ge(bank_free, first_unit["f", f, "R"] + NB)
            experts_of = logits[:, :, 0:NEXP]
            for t in range(T):
                dve.max(top[:, t, :], logits[:, t, 0:NEXP]).then_inc(top_done, 1)
            dve.wait_ge(top_done, T * (f + 1))
            step = ROUTE_STEPS * f
            dve.tensor_tensor(route[:, :, 0:NEXP], experts_of, top[:, :, 0:1].broadcast_to([P, T, NEXP]), ALU.subtract)\
                .then_inc(route_step, 1)
            dve.tensor_scalar(route[:, :, NEXP:GC], logits[:, :, NEXP:GC], -1.0, None, ALU.mult).then_inc(route_step, 1)
            for t in range(T):
                dve.match_replace(out=chosen[:, t, :], in_to_replace=top[:, t, :], in_values=logits[:, t, 0:NEXP],
                                  imm_value=VLOW).then_inc(route_step, 1)
            dve.wait_ge(route_step, step + 2 + T)
            dve.tensor_tensor(chosen[:, :, :], chosen[:, :, :], experts_of, ALU.not_equal).then_inc(route_step, 1)
            dve.wait_ge(route_exp, f + 1)
            dve.wait_ge(route_step, step + 3 + T)
            dve.tensor_tensor(route[:, :, 0:NEXP], route[:, :, 0:NEXP], chosen[:, :, :], ALU.mult).then_inc(route_step, 1)
            dve.wait_ge(route_step, step + 4 + T)
            dve.tensor_reduce(route_sum[:, :], route[:, :, 0:NEXP], AX.X, ALU.add).then_inc(route_step, 1)
            dve.wait_ge(route_step, step + 5 + T)
            dve.reciprocal(route_inv[:, :], route_sum[:, :]).then_inc(route_step, 1)
            dve.tensor_scalar(route[:, :, NEXP:NEXP + 1], route[:, :, NEXP:NEXP + 1], 1.0, None, ALU.add).then_inc(route_step, 1)
            dve.wait_ge(route_step, step + 7 + T)
            inv = route_inv[:, :].rearrange("p (t o) -> p t o", o=1).broadcast_to([P, T, NEXP])
            dve.tensor_tensor(route[:, :, 0:NEXP], route[:, :, 0:NEXP], inv, ALU.mult).then_inc(route_step, 1)
            dve.reciprocal(route[:, :, NEXP:NEXP + 1], route[:, :, NEXP:NEXP + 1]).then_inc(route_step, 1)
            dve.memset(route[:, :, NEXP + 1:GC], 0.0).then_inc(route_step, 1)
            for i in range(NB):
                u = first_unit["f", f, "W"] + i
                dve.wait_ge(product, u + 1)
                dve.tensor_copy(route_rows_sb[:, i * QB:(i + 1) * QB], BANK[u % NBANK][0:GC, :]).then_inc(bank_free, 1)
            for fb in range(NFB):
                at = unit_base(f, fb)
                loads = [(f * NFB + fb) * (PAIRS // 2 + 1), (f * NFB + fb) * PAIRS // 2]

                def unit(v, s, k, load, first=False):
                    dve.wait_ge(silu_done, at + v + 1)
                    if not first:
                        dve.wait_ge(i_split, at + v - 1)
                    dve.tensor_tensor(inter[s][:, :], BANK[2 * s + 1], silu[s][:, :], ALU.mult).then_inc(gated, 1)
                    if s == 0:
                        dve.wait_ge(wide_in[k], 16 * load)
                    dve.wait_ge(gated, at + v + 1)
                    dve.tensor_tensor(inter[s][:, :], inter[s][:, :], wide[k][:, s * QB:(s + 1) * QB], ALU.mult)\
                        .then_inc(weighted, 1)
                    dve.wait_ge(i_high, at + v + 1)
                    if not first:
                        dve.wait_ge(down_done, at + v - 1)
                    dve.tensor_tensor(i_lo[s][:, :], inter[s][:, :], i_hi[s][:, :].bitcast(F32), ALU.subtract)\
                        .then_inc(i_split, 1)

                for v in range(4):
                    unit(v, v % 2, v // 2, loads[v // 2] + 1, first=(at == 0 and v < 2))
                with dve.Fori(1, PAIRS // 2) as i:
                    for r in range(4):
                        unit(4 * i + r, r % 2, r // 2, loads[r // 2] + 1 + i)
                for v in range(2 * PAIRS, HU):
                    unit(v, v % 2, 0, loads[0] + PAIRS // 2 + 1)
                for i in range(FB // P // 2):
                    u = first_unit["f", f, f"F{fb}"] + i
                    dve.wait_ge(product, u + 1)
                    t = fb * FB // P + 2 * i
                    dve.tensor_tensor(x[:, t:t + 2, :], BANK[u % NBANK].rearrange("p (t e) -> p t e", t=2),
                                      x[:, t:t + 2, :], ALU.add).then_inc(bank_free, 1)
            dve.wait_ge(bank_free, first_unit["f", f, "F1"] + 4)

        @block.vector
        def _(dve):
            def norm(phase):
                n = norm_of[phase]
                for t in range(T):
                    dve.bn_stats(stats[:, t, :], x[:, t, :]).then_inc(stats_done, 1)
                for t in range(T):
                    dve.wait_ge(stats_done, n * T + t + 1)
                    dve.bn_aggr(mean_var[:, t, :], stats[:, t, :]).then_inc(aggr_done, 1)
                dve.wait_ge(aggr_done, (n + 1) * T)
                dve.tensor_scalar(var_eps[:, :], mean_var[:, :, 1], EPS, None, ALU.add).then_inc(eps_done, 1)
                dve.wait_ge(std_done, n + 1)
                dve.reciprocal(rstd[:, :], std[:, :]).then_inc(rstd_done, 1)
                dve.wait_ge(rstd_done, n + 1)
                for t in range(T):
                    dve.tensor_scalar(xn[:, t, :], x[:, t, :], mean_var[:, t, 0:1], rstd[:, t:t + 1],
                                      ALU.subtract, ALU.mult).then_inc(xn_done, 1)

            def low_parts(phase, name, count, hi, lo, bias=None, rows=P):
                for i in range(count):
                    u = first_unit[(*phase, name)] + i
                    dve.wait_ge(hi_done, first_hi[(*phase, name)] + i + 1)
                    bank = BANK[u % NBANK][0:rows, :]
                    if bias is None:
                        dve.tensor_tensor(lo(i), bank, hi(i).bitcast(F32), ALU.subtract).then_inc(bank_free, 1)
                    else:
                        dve.scalar_tensor_tensor(out=lo(i), in0=bank, scalar=bias(i), in1=hi(i).bitcast(F32),
                                                 op0=ALU.add, op1=ALU.subtract).then_inc(bank_free, 1)

            def attention(kind, layer):
                phase = (kind, layer)
                norm(phase)
                low_parts(phase, "T", 2 * NB, in_block(xT, 0), in_block(xT, 1))
                if layer == 0:
                    low_parts(phase, "Q", 2 * NB, staged(layer, "Q", part_hi), staged(layer, "Q", part_lo))
                    low_parts(phase, "K", 2 * NB, staged(layer, "K", part_hi), staged(layer, "K", part_lo))
                else:
                    low_parts(phase, "Q", 2 * NB, staged(layer, "Q", part_hi), staged(layer, "Q", part_lo), bias_col("q"))
                    low_parts(phase, "K1", 2 * NB, in_block(mid, 0), in_block(mid, 1), bias_col("k"))
                    low_parts(phase, "KL", NB, in_lat(0), in_lat(1), bias_col("kl", DL), DL)
                    low_parts(phase, "K", 2 * NB, staged(layer, "K", part_hi), staged(layer, "K", part_lo), bias_col("upk"))
                    low_parts(phase, "V1", 2 * NB, in_block(mid, 0), in_block(mid, 1), bias_col("v"))
                    low_parts(phase, "VL", NB, in_lat(0), in_lat(1), bias_col("vl", DL), DL)
                for i in range(T // 2):
                    u = first_unit[kind, layer, "V"] + i
                    dve.wait_ge(product, u + 1)
                    for t in range(2):
                        bank = BANK[u % NBANK][:, t * E:(t + 1) * E].rearrange("p (h d) -> p h d", h=H)
                        dst = values[:, 2 * i + t, :, 0:D]
                        if layer == 0:
                            op = dve.tensor_copy(dst, bank)
                        else:
                            op = dve.tensor_tensor(dst, bank, bias_rows[:, 2, :].rearrange("p (h d) -> p h d", h=H), ALU.add)
                    op.then_inc(bank_free, 1)
                dve.wait_ge(product, first_unit[kind, layer, "V"] + 8)
                dve.wait_ge(bank_free, first_unit[kind, layer, "V"] + 8)
                if layer == 0:
                    dve.wait_ge(ident_ready, 2)
                masked_at = []
                begun = set()
                for item in plan:
                    if item[0] == "max":
                        _, g, h, t, c = item
                        b, n = t // TPB, min(QB, P * (t + 1) - QB * c)
                        bn = block_no(layer, g, b)
                        mu = layer * MU + mu_of[item]
                        slot = bn % 2
                        if bn not in begun:
                            begun.add(bn)
                            if bn >= 2:
                                dve.wait_ge(neg_done, bn - 1)
                        bank = max_banks[mu % NMAX]
                        dve.wait_ge(max_product, mu + 1)
                        to = chunk_max[:, slot, h, t % TPB, c:c + 1]
                        if c == b:
                            k = len(masked_at)
                            if k >= 2:
                                dve.wait_ge(max_free, masked_at[k - 2] + 1)
                            dve.tensor_tensor_reduce(masked[k % 2][:, 0:n], bank[:, 0:n], diag_mask[:, QB - n:QB],
                                                     1.0, VLOW, ALU.add, ALU.max, to).then_inc(max_free, 1)
                            masked_at.append(mu)
                        else:
                            dve.tensor_reduce(to, bank[:, 0:n], AX.X, ALU.max).then_inc(max_free, 1)
                        if t % TPB == TPB - 1 and h == GH - 1 and c == b:
                            dve.wait_ge(max_free, mu + 1)
                            if bn >= 2:
                                last = divmod(g * NB + b - 2, NB) if g * NB + b >= 2 else divmod(G * NB + b - 2, NB)
                                base = layer * MU if g * NB + b >= 2 else (layer - 1) * MU
                                dve.wait_ge(max_product, base + mu_of[("turn", *last)] + 1)
                            dve.tensor_reduce(neg_max[:, slot, :, :], chunk_max[:, slot, :, :, 0:b + 1], AX.X, ALU.max,
                                              negate=True).then_inc(neg_done, 1)
                    elif item[0] == "turn":
                        _, g, b = item
                        n = block_no(layer, g, b)
                        mu = layer * MU + mu_of[item]
                        bank = max_banks[mu % NMAX][0:GH * TPB, 0:P]
                        dve.wait_ge(max_product, mu + 1)
                        if n >= 2:
                            dve.wait_ge(neg_in, 64 * (n - 1))
                        dve.tensor_copy(neg_hi[:, n % 2, :], bank).then_inc(neg_high, 1)
                        dve.wait_ge(neg_high, n + 1)
                        dve.tensor_tensor(neg_lo[:, n % 2, :], bank, neg_hi[:, n % 2, :].bitcast(F32), ALU.subtract)\
                            .then_inc(max_free, 1)
                    elif item[0] == "ctx":
                        _, g, b = item
                        n = block_no(layer, g, b)
                        mu = layer * MU + mu_of[item]
                        dve.wait_ge(max_product, mu + 1)
                        if n >= 2:
                            dve.wait_ge(inv_done, n - 1)
                        bank = max_banks[mu % NMAX][:, :].rearrange("p (t r) -> p t r", r=2 * D)
                        dve.reciprocal(inv_den[:, n % 2, :], bank[:, :, D]).then_inc(inv_done, 1)
                        dve.wait_ge(inv_done, n + 1)
                        out = context[:, b * TPB:(b + 1) * TPB, g * GH * D:(g + 1) * GH * D]
                        inv = inv_den[:, n % 2, :].rearrange("p (t h o) -> p t h o", h=GH, o=1)
                        dve.tensor_tensor(out.rearrange("p t (h d) -> p t h d", h=GH),
                                          bank[:, :, 0:D].rearrange("p (t h) d -> p t h d", h=GH),
                                          inv.broadcast_to([P, TPB, GH, D]), ALU.mult).then_inc(max_free, 1)
                low_parts(phase, "C", 2 * NB, in_block(xT, 0), in_block(xT, 1))
                dve.wait_ge(bias_added, layer + 1)
                for i in range(T // 2):
                    u = first_unit[kind, layer, "O"] + i
                    dve.wait_ge(product, u + 1)
                    pair = x[:, 2 * i:2 * i + 2, :]
                    dve.tensor_tensor(pair, BANK[u % NBANK].rearrange("p (t e) -> p t e", t=2), pair, ALU.add)\
                        .then_inc(bank_free, 1)
                dve.wait_ge(bank_free, first_unit[kind, layer, "O"] + 8)

            dve.wait_ge(slopes_ready, 1)
            dve.tensor_tensor(slope_lo[:, :], slope_raw[:, :], slope_hi[:, :].bitcast(F32), ALU.subtract)\
                .then_inc(slopes_ready, 1)
            dve.wait_ge(x_in, 16 * T)
            for kind, n in phases:
                if kind != "f":
                    attention(kind, n)
                else:
                    experts_dve(dve, n, norm, low_parts)


_INPUTS = ("x", "w_a", "w_a_post", "w_b", "w_b_post", "bias_cols", "bias_rows", "slopes", "router", "experts")


def lay_out(L):
    def chunks(w):
        return w.reshape(KC, P, -1).transpose(1, 0, 2).reshape(P, -1)

    def rows(w, n=P):
        return np.concatenate([w, np.zeros((n - w.shape[0], *w.shape[1:]), w.dtype)], 0)

    a = {k[len("L0_attn_a_"):]: np.asarray(v) for k, v in L.items() if k.startswith("L0_attn_a_")}
    b = {k[len("L0_attn_b_"):]: np.asarray(v) for k, v in L.items() if k.startswith("L0_attn_b_")}
    f = {k[len("L0_ffn_"):]: np.asarray(v) for k, v in L.items() if k.startswith("L0_ffn_")}
    up = {n: b[f"up{n}_w"].transpose(1, 0, 2).reshape(DL, E) for n in "kv"}
    w_a = np.concatenate([chunks(a["Wq"]), chunks(a["Wk"]), chunks(a["Wv"])], 1)
    w_b = np.concatenate([chunks(b["wq_w"]), chunks(b["wk_w"]), chunks(b["wv_w"]), chunks(b["wkl_w"]),
                          chunks(b["wvl_w"]), rows(up["k"]), rows(up["v"])], 1)
    bias_cols = np.stack([b["wq_b"][0:P], b["wq_b"][P:E], b["wk_b"][0:P], b["wk_b"][P:E], b["wv_b"][0:P], b["wv_b"][P:E],
                          b["upk_b"].reshape(E)[0:P], b["upk_b"].reshape(E)[P:E], rows(b["wkl_b"]), rows(b["wvl_b"])], 1)
    bias_rows = np.stack([a["bo"], b["wo_b"], b["upv_b"].reshape(E)])
    slope = (2.0 ** (-8.0 * np.arange(1, H + 1) / H)).astype(np.float32)
    slopes = slope[:, None] * (np.arange(S) - S // 2).astype(np.float32)[None, :]
    router = chunks(np.concatenate([f["gate_w"], f["sh_gate1_w"], np.zeros_like(f["sh_gate1_w"])], 0).T)
    pad = np.zeros((1, EI, E), np.float32)
    gate = np.concatenate([f["gu_w"][:, 0:EI], f["sh_gate_w"][None], pad], 0)
    upw = np.concatenate([f["gu_w"][:, EI:], f["sh_up_w"][None], pad], 0)
    down = np.concatenate([f["dp_w"].transpose(0, 2, 1), f["sh_down_w"].T[None], pad], 0)
    gu = np.stack([gate.reshape(PAIRS + 1, P, KC, P), upw.reshape(PAIRS + 1, P, KC, P)], 0)
    gu = gu.transpose(1, 4, 3, 0, 2).reshape(PAIRS + 1, P, KC * 2 * P)
    experts = np.concatenate([gu, down.reshape(PAIRS + 1, P, E)], 2)
    return {"x": a["x"].reshape(S, E), "w_a": w_a, "w_a_post": chunks(a["Wo"]), "w_b": w_b, "w_b_post": chunks(b["wo_w"]),
            "bias_cols": bias_cols, "bias_rows": bias_rows, "slopes": slopes.reshape(P, -1), "router": router,
            "experts": experts}


def kernel(**inputs):
    import concourse.bacc as bacc
    from concourse.bass_utils import run_bass_kernel_spmd

    nc = bacc.Bacc("TRN2", target_bir_lowering=False, num_devices=1)
    laid = lay_out(inputs)
    arrays, aps = {}, {}
    for name in _INPUTS:
        array = np.ascontiguousarray(laid[name])
        arrays[f"in_{name}"] = array
        aps[name] = nc.dram_tensor(f"in_{name}", array.shape, mybir.dt.from_np(array.dtype), kind="ExternalInput").ap()
    aps["out"] = nc.dram_tensor("result", (S, E), F32, kind="ExternalOutput").ap()
    build(nc, aps)
    got = run_bass_kernel_spmd(nc, [arrays], core_ids=[0])
    return got.results[0]["result"].reshape(1, S, E)
```

```python
from contextlib import ExitStack

import numpy as np

import concourse.bass as bass
from concourse import mybir

F32 = mybir.dt.float32
F32R = mybir.dt.float32r
BF16 = mybir.dt.bfloat16
ALU = mybir.AluOpType
ACT = mybir.ActivationFunctionType
AX = mybir.AxisListType

P = 128
S = 2048
E = 256
T = S // P
KC = E // P
QB = 512
NB = S // QB
TPB = QB // P
H = 16
D = E // H
DL = 64
EPS = 1e-5
NEG = -1e30
VLOW = -3e38

ROWS_HEAD = 3 * D
ROW_BIAS = 2 * ROWS_HEAD
ROW_MAX = ROW_BIAS + 2
ROWS = ROW_MAX + 4
GH = 4
G = H // GH
NP = 3
FILL = 256
NSTAGE = 3
NMAX, NPV = 3, 1

NEXP = 64
EI = 64
TOPK = 8
GC = NEXP + 2
PAIRS = NEXP // 2
RT = T // 2
ROUTE_STEPS = RT + 10
EW = KC * 2 * P + E
FB = 1024
NFB = S // FB


W_COLS = {"q": E, "k": E, "v": E, "kl": 2 * DL, "vl": DL, "upk": E, "upv": E}
W_CHUNKS = {"q": KC, "k": KC, "v": KC, "kl": KC, "vl": KC, "upk": 1, "upv": 1}
W_OFF, NWB = {}, 0
for _name in W_COLS:
    W_OFF[_name] = NWB
    NWB += W_COLS[_name] * W_CHUNKS[_name]
NWA = W_OFF["kl"]
W_ORDER = [["q", "k", "v"], ["v", "q", "vl", "k", "kl", "upk", "upv"]]
STAGED = [["Q0", "K0", "Q1", "K1"], ["Q0", "Q1", "K0", "K1"]]


def core_plan():
    SIGNAL, ROWS_BACK, LOAD = 250, 3600, 12000

    maxima = []
    for g in range(G):
        for b in range(NB):
            if (g, b) != (0, 0):
                pending = ("turn", *divmod(g * NB + b - 1, NB))
            else:
                pending = None
            for t in range(b * TPB, (b + 1) * TPB):
                for h in range(GH):
                    for c in range(t // TPB + 1):
                        maxima.append(("max", g, h, t, c))
                        if pending and len(maxima) and (h, t, c) == (1, b * TPB, 0):
                            maxima.append(pending)
    maxima.append(("turn", G - 1, NB - 1))
    units = [(g, b, j) for g in range(G) for b in range(NB) for j in range(TPB * (b + 1))]
    scores = [("qk", g, b, j, p, e) for e, (g, b, j) in enumerate(units) for p in range(2)]
    sums = [("pv", g, b, j, e) for e, (g, b, j) in enumerate(units)]
    contexts = []
    for g in range(G):
        for b in range(NB):
            contexts.append(("ctx", g, b))
            if g == G - 1:
                contexts += [("turn_ctx", b, k) for k in range(KC)]
                contexts += [("project", i) for i in range(b * TPB // 2, (b + 1) * TPB // 2)]
    streams = [contexts, maxima, scores, sums]
    at = [0] * 4

    plan = []
    pe = dve = act = 0.0
    max_bank_free = [0.0] * NMAX
    exp_bank_free = [0.0] * 2
    uses = 0
    context_at = 0.0
    reduced, turned, loaded = {}, {}, {0: 0.0, 1: 0.0}
    exps, products, scored, summed = {}, {}, {}, {}

    def width(b, j):
        return QB - P * max(0, j - TPB * b)

    def ready(item):
        kind, g = item[0], item[1]
        if kind in ("max", "turn", "ctx"):
            bank = max_bank_free[uses % NMAX]
            if kind == "max":
                return max(bank, loaded[g]) if g in loaded else None
            if kind == "turn":
                return max(bank, reduced[item[1:]]) if item[1:] in reduced else None
            return max(bank, summed[item[1:]]) if item[1:] in summed else None
        if kind in ("turn_ctx", "project"):
            return max(max_bank_free[uses % NMAX], context_at)
        if kind == "qk":
            return max(exp_bank_free[item[4]], turned[item[1:3]]) if item[1:3] in turned and \
                (item[5] < NP or item[5] - NP in products) else None
        n = item[1] * NB + item[2]
        if item[3] == TPB * (item[2] + 1) - 1 and n >= 2 and ("ctx", *divmod(n - 2, NB)) in contexts[at[0]:]:
            return None
        return exps.get((item[4], 1))

    while any(at[k] < len(s) for k, s in enumerate(streams)):
        best = None
        for k, s in enumerate(streams):
            if at[k] < len(s):
                when = ready(s[at[k]])
                if when is not None:
                    when = max(when, pe)
                    if best is None or when < best[0]:
                        best = (when, k)
        start, k = best
        item = streams[k][at[k]]
        at[k] += 1
        plan.append(item)
        kind, g = item[0], item[1]
        if kind == "max":
            _, g, h, t, c = item
            n = min(QB, P * (t + 1) - QB * c)
            pe = start + n / 2.4 + 3
            dve = max(dve, pe + SIGNAL) + n / 0.96 + 75
            max_bank_free[uses % NMAX] = dve + 50
            uses += 1
            if h == GH - 1 and t % TPB == TPB - 1 and c == t // TPB:
                dve += 250
                reduced[g, t // TPB] = dve + 50
        elif kind == "turn":
            pe = start + 110
            dve = max(dve, pe + SIGNAL) + 600
            max_bank_free[uses % NMAX] = dve + 50
            uses += 1
            turned[item[1:]] = dve + ROWS_BACK
        elif kind == "ctx":
            pe = start + 450
            dve = max(dve, pe + SIGNAL) + 550
            max_bank_free[uses % NMAX] = context_at = dve + 50
            uses += 1
        elif kind == "turn_ctx":
            pe = start + 450
            act = max(act, pe + SIGNAL) + 600
            dve = max(dve, act + 50) + 600
            max_bank_free[uses % NMAX] = dve + 50
            uses += 1
            context_at = dve + 50 if item[2] == KC - 1 else pe
        elif kind == "project":
            pe = start + 12 * 110
            dve = max(dve, pe + SIGNAL) + 600
            max_bank_free[uses % NMAX] = dve + 50
            uses += 1
            context_at = pe
            dve += 3200 * (item[1] % 2)
        elif kind == "qk":
            _, g, b, j, p, e = item
            n = width(b, j)
            pe = start + 2 * (n / 2.4 + 3) + (120 if j >= TPB * b else 0)
            free = products[e - NP] if e >= NP else 0
            act = max(act, pe + SIGNAL, free) + 2 * n / 1.2 + 60
            exp_bank_free[p] = act + 50
            exps[e, p] = act + 50
            if j == T - 1 and p == 1 and g + 2 < G:
                loaded[g + 2] = max(pe, turned[g + 1, NB - 2] if (g + 1, NB - 2) in turned else pe) + LOAD
        elif kind == "pv":
            _, g, b, j, e = item
            n = width(b, j)
            pe = start + 4 * (n / 2.4 + 3) + 100
            products[e] = pe + SIGNAL
            if j == TPB * (b + 1) - 1:
                act = max(act, pe + SIGNAL) + 600
                summed[g, b] = act + 50
                plan.append(("out", g, b))
    return plan


def build(nc, A, parts="afbf"):
    plan = core_plan()
    ctx = ExitStack()
    with ctx:
        def sem(name):
            return ctx.enter_context(nc.semaphore(name))

        def tile(name, shape, dt=F32, stack=ctx):
            return stack.enter_context(nc.sbuf_tensor(f"{name}_t", shape, dt))

        exp_banks = [ctx.enter_context(nc.psum_tensor(f"exp_banks{i}", [P, 2, QB], F32)) for i in range(2)]
        max_banks = [ctx.enter_context(nc.psum_tensor(f"max_bank{i}", [P, QB], F32)) for i in range(NMAX)]
        pv_banks = [ctx.enter_context(nc.psum_tensor(f"pv_bank{i}", [P, QB], F32)) for i in range(NPV)]
        BANK = [exp_banks[0][:, 0, :], exp_banks[0][:, 1, :], exp_banks[1][:, 0, :], exp_banks[1][:, 1, :],
                *(bank[:, :] for bank in max_banks + pv_banks)]
        NBANK = len(BANK)

        x = tile("x_sb", [P, T, E])
        ident = tile("ident", [P, P])
        ones = tile("ones", [P, 1])
        minus_half = tile("minus_half", [P, 1])
        var_eps = tile("var_eps", [P, T])
        diag_mask = tile("diag_mask", [P, QB])
        ident16 = tile("ident16", [P, P], BF16)
        cut16 = tile("cut16", [P, P], BF16)
        values = tile("values", [P, T, H, 2 * D])
        w_post_raw = tile("w_post_raw", [P, KC * E])
        w_post = tile("w_post", [P, 2, KC, E], F32R)
        bias_cols = tile("bias_cols", [P, 10])
        bias_rows = tile("bias_rows", [P, 3, E])
        stats = tile("stats", [P, T, 6])
        mean_var = tile("mean_var", [P, T, 2])
        rstd = tile("rstd", [P, T])

        outer = ExitStack()
        xT = tile("xT", [P, 2, KC, S], F32R, outer)
        xn = tile("xn", [P, T, E], F32, outer)
        pre = ExitStack()
        mid = tile("mid", [P, 2, KC, S], F32R, pre)
        lat = tile("lat", [P, 2, S], F32R, pre)
        part_hi = [tile(f"part_hi{i}", [P, QB], F32R, pre) for i in range(NSTAGE)]
        part_lo = [tile(f"part_lo{i}", [P, QB], F32R, pre) for i in range(NSTAGE)]
        w_raw = tile("w_raw", [P, NWB], F32, pre)
        w_hi = tile("w_hi", [P, NWB], F32R, pre)
        w_lo = tile("w_lo", [P, NWB], F32R, pre)
        slope_raw = tile("slope_raw", [P, S * H // P], F32, pre)
        slope_hi = tile("slope_hi", [P, S * H // P], F32R, pre)
        slope_lo = tile("slope_lo", [P, S * H // P], F32R, pre)
        fill = tile("fill", [ROWS_HEAD, 2, FILL], F32R, pre)
        pre.close()
        moe = ExitStack()
        g_raw = tile("g_raw", [P, KC * GC], F32, moe)
        g_hi = tile("g_hi", [P, KC * GC], F32R, moe)
        g_lo = tile("g_lo", [P, KC * GC], F32R, moe)
        logits = tile("logits", [P, T, GC], F32, moe)
        top = tile("top", [P, T, TOPK], F32, moe)
        route = tile("route", [P, T, GC], F32, moe)
        chosen = tile("chosen", [P, T, NEXP], F32, moe)
        route_sum = tile("route_sum", [P, T], F32, moe)
        route_inv = tile("route_inv", [P, T], F32, moe)
        route_rows_sb = tile("route_rows_sb", [GC, S], F32, moe)
        e_raw = [tile(f"e_raw{i}", [P, EW], F32, moe) for i in range(3)]
        e_hi = [tile(f"e_hi{i}", [P, EW], F32R, moe) for i in range(3)]
        e_lo = [tile(f"e_lo{i}", [P, EW], F32R, moe) for i in range(3)]
        wide = [tile(f"wide{i}", [P, FB], F32, moe) for i in range(2)]
        silu = [tile(f"silu{i}", [P, QB], F32, moe) for i in range(2)]
        inter = [tile(f"inter{i}", [P, QB], F32, moe) for i in range(2)]
        i_hi = [tile(f"i_hi{i}", [P, QB], F32R, moe) for i in range(2)]
        i_lo = [tile(f"i_lo{i}", [P, QB], F32R, moe) for i in range(2)]
        moe_out = tile("moe_out", [P, KC, FB], F32, moe)
        moe.close()
        outer.close()

        core = ExitStack()
        Qp, Kp = [None, None], [None, None]
        Qp[1] = tile("Qp1", [P, 2, S], F32R, core)
        context = tile("context", [P, T, E], F32, core)
        Qp[0] = tile("Qp0", [P, 2, S], F32R, core)
        Kp[0] = tile("Kp0", [P, 2, 2, S], F32R, core)
        Kp[1] = tile("Kp1", [P, 2, 2, S], F32R, core)
        contextT = Kp[0]
        probs = tile("probs", [P, NP, GH, QB], F32, core)
        masked = [tile(f"masked{i}", [P, QB], F32, core) for i in range(2)]
        chunk_max = tile("chunk_max", [P, 2, GH, TPB, NB], F32, core)
        neg_max = tile("neg_max", [P, 2, GH, TPB], F32, core)
        neg_hi = tile("neg_hi", [GH * TPB, 2, P], F32R, core)
        neg_lo = tile("neg_lo", [GH * TPB, 2, P], F32R, core)
        sums = tile("sums", [P, 2, QB], F32, core)
        inv_den = tile("inv_den", [P, 2, TPB * GH], F32, core)
        core.close()

        q_parts = nc.dram_tensor("q_parts", [H, ROWS_HEAD, S], F32).ap()
        k_parts = nc.dram_tensor("k_parts", [H, ROWS_HEAD, S], F32).ap()
        slope_parts = nc.dram_tensor("slope_parts", [2, H, S], F32).ap()
        zero_rows = nc.dram_tensor("zero_rows", [ROWS_HEAD, S], F32).ap()
        one_rows = nc.dram_tensor("one_rows", [2, S], F32).ap()
        max_rows = nc.dram_tensor("max_rows", [4, 2, S], F32).ap()
        route_rows = [nc.dram_tensor(f"route_rows{f}", [GC, S], F32).ap() for f in range(2)]

        x_in = [sem(f"x_in{b}") for b in range(NB)]
        consts_in = sem("consts_in")
        w_in = sem("w_in")
        wpost_in = sem("wpost_in")
        set_zero = sem("set_zero")
        ident_ready = sem("ident_ready")
        fill_ready = sem("fill_ready")
        w_high = sem("w_high")
        w_split = sem("w_split")
        wpost_split = sem("wpost_split")
        const_out = sem("const_out")
        slopes_ready = sem("slopes_ready")
        stats_done = sem("stats_done")
        aggr_done = sem("aggr_done")
        eps_done = sem("eps_done")
        rstd_done = sem("rstd_done")
        xn_done = sem("xn_done")
        product = sem("product")
        hi_done = sem("hi_done")
        bank_free = sem("bank_free")
        part_out = [sem(f"part_out{i}") for i in range(NSTAGE)]
        ops_in = [sem(f"ops_in{i}") for i in range(2)]
        first_in = [sem(f"first_in{b}") for b in range(NB)]
        max_product = sem("max_product")
        max_free = sem("max_free")
        neg_done = sem("neg_done")
        neg_high = sem("neg_high")
        neg_in = sem("neg_in")
        qk_product = sem("qk_product")
        exp_done = sem("exp_done")
        pv_done = sem("pv_done")
        sums_out = sem("sums_out")
        inv_done = sem("inv_done")
        ctx_high = sem("ctx_high")
        bias_added = sem("bias_added")
        g_in = sem("g_in")
        g_split = sem("g_split")
        top_done = sem("top_done")
        route_step = sem("route_step")
        route_exp = sem("route_exp")
        rows_out = sem("rows_out")
        raw_in = [sem(f"raw_in{i}") for i in range(3)]
        wide_in = [sem(f"wide_in{i}") for i in range(2)]
        gu_high = sem("gu_high")
        gu_split = sem("gu_split")
        dn_high = sem("dn_high")
        dn_split = sem("dn_split")
        gu_product = sem("gu_product")
        silu_done = sem("silu_done")
        gated = sem("gated")
        weighted = sem("weighted")
        i_high = sem("i_high")
        i_split = sem("i_split")
        down_done = sem("down_done")
        moe_sums = sem("moe_sums")
        x_out = sem("x_out")

        STAGES = {("a", 0): [("T", 8), ("Q0", 4), ("K0", 4), ("V0", 4), ("Q1", 4), ("V1", 4), ("K1", 4),
                              ("core", 0)],
                  ("b", 1): [("T", 8), ("VM", 8), ("Q0", 4), ("VL", 4), ("KM", 8), ("Q1", 4), ("KL", 4),
                             ("K0", 4), ("V0", 4), ("K1", 4), ("V1", 4), ("core", 0)],
                  "f": [("T", 8), ("R", 4), ("W0", 2), ("F0", 4), ("W1", 2), ("F1", 4)]}
        WITH_HI = {"T", "Q0", "Q1", "K0", "K1", "VM", "VL", "KM", "KL"}
        first_unit, first_hi, norm_of, phases = {}, {}, {}, []
        u = hi = 0
        for i, kind in enumerate(parts):
            n = parts[:i].count("f") if kind == "f" else "ab".index(kind)
            phases.append((kind, n))
            norm_of[kind, n] = i
            for name, count in STAGES["f"] if kind == "f" else STAGES[kind, n]:
                first_unit[kind, n, name], first_hi[kind, n, name] = u, hi
                u += count
                hi += count * (name in WITH_HI)
        total_units = u
        LAYER = ["a", "b"]
        bias_of_col = {"q": 0, "k": 2, "v": 4, "upk": 6, "kl": 8, "vl": 9}

        def w_ready(layer, name):
            return sum(len(W_ORDER[i]) for i in range(layer)) + W_ORDER[layer].index(name) + 1

        def weight(part, name, k, cols):
            at = W_OFF[name] + k * W_COLS[name]
            return part[:, at + cols.start:at + cols.stop]

        e_of = {}
        n = 0
        for layer in range(2):
            for g in range(G):
                for b in range(NB):
                    for j in range(TPB * (b + 1)):
                        e_of[layer, g, b, j] = n
                        n += 1
        mu_of = {}
        for item in plan:
            if item[0] in ("max", "turn", "ctx", "turn_ctx", "project"):
                mu_of[item] = len(mu_of)
        MU = len(mu_of)

        def block_no(layer, g, b):
            return (layer * G + g) * NB + b

        FRESH_LOADS, LOADS = 5, 4
        HU = 2 * (PAIRS + 1)

        def split_base(f, fb):
            return f * (1 + NFB * PAIRS) + 1 + fb * PAIRS

        def unit_base(f, fb):
            return (f * NFB + fb) * HU

        def turned(t, part):
            return lambda i: t[:, part, i % KC, (i // KC) * QB:(i // KC + 1) * QB]

        def in_block(t, part):
            return lambda i: t[:, part, i // NB, (i % NB) * QB:(i % NB + 1) * QB]

        PROJECTIONS = [[name for name, _ in STAGES[phase] if name not in ("T", "core")]
                       for phase in (("a", 0), ("b", 1))]
        LAT_OF = {"VL": slice(0, DL), "KL": slice(DL, 2 * DL)}

        def in_lat(name, part):
            return lambda i: lat[LAT_OF[name], part, i * QB:(i + 1) * QB]

        def staged_no(layer, name, i):
            return (layer * 4 + STAGED[layer].index(name)) * NB + i

        def staged(layer, name, tiles):
            return lambda i: tiles[staged_no(layer, name, i) % NSTAGE][:, :]

        def bias_col(name, half=0, rows=slice(0, P)):
            return lambda i: bias_cols[rows, bias_of_col[name] + half + i // NB:bias_of_col[name] + half + i // NB + 1]

        block = ctx.enter_context(nc.Block())

        def experts_dma(sp, f, last, store):
            sp.wait_ge(max_free, (f + 1) * MU)
            sp.dma_start(g_raw[:, :], A["router"]).then_inc(g_in, 16)
            sp.dma_start(e_raw[2][:, :], A["experts"][PAIRS]).then_inc(raw_in[2], 16)

            def load_raw(fb, q, k, first=False):
                if not first:
                    sp.wait_ge(dn_split, split_base(f, fb) + q - 1)
                sp.dma_start(e_raw[k][:, :], A["experts"][q]).then_inc(raw_in[k], 16)

            def load_wide(fb, q, k, value):
                if value is not None:
                    sp.wait_ge(weighted, value)
                rows = route_rows[f][bass.ds(2 * q, 2), fb * FB:(fb + 1) * FB]
                sp.dma_start(wide[k][:, :],
                             rows.rearrange("e (o c) -> e o c", o=1).broadcast_to([2, EI, FB])).then_inc(wide_in[k], 16)

            for fb in range(NFB):
                at = unit_base(f, fb)
                for k in range(2):
                    load_raw(fb, k, k, first=(f == 0 and fb == 0 and k == 0))
                sp.wait_ge(bank_free, first_unit["f", f, f"W{fb}"] + 2)
                tokens = slice(fb * FB, (fb + 1) * FB)
                sp.dma_start(route_rows[f][:, tokens], route_rows_sb[:, tokens]).then_inc(rows_out, 16)
                sp.wait_ge(rows_out, 16 * (2 * f + fb + 1))
                for k in range(2):
                    load_wide(fb, k, k, at - 2 * k if at else None)
                if fb and last:
                    for i in range(FB // QB):
                        sp.wait_ge(bank_free, first_unit["f", f, "F0"] + 2 * (i + 1))
                        store(i)
                with sp.Fori(1, PAIRS // 2) as i:
                    for k in range(2):
                        load_raw(fb, 2 * i + k, k)
                        load_wide(fb, 2 * i + k, k, at + 4 * i + 2 * k - 2)
                load_wide(fb, PAIRS, 0, at + 2 * PAIRS - 2)

        @block.sync
        def _(sp):
            def block_of(a, b):
                return a[b * QB:(b + 1) * QB, :].rearrange("(t p) e -> p t e", p=P)

            def store(b):
                sp.dma_start(block_of(A["out"], b), x[:, b * TPB:(b + 1) * TPB, :]).then_inc(x_out, 16)

            for b in range(NB):
                sp.dma_start(x[:, b * TPB:(b + 1) * TPB, :], block_of(A["x"], b)).then_inc(x_in[b], 16)
                if b == 0:
                    sp.dma_start(w_raw[:, 0:NWA], A["w_a"]).then_inc(w_in, 16)
            sp.dma_start(bias_cols[:, :], A["bias_cols"]).then_inc(consts_in, 16)
            sp.dma_start(bias_rows[:, :, :], A["bias_rows"].rearrange("(a r) e -> a r e", a=1)
                         .broadcast_to([P, 3, E])).then_inc(consts_in, 16)
            sp.dma_start(slope_raw[:, :], A["slopes"]).then_inc(consts_in, 16)
            sp.dma_start(w_post_raw[:, :], A["w_a_post"]).then_inc(wpost_in, 16)
            sp.wait_ge(slopes_ready, 2)
            for i, part in enumerate((slope_hi, slope_lo)):
                sp.dma_start(slope_parts[i, :, :].rearrange("h (k c) -> h k c", k=P // H),
                             part[:, :].bitcast(F32)).then_inc(const_out, 16)
            sp.wait_ge(fill_ready, 4)
            for c in range(S // FILL):
                cols = slice(c * FILL, (c + 1) * FILL)
                sp.dma_start(zero_rows[:, cols], fill[:, 0, :].bitcast(F32)).then_inc(const_out, 16)
                sp.dma_start(one_rows[:, cols], fill[0:2, 1, :].bitcast(F32)).then_inc(const_out, 16)
            for part in range(2):
                for h in range(2):
                    for row in range(2):
                        sp.dma_start(max_rows[2 * part + row, h, :].rearrange("(r c) -> r c", c=FILL),
                                     fill[0:S // FILL, int(row == h), :].bitcast(F32)).then_inc(const_out, 16)

            def attention(kind, layer):
                if layer == 1:
                    sp.wait_ge(product, first_unit[kind, layer, "T"])
                    sp.dma_start(w_raw[:, :], A["w_b"]).then_inc(w_in, 16)
                    sp.dma_start(w_post_raw[:, :], A["w_b_post"]).then_inc(wpost_in, 16)
                def load_fresh(s):
                    zeros = zero_rows.rearrange("r (o s) -> r o s", o=1).broadcast_to([ROWS_HEAD, 2, S])
                    sp.dma_start(Kp[s][ROWS_HEAD:2 * ROWS_HEAD, :, 0, :].bitcast(F32), zeros).then_inc(ops_in[s], 16)
                    sp.dma_start(Kp[s][0:ROWS_HEAD, :, 1, :].bitcast(F32), zeros).then_inc(ops_in[s], 16)
                    sp.dma_start(Qp[s][ROW_BIAS:ROW_MAX, :, :].bitcast(F32),
                                 one_rows.rearrange("r (o s) -> r o s", o=1).broadcast_to([2, 2, S])).then_inc(ops_in[s], 16)
                    for p in range(2):
                        sp.dma_start(Kp[s][ROW_MAX:ROWS, p, :, :].bitcast(F32), max_rows[:, :, :]).then_inc(ops_in[s], 16)

                def load_group(g, cols, done):
                    s, heads, n = g % 2, slice(GH * g, GH * (g + 1)), cols.stop - cols.start
                    sp.dma_start(Qp[s][0:2 * ROWS_HEAD, :, cols].bitcast(F32),
                                 q_parts[heads, :, cols].rearrange("(p h) r s -> (h r) p s", p=2)).then_inc(done, 16)
                    for hh in range(2):
                        sp.dma_start(Kp[s][hh * ROWS_HEAD:(hh + 1) * ROWS_HEAD, :, hh, cols].bitcast(F32),
                                     k_parts[heads, :, cols].rearrange("(p h) r s -> h r p s", p=2)[hh]).then_inc(done, 16)
                    if layer == 0:
                        bias = slope_parts[:, heads, cols]
                    else:
                        bias = zero_rows[0:2, cols].rearrange("r (o s) -> r o s", o=1).broadcast_to([2, GH, n])
                    sp.dma_start(Kp[s][ROW_BIAS:ROW_MAX, :, :, cols].bitcast(F32).rearrange("r p h s -> r (p h) s"), bias).then_inc(done, 16)

                for k, name in enumerate(STAGED[layer]):
                    if name == "K0":
                        sp.wait_ge(product, first_unit[kind, layer, "T"] + 2 * NB if layer == 0 else
                                   first_unit[kind, layer, "KL"] + NB)
                        if layer == 0:
                            sp.wait_ge(const_out, 16 * (2 + 2 * S // FILL + 8))
                        load_fresh(0)
                    for i in range(NB):
                        n = staged_no(layer, name, i)
                        sp.wait_ge(bank_free, first_unit[kind, layer, name] + i + 1)
                        dst, m = q_parts if name[0] == "Q" else k_parts, int(name[1])
                        out = dst[m * 8:(m + 1) * 8, :, i * QB:(i + 1) * QB]
                        order = (part_hi, part_hi, part_lo) if name[0] == "Q" else (part_hi, part_lo, part_hi)
                        for r, part in enumerate(order):
                            sp.dma_start(out[:, r * D:(r + 1) * D, :], part[n % NSTAGE][:, :].bitcast(F32))\
                                .then_inc(part_out[n % NSTAGE], 16)
                        if k and STAGED[layer][k - 1] == "K0":
                            before = staged_no(layer, "Q0", i)
                            sp.wait_ge(part_out[before % NSTAGE], 48 * (before // NSTAGE + 1))
                            before = staged_no(layer, "K0", i)
                            sp.wait_ge(part_out[before % NSTAGE], 48 * (before // NSTAGE + 1))
                            load_group(0, slice(i * QB, (i + 1) * QB), first_in[i])

                sp.wait_ge(product, first_unit[kind, layer, "core"])
                sp.wait_ge(bank_free, first_unit[kind, layer, "core"])
                for n in range(staged_no(layer, "K1", NB), staged_no(layer, "K1", NB) - NSTAGE, -1):
                    sp.wait_ge(part_out[(n - 1) % NSTAGE], 48 * ((n - 1) // NSTAGE + 1))
                load_fresh(1)
                load_group(1, slice(0, S), ops_in[1])
                for g in range(G):
                    for b in range(NB):
                        n = block_no(layer, g, b)
                        s = g % 2
                        sp.wait_ge(max_free, layer * MU + mu_of["turn", g, b] + 1)
                        for p in range(2):
                            for r, rows in ((ROW_MAX, neg_hi), (ROW_MAX + 2, neg_lo)):
                                sp.dma_start(Qp[s][r:r + 2, p, b * QB:(b + 1) * QB].bitcast(F32),
                                             rows[8 * p:8 * p + 8, n % 2, :].bitcast(F32)).then_inc(neg_in, 16)
                        sp.wait_ge(neg_in, 64 * (n + 1))
                        if b == NB - 2 and 1 <= g < G - 1:
                            sp.wait_ge(qk_product, 2 * (e_of[layer, g - 1, NB - 1, T - 1] + 1))
                            load_group(g + 1, slice(0, S), ops_in[s ^ 1])

            for kind, n in phases:
                if kind != "f":
                    attention(kind, n)
                else:
                    experts_dma(sp, n, (kind, n) == phases[-1], store)
            done = FB // QB if phases[-1][0] == "f" else 0
            sp.wait_ge(max_free, MU * sum(kind != "f" for kind, _ in phases))
            for b in range(done, NB):
                sp.wait_ge(bank_free, total_units - 2 * (NB - 1 - b) if done else total_units)
                store(b)
            sp.wait_ge(x_out, 16 * NB)

        def inverse_std(pool, n, b):
            if n < len(phases):
                pool.wait_ge(aggr_done, n * T + (b + 1) * TPB)
                tiles = slice(b * TPB, (b + 1) * TPB)
                pool.tensor_scalar(var_eps[:, tiles], mean_var[:, tiles, 1], EPS, None, ALU.add).then_inc(eps_done, 1)
                pool.wait_ge(eps_done, n * NB + b + 1)
                pool.tensor_tensor(rstd[:, tiles], var_eps[:, tiles], minus_half[:, :].broadcast_to([P, TPB]), ALU.pow)\
                    .then_inc(rstd_done, 1)

        def experts_pool(pool, f):
            pool.wait_ge(g_in, 16 * (f + 1))
            pool.tensor_copy(g_hi[:, :], g_raw[:, :]).then_inc(g_split, 1)
            pool.wait_ge(g_split, 2 * f + 1)
            pool.tensor_tensor(g_lo[:, :], g_raw[:, :], g_hi[:, :].bitcast(F32), ALU.subtract).then_inc(g_split, 1)

            def split(k, cols, high, low, value):
                pool.tensor_tensor(e_hi[k][:, cols], e_raw[k][:, cols], ones[:, :].broadcast_to([P, cols.stop - cols.start]),
                                   ALU.mult).then_inc(high, 1)
                pool.wait_ge(high, value)
                pool.tensor_tensor(e_lo[k][:, cols], e_raw[k][:, cols], e_hi[k][:, cols].bitcast(F32), ALU.subtract)\
                    .then_inc(low, 1)

            GU, DN = slice(0, EW - E), slice(EW - E, EW)
            pool.wait_ge(raw_in[2], 16 * (f + 1))
            split(2, GU, gu_high, gu_split, split_base(f, 0))
            split(2, DN, dn_high, dn_split, split_base(f, 0))
            for fb in range(NFB):
                at, sb = unit_base(f, fb), split_base(f, fb)
                loads = (f * NFB + fb) * PAIRS // 2

                def pair(i, k, used):
                    pool.wait_ge(raw_in[k], 16 * (loads + 1 + i))
                    if used is not None:
                        pool.wait_ge(gu_product, used)
                    split(k, GU, gu_high, gu_split, sb + 2 * i + k + 1)
                    if used is not None:
                        pool.wait_ge(down_done, used)
                    split(k, DN, dn_high, dn_split, sb + 2 * i + k + 1)

                for k in range(2):
                    pair(0, k, at - 4 + 2 * k if at else None)
                if fb == 1:
                    for b in range(FB // QB):
                        inverse_std(pool, norm_of["f", f] + 1, b)
                with pool.Fori(1, PAIRS // 2) as i:
                    for k in range(2):
                        pair(i, k, at + 4 * i + 2 * k - 2)
            for b in range(FB // QB, NB):
                inverse_std(pool, norm_of["f", f] + 1, b)

        @block.gpsimd
        def _(pool):
            pool.memset(ident[:, :], 0.0).then_inc(set_zero, 1)
            pool.memset(diag_mask[:, :], 0.0).then_inc(set_zero, 1)
            pool.memset(cut16[:, :], 0.0).then_inc(set_zero, 1)
            pool.wait_ge(set_zero, 3)
            pool.affine_select(out=ident[:, :], in_=ident[:, :], compare_op=ALU.not_equal, fill=1.0, base=0,
                               pattern=[[-1, P]], channel_multiplier=1).then_inc(ident_ready, 1)
            pool.affine_select(out=diag_mask[:, QB - P:QB], in_=diag_mask[:, QB - P:QB], compare_op=ALU.is_ge,
                               fill=NEG, base=0, pattern=[[-1, P]], channel_multiplier=1).then_inc(ident_ready, 1)
            pool.affine_select(out=cut16[:, :], in_=cut16[:, :], compare_op=ALU.is_ge, fill=NEG, base=0,
                               pattern=[[1, P]], channel_multiplier=-1).then_inc(ident_ready, 1)
            pool.wait_ge(ident_ready, 1)
            pool.tensor_copy(ident16[:, :], ident[:, :]).then_inc(ident_ready, 1)
            pool.memset(ones[:, :], 1.0).then_inc(fill_ready, 1)
            pool.memset(minus_half[:, :], -0.5).then_inc(fill_ready, 1)
            pool.memset(fill[:, 0, :].bitcast(F32), 0.0).then_inc(fill_ready, 1)
            pool.memset(fill[:, 1, :].bitcast(F32), 1.0).then_inc(fill_ready, 1)

            def attention(kind, layer):
                pool.wait_ge(fill_ready, 2)
                for b in range(2 if norm_of[kind, layer] == 0 else 0):
                    inverse_std(pool, 0, b)
                pool.wait_ge(w_in, 16 * (layer + 1))
                for name in W_ORDER[layer]:
                    cols = slice(W_OFF[name], W_OFF[name] + W_CHUNKS[name] * W_COLS[name])
                    pool.tensor_tensor(w_hi[:, cols], w_raw[:, cols], ones[:, :].broadcast_to([P, cols.stop - cols.start]),
                                       ALU.mult).then_inc(w_high, 1)
                    pool.wait_ge(w_high, w_ready(layer, name))
                    pool.tensor_tensor(w_lo[:, cols], w_raw[:, cols], w_hi[:, cols].bitcast(F32), ALU.subtract)\
                        .then_inc(w_split, 1)
                    if norm_of[kind, layer] == 0 and name == W_ORDER[layer][0]:
                        for b in range(2, NB):
                            inverse_std(pool, 0, b)
                if layer == 0:
                    pool.memset(values[:, :, :, D:2 * D], 0.0).then_inc(set_zero, 1)
                    pool.wait_ge(set_zero, 4)
                    pool.memset(values[:, :, :, D:D + 1], 1.0).then_inc(ident_ready, 1)
                pool.wait_ge(wpost_in, 16 * (layer + 1))
                wp = w_post_raw[:, :].rearrange("p (k e) -> p k e", k=KC)
                pool.tensor_copy(w_post[:, 0, :, :], wp).then_inc(wpost_split, 1)
                pool.wait_ge(wpost_split, 2 * layer + 1)
                pool.tensor_tensor(w_post[:, 1, :, :], wp, w_post[:, 0, :, :].bitcast(F32), ALU.subtract)\
                    .then_inc(wpost_split, 1)
                pool.wait_ge(consts_in, 48)
                pool.wait_ge(xn_done, T * (norm_of[kind, layer] + 1))
                pool.tensor_tensor(x[:, :, :], x[:, :, :], bias_rows[:, layer:layer + 1, :].broadcast_to([P, T, E]),
                                   ALU.add).then_inc(bias_added, 1)
                for b in range(NB):
                    inverse_std(pool, norm_of[kind, layer] + 1, b)

            for kind, n in phases:
                if kind != "f":
                    attention(kind, n)
                else:
                    experts_pool(pool, n)

        def experts_act(act, f, high_parts):
            phase = ("f", f)
            high_parts(phase, "T", KC * NB, turned(xT, 0))

            def route_exps(half):
                tiles = slice(half * RT, (half + 1) * RT)
                act.wait_ge(route_step, ROUTE_STEPS * (2 * f + half) + 2)
                act.activation(route[:, tiles, :], route[:, tiles, :], ACT.Exp).then_inc(route_exp, 1)

            route_exps(0)
            for fb in range(NFB):
                at = unit_base(f, fb)

                def unit(v, s, first=False):
                    act.wait_ge(gu_product, at + v + 1)
                    if not first:
                        act.wait_ge(gated, at + v - 1)
                    act.activation(silu[s][:, :], BANK[2 * s], ACT.Silu).then_inc(silu_done, 1)
                    act.wait_ge(weighted, at + v + 1)
                    if not first:
                        act.wait_ge(down_done, at + v - 1)
                    act.activation(i_hi[s][:, :], inter[s][:, :], ACT.Copy).then_inc(i_high, 1)

                for v in range(4):
                    unit(v, v % 2, first=(at == 0 and v < 2))
                    if fb == 0 and v == 1:
                        route_exps(1)
                with act.Fori(1, PAIRS // 2) as i:
                    for r in range(4):
                        unit(4 * i + r, r % 2)
                for v in range(2 * PAIRS, HU):
                    unit(v, v % 2)
                act.wait_ge(down_done, at + HU)
                if fb:
                    act.wait_ge(product, first_unit["f", f, "F0"] + 4)
                for n in range(2 * KC):
                    act.activation(moe_out[:, n // 2, (n % 2) * QB:(n % 2 + 1) * QB], BANK[4 + n], ACT.Copy)\
                        .then_inc(moe_sums, 1)

        @block.scalar
        def _(act):
            def high_parts(phase, name, count, dst, bias=None, rows=slice(0, P)):
                for i in range(count):
                    u = first_unit[(*phase, name)] + i
                    act.wait_ge(product, u + 1)
                    if phase[0] != "f" and name in STAGED[0]:
                        n = staged_no(phase[1], name, i)
                        if n >= NSTAGE:
                            act.wait_ge(part_out[n % NSTAGE], 48 * (n // NSTAGE))
                    bank = BANK[u % NBANK][rows, :]
                    if bias is None:
                        act.activation(dst(i), bank, ACT.Copy).then_inc(hi_done, 1)
                    else:
                        act.activation(dst(i), bank, ACT.Identity, bias=bias(i)).then_inc(hi_done, 1)

            def attention(kind, layer):
                phase = (kind, layer)
                high_parts(phase, "T", KC * NB, turned(xT, 0))
                for name in PROJECTIONS[layer]:
                    if name in STAGED[layer]:
                        bias = None if layer == 0 else bias_col("q" if name[0] == "Q" else "upk", int(name[1]))
                        high_parts(phase, name, NB, staged(layer, name, part_hi), bias)
                    elif name in ("V0", "V1"):
                        pass
                    elif name in ("VM", "KM"):
                        high_parts(phase, name, 2 * NB, in_block(mid, 0), bias_col(name[0].lower()))
                    else:
                        rows = LAT_OF[name]
                        high_parts(phase, name, NB, in_lat(name, 0), bias_col(name[0].lower() + "l", 0, rows), rows)
                act.wait_ge(product, first_unit[kind, layer, "core"])
                act.wait_ge(bank_free, first_unit[kind, layer, "core"])
                for item in plan:
                    if item[0] == "qk":
                        _, g, b, j, p, _ = item
                        e = e_of[layer, g, b, j]
                        off = P * max(0, j - TPB * b)
                        act.wait_ge(qk_product, 2 * e + p + 1)
                        if e >= NP:
                            act.wait_ge(pv_done, e - NP + 1)
                        act.activation(probs[:, e % NP, 2 * p:2 * p + 2, off:QB], exp_banks[p][:, :, off:QB],
                                       ACT.Exp, scale=D ** -0.5).then_inc(exp_done, 1)
                    elif item[0] == "out":
                        _, g, b = item
                        n = block_no(layer, g, b)
                        act.wait_ge(pv_done, e_of[layer, g, b, TPB * (b + 1) - 1] + 1)
                        if n % (G * NB) >= 2:
                            before = (g * NB + b - 2) // NB, (g * NB + b - 2) % NB
                            act.wait_ge(max_product, layer * MU + mu_of["ctx", before[0], before[1]] + 1)
                        act.activation(sums[:, n % 2, :], pv_banks[n % NPV][:, :], ACT.Copy).then_inc(sums_out, 1)
                    elif item[0] == "turn_ctx":
                        mu = layer * MU + mu_of[item]
                        act.wait_ge(max_product, mu + 1)
                        act.activation(turned(contextT, 0)(item[1] * KC + item[2]), max_banks[mu % NMAX][:, :], ACT.Copy)\
                            .then_inc(ctx_high, 1)

            act.wait_ge(consts_in, 48)
            act.activation(slope_hi[:, :], slope_raw[:, :], ACT.Copy).then_inc(slopes_ready, 1)
            for kind, n in phases:
                if kind != "f":
                    attention(kind, n)
                else:
                    experts_act(act, n, high_parts)

        def experts_pe(pe, f, turn, bank_of, three_passes):
            phase = ("f", f)
            turn(phase)
            pe.wait_ge(g_split, 2 * (f + 1))
            for i in range(NB):
                bank = bank_of(first_unit["f", f, "R"] + i)
                pe.wait_ge(bank_free, first_unit["f", f, "T"] + KC * (i + 1))
                for t in range(TPB):
                    cols = slice((i * TPB + t) * P, (i * TPB + t + 1) * P)
                    last = three_passes(bank[:, t * P:t * P + GC], lambda a, k: xT[:, a, k, cols],
                                        lambda c, k: (g_hi, g_lo)[c][:, k * GC:(k + 1) * GC], KC)
                last.then_inc(product, 1)

            def turn_routes(half):
                pe.wait_ge(route_step, ROUTE_STEPS * (2 * f + half + 1))
                for i in range(NB // 2):
                    bank = bank_of(first_unit["f", f, f"W{half}"] + i)
                    for t in range(TPB):
                        last = pe.transpose(bank[0:GC, t * P:(t + 1) * P], route[:, half * RT + i * TPB + t, :], ident[:, :])
                    last.then_inc(product, 1)

            turn_routes(0)
            for fb in range(NFB):
                at, sb = unit_base(f, fb), split_base(f, fb)
                pe.wait_ge(bank_free, first_unit["f", f, f"F{fb}"])

                def gate_up(v, k, s, new_pair, split_value, first=False):
                    if new_pair:
                        pe.wait_ge(gu_split, split_value)
                    if not first:
                        pe.wait_ge(gated, at + v - 1)
                    tokens = slice(fb * FB + s * QB, fb * FB + (s + 1) * QB)
                    for n in range(2):
                        last = three_passes(BANK[2 * s + n],
                                            lambda a, c: (e_hi, e_lo)[a][k][:, (2 * c + n) * P:(2 * c + n + 1) * P],
                                            lambda a, c: xT[:, a, c, tokens], KC)
                    last.then_inc(gu_product, 1)

                def down(v, k, s, new_pair, split_value, start=False, stop=False):
                    if new_pair:
                        pe.wait_ge(dn_split, split_value)
                    pe.wait_ge(i_split, at + v + 1)
                    for m in range(KC):
                        cols = slice(EW - E + m * P, EW - E + (m + 1) * P)
                        last = three_passes(BANK[4 + 2 * m + s], lambda a, c: (e_hi, e_lo)[a][k][:, cols],
                                            lambda a, c: (i_hi, i_lo)[a][s][:, :], 1, start, stop)
                    last.then_inc(down_done, 1)

                def four(i, first=False, last=False):
                    for r in range(4):
                        k, pair = (1, 2 * i + 1) if r < 2 else (0, 2 * i + 2)
                        if last and r >= 2:
                            gate_up(4 * i + r + 2, 2, r % 2, False, None)
                        else:
                            gate_up(4 * i + r + 2, k, r % 2, r % 2 == 0, sb + pair + 1)
                        down(4 * i + r, r // 2, r % 2, r % 2 == 0, sb + 2 * i + r // 2 + 1, start=first and r < 2)

                for v in range(2):
                    gate_up(v, 0, v, v == 0, sb + 1, first=True)
                four(0, first=True)
                with pe.Fori(1, PAIRS // 2 - 1) as i:
                    four(i)
                four(PAIRS // 2 - 1, last=True)
                for v in range(2 * PAIRS, HU):
                    down(v, 2, v % 2, False, None, stop=True)
                pe.wait_ge(moe_sums, 4 * (f * NFB + fb + 1))
                for i in range(FB // P // 2):
                    bank = bank_of(first_unit["f", f, f"F{fb}"] + i)
                    for n in range(2 * KC):
                        t, m = 2 * i + n // 2, n % 2
                        last = pe.transpose(bank[:, n * P:(n + 1) * P], moe_out[:, m, t * P:(t + 1) * P], ident[:, :])
                    last.then_inc(product, 1)
                if fb == 0:
                    turn_routes(1)

        @block.tensor
        def _(pe):
            def bank_of(u):
                if u >= NBANK:
                    pe.wait_ge(bank_free, u - NBANK + 1)
                return BANK[u % NBANK]

            def three_passes(out, stationary, moving, chunks, start=True, stop=True):
                order = [(k, a, c) for k in range(chunks) for a, c in ((0, 0), (0, 1), (1, 0))]
                for n, (k, a, c) in enumerate(order):
                    last = pe.matmul(out, stationary(a, k), moving(c, k), start=start and n == 0,
                                     stop=stop and n == len(order) - 1, skip_group_check=not (start and stop))
                return last

            def turn(phase):
                for i in range(KC * NB):
                    b, k = i // KC, i % KC
                    pe.wait_ge(xn_done, T * norm_of[phase] + (b + 1) * TPB)
                    bank = bank_of(first_unit[(*phase, "T")] + i)
                    for t in range(TPB):
                        last = pe.transpose(bank[:, t * P:(t + 1) * P], xn[:, b * TPB + t, k * P:(k + 1) * P], ident[:, :])
                    last.then_inc(product, 1)

            def features(phase, name, w, src, halves, chunks=KC, first=False):
                pe.wait_ge(w_split, w_ready(phase[1], w))
                for i in range(len(halves) * NB):
                    m, b = halves[i // NB], i % NB
                    bank = bank_of(first_unit[(*phase, name)] + i)
                    if first and i < NB:
                        pe.wait_ge(bank_free, first_unit[(*phase, "T")] + KC * (b + 1))
                    three_passes(bank, lambda a, k: weight((w_hi, w_lo)[a], w, k, slice(m * P, (m + 1) * P)),
                                 lambda c, k: src(c, k, slice(b * QB, (b + 1) * QB)), chunks).then_inc(product, 1)

            def latent(phase, name, w, since):
                pe.wait_ge(w_split, w_ready(phase[1], w))
                pe.wait_ge(bank_free, first_unit[(*phase, since)] + 2 * NB)
                for b in range(NB):
                    bank = bank_of(first_unit[(*phase, name)] + b)
                    three_passes(bank[0:W_COLS[w], :], lambda a, k: weight((w_hi, w_lo)[a], w, k, slice(0, W_COLS[w])),
                                 lambda c, k: mid[:, c, k, b * QB:(b + 1) * QB], KC).then_inc(product, 1)

            def token_pair(bank, pair, stationary, moving, chunks):
                for t in range(2):
                    last = three_passes(bank[:, t * E:(t + 1) * E], lambda a, k: stationary(a, k, 2 * pair + t),
                                        moving, chunks)
                return last

            def tokens_out(phase, name, stationary, moving, chunks, pairs):
                for i, pair in enumerate(pairs):
                    token_pair(bank_of(first_unit[(*phase, name)] + i), pair, stationary, moving, chunks).then_inc(product, 1)

            def from_xT(c, k, cols):
                return xT[:, c, k, cols]

            def max_bank(n):
                if n >= NMAX:
                    pe.wait_ge(max_free, n - NMAX + 1)
                return max_banks[n % NMAX]

            def attention(kind, layer):
                phase = (kind, layer)
                turn(phase)
                for name in PROJECTIONS[layer]:
                    if name in ("VM", "KM"):
                        features(phase, name, name[0].lower(), from_xT, (0, 1), first=name == "VM")
                    elif name in ("VL", "KL"):
                        latent(phase, name, name[0].lower() + "l", name[0] + "M")
                    elif name in ("V0", "V1"):
                        pairs = range(int(name[1]) * NB, (int(name[1]) + 1) * NB)
                        pe.wait_ge(w_split, w_ready(layer, "v" if layer == 0 else "upv"))
                        if layer == 0:
                            tokens_out(phase, name, lambda a, k, t: xT[:, a, k, t * P:(t + 1) * P],
                                       lambda c, k: weight((w_hi, w_lo)[c], "v", k, slice(0, E)), KC, pairs)
                        else:
                            tokens_out(phase, name, lambda a, k, t: lat[:, a, t * P:(t + 1) * P],
                                       lambda c, k: weight((w_hi, w_lo)[c], "upv", 0, slice(0, E)), 1, pairs)
                    elif layer == 1 and name[0] == "K":
                        pe.wait_ge(bank_free, first_unit[kind, layer, "KL"] + NB)
                        features(phase, name, "upk", lambda c, k, cols: lat[:, c, cols], (int(name[1]),), 1)
                    else:
                        features(phase, name, name[0].lower(), from_xT, (int(name[1]),), first=layer == 0 and name == "Q0")
                pe.wait_ge(bank_free, first_unit[kind, layer, "core"])
                pe.wait_ge(ident_ready, 5)
                begun = set()
                per_layer = (FRESH_LOADS + LOADS, FRESH_LOADS + 2 * LOADS)
                for item in plan:
                    if item[0] == "max":
                        _, g, h, t, c = item
                        s, p, hh = g % 2, h // 2, h % 2
                        if g not in begun:
                            begun.add(g)
                            count = FRESH_LOADS + LOADS * (g // 2 + s)
                            pe.wait_ge(ops_in[s], 16 * (layer * per_layer[s] + count))
                        if g == 0 and (g, t // TPB) not in begun:
                            begun.add((g, t // TPB))
                            pe.wait_ge(first_in[t // TPB], 16 * LOADS * (layer + 1))
                        n = min(QB, P * (t + 1) - QB * c)
                        bank = max_bank(layer * MU + mu_of[item])
                        pe.matmul(bank[:, 0:n], Qp[s][0:ROW_MAX, p, t * P:(t + 1) * P],
                                  Kp[s][0:ROW_MAX, p, hh, c * QB:c * QB + n], start=True, stop=True)\
                            .then_inc(max_product, 1)
                    elif item[0] == "turn":
                        _, g, b = item
                        n = block_no(layer, g, b)
                        bank = max_bank(layer * MU + mu_of[item])
                        pe.wait_ge(neg_done, n + 1)
                        pe.transpose(bank[0:GH * TPB, 0:P], neg_max[:, n % 2, :, :].rearrange("p h t -> p (h t)"),
                                     ident[:, :]).then_inc(max_product, 1)
                    elif item[0] == "qk":
                        _, g, b, j, p, _ = item
                        e = e_of[layer, g, b, j]
                        s = g % 2
                        off = P * max(0, j - TPB * b)
                        if j == 0 and p == 0:
                            pe.wait_ge(neg_in, 64 * (block_no(layer, g, b) + 1))
                        if e >= 1:
                            pe.wait_ge(exp_done, 2 * (e - 1) + p + 1)
                        for hh in range(2):
                            last = pe.matmul(exp_banks[p][:, hh, off:QB], Kp[s][0:ROWS, p, hh, j * P:(j + 1) * P],
                                             Qp[s][0:ROWS, p, b * QB + off:(b + 1) * QB], start=True,
                                             stop=j < TPB * b)
                            if j >= TPB * b:
                                last = pe.matmul(exp_banks[p][:, hh, off:off + P], ident16[:, :], cut16[:, :],
                                                 start=False, stop=True)
                        last.then_inc(qk_product, 1)
                    elif item[0] == "pv":
                        _, g, b, j, _ = item
                        e = e_of[layer, g, b, j]
                        off = P * max(0, j - TPB * b)
                        n = block_no(layer, g, b)
                        if j == 0 and n >= NPV:
                            pe.wait_ge(sums_out, n - NPV + 1)
                        pe.wait_ge(exp_done, 2 * (e + 1))
                        for h in range(GH):
                            last = pe.matmul(pv_banks[n % NPV][32 * h:32 * h + 32, off:QB],
                                             values[:, j, GH * g + h, :], probs[:, e % NP, h, off:QB],
                                             start=(j == 0), stop=(j == TPB * (b + 1) - 1))
                        last.then_inc(pv_done, 1)
                    elif item[0] == "ctx":
                        _, g, b = item
                        n = block_no(layer, g, b)
                        bank = max_bank(layer * MU + mu_of[item])
                        pe.wait_ge(sums_out, n + 1)
                        for t in range(TPB):
                            last = pe.transpose(bank[:, t * P:(t + 1) * P], sums[:, n % 2, t * P:(t + 1) * P], ident[:, :])
                        last.then_inc(max_product, 1)
                    elif item[0] == "turn_ctx":
                        _, b, k = item
                        bank = max_bank(layer * MU + mu_of[item])
                        pe.wait_ge(max_free, layer * MU + mu_of["ctx", G - 1, b] + 1)
                        for t in range(TPB):
                            last = pe.transpose(bank[:, t * P:(t + 1) * P], context[:, b * TPB + t, k * P:(k + 1) * P],
                                                ident[:, :])
                        last.then_inc(max_product, 1)
                    elif item[0] == "project":
                        i = item[1]
                        bank = max_bank(layer * MU + mu_of[item])
                        pe.wait_ge(max_free, layer * MU + mu_of["turn_ctx", 2 * i // TPB, KC - 1] + 1)
                        pe.wait_ge(wpost_split, 2 * (layer + 1))
                        token_pair(bank, i, lambda a, k, t: contextT[:, a, k, t * P:(t + 1) * P],
                                   lambda c, k: w_post[:, c, k, :], KC).then_inc(max_product, 1)
                pe.wait_ge(max_free, (layer + 1) * MU)

            pe.wait_ge(ident_ready, 1)
            for kind, n in phases:
                if kind != "f":
                    attention(kind, n)
                else:
                    experts_pe(pe, n, turn, bank_of, three_passes)

        def experts_dve(dve, f, norm_next, low_parts):
            phase = ("f", f)
            low_parts(phase, "T", KC * NB, turned(xT, 0), turned(xT, 1))
            for i in range(NB):
                u = first_unit["f", f, "R"] + i
                dve.wait_ge(product, u + 1)
                dve.tensor_copy(logits[:, i * TPB:(i + 1) * TPB, :],
                                BANK[u % NBANK].rearrange("p (t c) -> p t c", t=TPB)[:, :, 0:GC]).then_inc(bank_free, 1)
            dve.wait_ge(bank_free, first_unit["f", f, "R"] + NB)

            def routing(half):
                tiles = slice(half * RT, (half + 1) * RT)
                step = ROUTE_STEPS * (2 * f + half)
                logit, weight, picked = logits[:, tiles, 0:NEXP], route[:, tiles, 0:NEXP], chosen[:, tiles, :]
                for t in range(tiles.start, tiles.stop):
                    dve.max(top[:, t, :], logits[:, t, 0:NEXP]).then_inc(top_done, 1)
                dve.wait_ge(top_done, RT * (2 * f + half + 1))
                dve.tensor_tensor(weight, logit, top[:, tiles, 0:1].broadcast_to([P, RT, NEXP]), ALU.subtract)\
                    .then_inc(route_step, 1)
                dve.tensor_scalar(route[:, tiles, NEXP:GC], logits[:, tiles, NEXP:GC], -1.0, None, ALU.mult)\
                    .then_inc(route_step, 1)
                for t in range(tiles.start, tiles.stop):
                    dve.match_replace(out=chosen[:, t, :], in_to_replace=top[:, t, :], in_values=logits[:, t, 0:NEXP],
                                      imm_value=VLOW).then_inc(route_step, 1)
                dve.wait_ge(route_step, step + 2 + RT)
                dve.tensor_tensor(picked, picked, logit, ALU.not_equal).then_inc(route_step, 1)
                dve.wait_ge(route_exp, 2 * f + half + 1)
                dve.wait_ge(route_step, step + 3 + RT)
                dve.tensor_tensor(weight, weight, picked, ALU.mult).then_inc(route_step, 1)
                dve.wait_ge(route_step, step + 4 + RT)
                dve.tensor_reduce(route_sum[:, tiles], weight, AX.X, ALU.add).then_inc(route_step, 1)
                dve.wait_ge(route_step, step + 5 + RT)
                dve.reciprocal(route_inv[:, tiles], route_sum[:, tiles]).then_inc(route_step, 1)
                gate = route[:, tiles, NEXP:NEXP + 1]
                dve.tensor_scalar(gate, gate, 1.0, None, ALU.add).then_inc(route_step, 1)
                dve.wait_ge(route_step, step + 7 + RT)
                inv = route_inv[:, tiles].rearrange("p (t o) -> p t o", o=1).broadcast_to([P, RT, NEXP])
                dve.tensor_tensor(weight, weight, inv, ALU.mult).then_inc(route_step, 1)
                dve.reciprocal(gate, gate).then_inc(route_step, 1)
                dve.memset(route[:, tiles, NEXP + 1:GC], 0.0).then_inc(route_step, 1)

            def rows_out_of_psum(half):
                for i in range(NB // 2):
                    u = first_unit["f", f, f"W{half}"] + i
                    dve.wait_ge(product, u + 1)
                    cols = slice(half * FB + i * QB, half * FB + (i + 1) * QB)
                    dve.tensor_copy(route_rows_sb[:, cols], BANK[u % NBANK][0:GC, :]).then_inc(bank_free, 1)

            routing(0)
            rows_out_of_psum(0)
            for fb in range(NFB):
                at = unit_base(f, fb)
                loads = [(f * NFB + fb) * (PAIRS // 2 + 1), (f * NFB + fb) * PAIRS // 2]

                def unit(v, s, k, load, first=False):
                    dve.wait_ge(silu_done, at + v + 1)
                    if not first:
                        dve.wait_ge(i_split, at + v - 1)
                    dve.tensor_tensor(inter[s][:, :], BANK[2 * s + 1], silu[s][:, :], ALU.mult).then_inc(gated, 1)
                    if s == 0:
                        dve.wait_ge(wide_in[k], 16 * load)
                    dve.wait_ge(gated, at + v + 1)
                    dve.tensor_tensor(inter[s][:, :], inter[s][:, :], wide[k][:, s * QB:(s + 1) * QB], ALU.mult)\
                        .then_inc(weighted, 1)
                    dve.wait_ge(i_high, at + v + 1)
                    if not first:
                        dve.wait_ge(down_done, at + v - 1)
                    dve.tensor_tensor(i_lo[s][:, :], inter[s][:, :], i_hi[s][:, :].bitcast(F32), ALU.subtract)\
                        .then_inc(i_split, 1)

                for v in range(4):
                    unit(v, v % 2, v // 2, loads[v // 2] + 1, first=(at == 0 and v < 2))
                    if fb == 0 and v == 1:
                        routing(1)
                with dve.Fori(1, PAIRS // 2) as i:
                    for r in range(4):
                        unit(4 * i + r, r % 2, r // 2, loads[r // 2] + 1 + i)
                for v in range(2 * PAIRS, HU):
                    unit(v, v % 2, 0, loads[0] + PAIRS // 2 + 1)
                for i in range(FB // P // 2):
                    u = first_unit["f", f, f"F{fb}"] + i
                    dve.wait_ge(product, u + 1)
                    t = fb * FB // P + 2 * i
                    dve.tensor_tensor(x[:, t:t + 2, :], BANK[u % NBANK].rearrange("p (t e) -> p t e", t=2),
                                      x[:, t:t + 2, :], ALU.add).then_inc(bank_free, 1)
                if fb == 0:
                    rows_out_of_psum(1)
                for b in range(fb * FB // QB, (fb + 1) * FB // QB):
                    dve.wait_ge(bank_free, first_unit["f", f, f"F{fb}"] + 2 * (b - fb * FB // QB) + 2)
                    norm_next(phase, b)

        @block.vector
        def _(dve):
            def norm_block(n, b):
                tiles = range(b * TPB, (b + 1) * TPB)
                for t in tiles:
                    dve.bn_stats(stats[:, t, :], x[:, t, :]).then_inc(stats_done, 1)
                for t in tiles:
                    dve.wait_ge(stats_done, n * T + t + 1)
                    dve.bn_aggr(mean_var[:, t, :], stats[:, t, :]).then_inc(aggr_done, 1)
                dve.wait_ge(rstd_done, n * NB + b + 1)
                for t in tiles:
                    dve.tensor_scalar(xn[:, t, :], x[:, t, :], mean_var[:, t, 0:1], rstd[:, t:t + 1],
                                      ALU.subtract, ALU.mult).then_inc(xn_done, 1)

            def norm_next(phase, b):
                if norm_of[phase] + 1 < len(phases):
                    norm_block(norm_of[phase] + 1, b)

            def low_parts(phase, name, count, hi, lo, bias=None, rows=slice(0, P)):
                for i in range(count):
                    u = first_unit[(*phase, name)] + i
                    dve.wait_ge(hi_done, first_hi[(*phase, name)] + i + 1)
                    bank = BANK[u % NBANK][rows, :]
                    if bias is None:
                        dve.tensor_tensor(lo(i), bank, hi(i).bitcast(F32), ALU.subtract).then_inc(bank_free, 1)
                    else:
                        dve.scalar_tensor_tensor(out=lo(i), in0=bank, scalar=bias(i), in1=hi(i).bitcast(F32),
                                                 op0=ALU.add, op1=ALU.subtract).then_inc(bank_free, 1)

            def attention(kind, layer):
                phase = (kind, layer)

                def values_out(first, at):
                    for i in range(NB):
                        dve.wait_ge(product, first + i + 1)
                        for t in range(2):
                            bank = BANK[(first + i) % NBANK][:, t * E:(t + 1) * E].rearrange("p (h d) -> p h d", h=H)
                            dst = values[:, 2 * (at + i) + t, :, 0:D]
                            if layer == 0:
                                op = dve.tensor_copy(dst, bank)
                            else:
                                op = dve.tensor_tensor(dst, bank, bias_rows[:, 2, :].rearrange("p (h d) -> p h d", h=H), ALU.add)
                        op.then_inc(bank_free, 1)

                low_parts(phase, "T", KC * NB, turned(xT, 0), turned(xT, 1))
                for name in PROJECTIONS[layer]:
                    if name in STAGED[layer]:
                        bias = None if layer == 0 else bias_col("q" if name[0] == "Q" else "upk", int(name[1]))
                        low_parts(phase, name, NB, staged(layer, name, part_hi), staged(layer, name, part_lo), bias)
                    elif name in ("V0", "V1"):
                        values_out(first_unit[kind, layer, name], int(name[1]) * NB)
                    elif name in ("VM", "KM"):
                        low_parts(phase, name, 2 * NB, in_block(mid, 0), in_block(mid, 1), bias_col(name[0].lower()))
                    else:
                        rows = LAT_OF[name]
                        low_parts(phase, name, NB, in_lat(name, 0), in_lat(name, 1),
                                  bias_col(name[0].lower() + "l", 0, rows), rows)
                dve.wait_ge(product, first_unit[kind, layer, "core"])
                dve.wait_ge(bank_free, first_unit[kind, layer, "core"])
                if layer == 0:
                    dve.wait_ge(ident_ready, 2)
                masked_at = []
                begun = set()
                for item in plan:
                    if item[0] == "max":
                        _, g, h, t, c = item
                        b, n = t // TPB, min(QB, P * (t + 1) - QB * c)
                        bn = block_no(layer, g, b)
                        mu = layer * MU + mu_of[item]
                        slot = bn % 2
                        if bn not in begun:
                            begun.add(bn)
                            if bn >= 2:
                                dve.wait_ge(neg_done, bn - 1)
                        bank = max_banks[mu % NMAX]
                        dve.wait_ge(max_product, mu + 1)
                        to = chunk_max[:, slot, h, t % TPB, c:c + 1]
                        if c == b:
                            k = len(masked_at)
                            if k >= 2:
                                dve.wait_ge(max_free, masked_at[k - 2] + 1)
                            dve.tensor_tensor_reduce(masked[k % 2][:, 0:n], bank[:, 0:n], diag_mask[:, QB - n:QB],
                                                     1.0, VLOW, ALU.add, ALU.max, to).then_inc(max_free, 1)
                            masked_at.append(mu)
                        else:
                            dve.tensor_reduce(to, bank[:, 0:n], AX.X, ALU.max).then_inc(max_free, 1)
                        if t % TPB == TPB - 1 and h == GH - 1 and c == b:
                            dve.wait_ge(max_free, mu + 1)
                            if bn >= 2:
                                last = divmod(g * NB + b - 2, NB) if g * NB + b >= 2 else divmod(G * NB + b - 2, NB)
                                base = layer * MU if g * NB + b >= 2 else (layer - 1) * MU
                                dve.wait_ge(max_product, base + mu_of[("turn", *last)] + 1)
                            dve.tensor_reduce(neg_max[:, slot, :, :], chunk_max[:, slot, :, :, 0:b + 1], AX.X, ALU.max,
                                              negate=True).then_inc(neg_done, 1)
                    elif item[0] == "turn":
                        _, g, b = item
                        n = block_no(layer, g, b)
                        mu = layer * MU + mu_of[item]
                        bank = max_banks[mu % NMAX][0:GH * TPB, 0:P]
                        dve.wait_ge(max_product, mu + 1)
                        if n >= 2:
                            dve.wait_ge(neg_in, 64 * (n - 1))
                        dve.tensor_copy(neg_hi[:, n % 2, :], bank).then_inc(neg_high, 1)
                        dve.wait_ge(neg_high, n + 1)
                        dve.tensor_tensor(neg_lo[:, n % 2, :], bank, neg_hi[:, n % 2, :].bitcast(F32), ALU.subtract)\
                            .then_inc(max_free, 1)
                    elif item[0] == "ctx":
                        _, g, b = item
                        n = block_no(layer, g, b)
                        mu = layer * MU + mu_of[item]
                        dve.wait_ge(max_product, mu + 1)
                        if n >= 2:
                            dve.wait_ge(inv_done, n - 1)
                        bank = max_banks[mu % NMAX][:, :].rearrange("p (t r) -> p t r", r=2 * D)
                        dve.reciprocal(inv_den[:, n % 2, :], bank[:, :, D]).then_inc(inv_done, 1)
                        dve.wait_ge(inv_done, n + 1)
                        out = context[:, b * TPB:(b + 1) * TPB, g * GH * D:(g + 1) * GH * D]
                        inv = inv_den[:, n % 2, :].rearrange("p (t h o) -> p t h o", h=GH, o=1)
                        dve.tensor_tensor(out.rearrange("p t (h d) -> p t h d", h=GH),
                                          bank[:, :, 0:D].rearrange("p (t h) d -> p t h d", h=GH),
                                          inv.broadcast_to([P, TPB, GH, D]), ALU.mult).then_inc(max_free, 1)
                    elif item[0] == "turn_ctx":
                        _, b, k = item
                        i = b * KC + k
                        mu = layer * MU + mu_of[item]
                        dve.wait_ge(ctx_high, layer * KC * NB + i + 1)
                        dve.tensor_tensor(turned(contextT, 1)(i), max_banks[mu % NMAX][:, :],
                                          turned(contextT, 0)(i).bitcast(F32), ALU.subtract).then_inc(max_free, 1)
                    elif item[0] == "project":
                        i = item[1]
                        mu = layer * MU + mu_of[item]
                        dve.wait_ge(max_product, mu + 1)
                        dve.wait_ge(bias_added, layer + 1)
                        pair = x[:, 2 * i:2 * i + 2, :]
                        dve.tensor_tensor(pair, max_banks[mu % NMAX][:, :].rearrange("p (t e) -> p t e", t=2), pair, ALU.add)\
                            .then_inc(max_free, 1)
                        if i % 2:
                            dve.wait_ge(max_free, mu + 1)
                            norm_next(phase, i // 2)

            dve.wait_ge(slopes_ready, 1)
            dve.tensor_tensor(slope_lo[:, :], slope_raw[:, :], slope_hi[:, :].bitcast(F32), ALU.subtract)\
                .then_inc(slopes_ready, 1)
            for b in range(NB):
                dve.wait_ge(x_in[b], 16)
                norm_block(0, b)
            for kind, n in phases:
                if kind != "f":
                    attention(kind, n)
                else:
                    experts_dve(dve, n, norm_next, low_parts)


_INPUTS = ("x", "w_a", "w_a_post", "w_b", "w_b_post", "bias_cols", "bias_rows", "slopes", "router", "experts")


def lay_out(L):
    def chunks(w):
        return w.reshape(KC, P, -1).transpose(1, 0, 2).reshape(P, -1)

    def top(w):
        return np.concatenate([w, np.zeros_like(w)], 0)

    def bottom(w):
        return np.concatenate([np.zeros_like(w), w], 0)

    a = {k[len("L0_attn_a_"):]: np.asarray(v) for k, v in L.items() if k.startswith("L0_attn_a_")}
    b = {k[len("L0_attn_b_"):]: np.asarray(v) for k, v in L.items() if k.startswith("L0_attn_b_")}
    f = {k[len("L0_ffn_"):]: np.asarray(v) for k, v in L.items() if k.startswith("L0_ffn_")}
    up = {n: b[f"up{n}_w"].transpose(1, 0, 2).reshape(DL, E) for n in "kv"}
    w_a = np.concatenate([chunks(a["Wq"]), chunks(a["Wk"]), chunks(a["Wv"])], 1)
    w_b = np.concatenate([chunks(b["wq_w"]), chunks(b["wk_w"]), chunks(b["wv_w"]), chunks(bottom(b["wkl_w"].T).T),
                          chunks(b["wvl_w"]), bottom(up["k"]), top(up["v"])], 1)
    bias_cols = np.stack([b["wq_b"][0:P], b["wq_b"][P:E], b["wk_b"][0:P], b["wk_b"][P:E], b["wv_b"][0:P], b["wv_b"][P:E],
                          b["upk_b"].reshape(E)[0:P], b["upk_b"].reshape(E)[P:E], bottom(b["wkl_b"]), top(b["wvl_b"])], 1)
    bias_rows = np.stack([a["bo"], b["wo_b"], b["upv_b"].reshape(E)])
    slope = (2.0 ** (-8.0 * np.arange(1, H + 1) / H)).astype(np.float32)
    slopes = slope[:, None] * (np.arange(S) - S // 2).astype(np.float32)[None, :]
    router = chunks(np.concatenate([f["gate_w"], f["sh_gate1_w"], np.zeros_like(f["sh_gate1_w"])], 0).T)
    pad = np.zeros((1, EI, E), np.float32)
    gate = np.concatenate([f["gu_w"][:, 0:EI], f["sh_gate_w"][None], pad], 0)
    upw = np.concatenate([f["gu_w"][:, EI:], f["sh_up_w"][None], pad], 0)
    down = np.concatenate([f["dp_w"].transpose(0, 2, 1), f["sh_down_w"].T[None], pad], 0)
    gu = np.stack([gate.reshape(PAIRS + 1, P, KC, P), upw.reshape(PAIRS + 1, P, KC, P)], 0)
    gu = gu.transpose(1, 4, 3, 0, 2).reshape(PAIRS + 1, P, KC * 2 * P)
    experts = np.concatenate([gu, down.reshape(PAIRS + 1, P, E)], 2)
    return {"x": a["x"].reshape(S, E), "w_a": w_a, "w_a_post": chunks(a["Wo"]), "w_b": w_b, "w_b_post": chunks(b["wo_w"]),
            "bias_cols": bias_cols, "bias_rows": bias_rows, "slopes": slopes.reshape(P, -1), "router": router,
            "experts": experts}


def kernel(**inputs):
    import concourse.bacc as bacc
    from concourse.bass_utils import run_bass_kernel_spmd

    nc = bacc.Bacc("TRN2", target_bir_lowering=False, num_devices=1)
    laid = lay_out(inputs)
    arrays, aps = {}, {}
    for name in _INPUTS:
        array = np.ascontiguousarray(laid[name])
        arrays[f"in_{name}"] = array
        aps[name] = nc.dram_tensor(f"in_{name}", array.shape, mybir.dt.from_np(array.dtype), kind="ExternalInput").ap()
    aps["out"] = nc.dram_tensor("result", (S, E), F32, kind="ExternalOutput").ap()
    build(nc, aps)
    got = run_bass_kernel_spmd(nc, [arrays], core_ids=[0])
    return got.results[0]["result"].reshape(1, S, E)
```

```python
from contextlib import ExitStack

import numpy as np

import concourse.bass as bass
from concourse import mybir

F32 = mybir.dt.float32
F32R = mybir.dt.float32r
BF16 = mybir.dt.bfloat16
ALU = mybir.AluOpType
ACT = mybir.ActivationFunctionType
AX = mybir.AxisListType

P = 128
S = 2048
E = 256
T = S // P
KC = E // P
QB = 512
NB = S // QB
TPB = QB // P
H = 16
D = E // H
DL = 64
EPS = 1e-5
NEG = -1e30
VLOW = -3e38

Q_PARTS, K_PARTS = (0, 0, 1), (0, 1, 0)
PAIR = 2 * D
ROW_BIAS = len(Q_PARTS) * PAIR
ROW_MAX = ROW_BIAS + 2
ROWS = ROW_MAX + 4
GH = 4
G = H // GH
UP, DOWN = list(range(NB)), list(range(NB))[::-1]
BLOCKS = [(g, b) for g in range(G) for b in (UP if g < G - 1 else DOWN)]
NP = 3
FILL = 256
NSTAGE = 3
NMAX, NPV = 3, 1

NEXP = 64
EI = 64
TOPK = 8
GC = NEXP + 2
PAIRS = NEXP // 2
RT = T // 2
ROUTE_STEPS = RT + 10
EW = KC * 2 * P + E
FB = 1024
NFB = S // FB


W_COLS = {"q": E, "k": E, "v": E, "kl": 2 * DL, "vl": DL, "upk": E, "upv": E}
W_CHUNKS = {"q": KC, "k": KC, "v": KC, "kl": KC, "vl": KC, "upk": 1, "upv": 1}
W_OFF, NWB = {}, 0
for _name in W_COLS:
    W_OFF[_name] = NWB
    NWB += W_COLS[_name] * W_CHUNKS[_name]
NWA = W_OFF["kl"]
W_ORDER = [["q", "k", "v"], ["k", "q", "kl", "upk", "v", "vl", "upv"]]
STAGED = ["Q0", "K0", "Q1", "K1"]
LOADS_AFTER = {"K0": "fresh", "Q1": 0, "K1": 1}


def core_plan():
    SIGNAL, ROWS_BACK, LOAD = 250, 7000, 12000

    maxima = []
    for number, (g, b) in enumerate(BLOCKS):
        pending = ("turn", *BLOCKS[number - 1]) if number else None
        for t in range(b * TPB, (b + 1) * TPB):
            for h in range(GH):
                for c in range(t // TPB + 1):
                    maxima.append(("max", g, h, t, c))
                    if pending and (h, t, c) == (1, b * TPB, 0):
                        maxima.append(pending)
    maxima.append(("turn", *BLOCKS[-1]))
    units = [(g, b, j) for g, b in BLOCKS for j in range(TPB * (b + 1))]
    scores = [("qk", g, b, j, p, e) for e, (g, b, j) in enumerate(units) for p in range(2)]
    sums = [("pv", g, b, j, e) for e, (g, b, j) in enumerate(units)]
    contexts = []
    for g, b in BLOCKS:
        contexts.append(("ctx", g, b))
        if g == G - 1:
            contexts += [("turn_ctx", b, k) for k in range(KC)]
            contexts += [("project", i) for i in range(b * TPB // 2, (b + 1) * TPB // 2)]
    streams = [contexts, maxima, scores, sums]
    at = [0] * 4

    plan = []
    pe = dve = act = 0.0
    max_bank_free = [0.0] * NMAX
    exp_bank_free = [0.0] * 2
    uses = 0
    context_at = 0.0
    reduced, turned, loaded = {}, {}, {0: 0.0, 1: 0.0}
    exps, products, scored, summed = {}, {}, {}, {}

    def width(b, j):
        return QB - P * max(0, j - TPB * b)

    def ready(item):
        kind, g = item[0], item[1]
        if kind in ("max", "turn", "ctx"):
            bank = max_bank_free[uses % NMAX]
            if kind == "max":
                return max(bank, loaded[g]) if g in loaded else None
            if kind == "turn":
                return max(bank, reduced[item[1:]]) if item[1:] in reduced else None
            return max(bank, summed[item[1:]]) if item[1:] in summed else None
        if kind in ("turn_ctx", "project"):
            return max(max_bank_free[uses % NMAX], context_at)
        if kind == "qk":
            return max(exp_bank_free[item[4]], turned[item[1:3]]) if item[1:3] in turned and \
                (item[5] < NP or item[5] - NP in products) else None
        n = BLOCKS.index(item[1:3])
        if item[3] == TPB * (item[2] + 1) - 1 and n >= 2 and ("ctx", *BLOCKS[n - 2]) in contexts[at[0]:]:
            return None
        return exps.get((item[4], 1))

    while any(at[k] < len(s) for k, s in enumerate(streams)):
        best = None
        for k, s in enumerate(streams):
            if at[k] < len(s):
                when = ready(s[at[k]])
                if when is not None:
                    when = max(when, pe)
                    if best is None or when < best[0]:
                        best = (when, k)
        start, k = best
        item = streams[k][at[k]]
        at[k] += 1
        plan.append(item)
        kind, g = item[0], item[1]
        if kind == "max":
            _, g, h, t, c = item
            n = min(QB, P * (t + 1) - QB * c)
            pe = start + n / 2.4 + 3
            dve = max(dve, pe + SIGNAL) + n / 0.96 + 75
            max_bank_free[uses % NMAX] = dve + 50
            uses += 1
            if h == GH - 1 and t % TPB == TPB - 1 and c == t // TPB:
                dve += 250
                reduced[g, t // TPB] = dve + 50
        elif kind == "turn":
            pe = start + 110
            dve = max(dve, pe + SIGNAL) + 600
            max_bank_free[uses % NMAX] = dve + 50
            uses += 1
            turned[item[1:]] = dve + ROWS_BACK
        elif kind == "ctx":
            pe = start + 450
            dve = max(dve, pe + SIGNAL) + 550
            max_bank_free[uses % NMAX] = context_at = dve + 50
            uses += 1
        elif kind == "turn_ctx":
            pe = start + 450
            act = max(act, pe + SIGNAL) + 600
            dve = max(dve, act + 50) + 600
            max_bank_free[uses % NMAX] = dve + 50
            uses += 1
            context_at = dve + 50 if item[2] == KC - 1 else pe
        elif kind == "project":
            pe = start + 12 * 110
            dve = max(dve, pe + SIGNAL) + 600
            max_bank_free[uses % NMAX] = dve + 50
            uses += 1
            context_at = pe
            dve += 3200 * (item[1] % 2)
        elif kind == "qk":
            _, g, b, j, p, e = item
            n = width(b, j)
            pe = start + 2 * (n / 2.4 + 3) + (120 if j >= TPB * b else 0)
            free = products[e - NP] if e >= NP else 0
            act = max(act, pe + SIGNAL, free) + 2 * n / 1.2 + 60
            exp_bank_free[p] = act + 50
            exps[e, p] = act + 50
            if j == T - 1 and p == 1 and g + 2 < G:
                loaded[g + 2] = max(pe, turned[g + 1, NB - 2] if (g + 1, NB - 2) in turned else pe) + LOAD
        elif kind == "pv":
            _, g, b, j, e = item
            n = width(b, j)
            pe = start + 4 * (n / 2.4 + 3) + 100
            products[e] = pe + SIGNAL
            if j == TPB * (b + 1) - 1:
                act = max(act, pe + SIGNAL) + 600
                summed[g, b] = act + 50
                plan.append(("out", g, b))
    return plan


def build(nc, A, parts="afbf"):
    plan = core_plan()
    ctx = ExitStack()
    with ctx:
        def sem(name):
            return ctx.enter_context(nc.semaphore(name))

        def tile(name, shape, dt=F32, stack=ctx):
            return stack.enter_context(nc.sbuf_tensor(f"{name}_t", shape, dt))

        exp_banks = [ctx.enter_context(nc.psum_tensor(f"exp_banks{i}", [P, 2, QB], F32)) for i in range(2)]
        max_banks = [ctx.enter_context(nc.psum_tensor(f"max_bank{i}", [P, QB], F32)) for i in range(NMAX)]
        pv_banks = [ctx.enter_context(nc.psum_tensor(f"pv_bank{i}", [P, QB], F32)) for i in range(NPV)]
        BANK = [exp_banks[0][:, 0, :], exp_banks[0][:, 1, :], exp_banks[1][:, 0, :], exp_banks[1][:, 1, :],
                *(bank[:, :] for bank in max_banks + pv_banks)]
        NBANK = len(BANK)

        x = tile("x_sb", [P, T, E])
        ident = tile("ident", [P, P])
        ones = tile("ones", [P, 1])
        g_hi = tile("g_hi", [P, KC * GC], F32R)
        g_lo = tile("g_lo", [P, KC * GC], F32R)
        minus_half = tile("minus_half", [P, 1])
        var_eps = tile("var_eps", [P, T])
        diag_mask = tile("diag_mask", [P, QB])
        ident16 = tile("ident16", [P, P], BF16)
        cut16 = tile("cut16", [P, P], BF16)
        values = tile("values", [P, T, H, 2 * D])
        w_post_raw = tile("w_post_raw", [P, KC * E])
        w_post = tile("w_post", [P, 2, KC, E], F32R)
        bias_cols = tile("bias_cols", [P, 10])
        bias_rows = tile("bias_rows", [P, 3, E])
        stats = tile("stats", [P, T, 6])
        mean_var = tile("mean_var", [P, T, 2])
        rstd = tile("rstd", [P, T])

        outer = ExitStack()
        xT = tile("xT", [P, 2, KC, S], F32R, outer)
        xn = tile("xn", [P, T, E], F32, outer)
        pre = ExitStack()
        mid = tile("mid", [P, 2, KC, S], F32R, pre)
        lat = tile("lat", [P, 2, S], F32R, pre)
        part_hi = [tile(f"part_hi{i}", [P, QB], F32R, pre) for i in range(NSTAGE)]
        part_lo = [tile(f"part_lo{i}", [P, QB], F32R, pre) for i in range(NSTAGE)]
        w_raw = tile("w_raw", [P, NWB], F32, pre)
        w_hi = tile("w_hi", [P, NWB], F32R, pre)
        w_lo = tile("w_lo", [P, NWB], F32R, pre)
        g_raw = tile("g_raw", [P, KC * GC], F32, pre)
        slope_raw = tile("slope_raw", [P, S * H // P], F32, pre)
        slope_hi = tile("slope_hi", [P, S * H // P], F32R, pre)
        slope_lo = tile("slope_lo", [P, S * H // P], F32R, pre)
        fill = tile("fill", [D, 2, FILL], F32R, pre)
        pre.close()
        moe = ExitStack()
        logits = tile("logits", [P, T, GC], F32, moe)
        top = tile("top", [P, T, TOPK], F32, moe)
        route = tile("route", [P, T, GC], F32, moe)
        chosen = tile("chosen", [P, T, NEXP], F32, moe)
        route_sum = tile("route_sum", [P, T], F32, moe)
        route_inv = tile("route_inv", [P, T], F32, moe)
        route_rows_sb = tile("route_rows_sb", [GC, S], F32, moe)
        e_raw = [tile(f"e_raw{i}", [P, EW], F32, moe) for i in range(3)]
        e_hi = [tile(f"e_hi{i}", [P, EW], F32R, moe) for i in range(3)]
        e_lo = [tile(f"e_lo{i}", [P, EW], F32R, moe) for i in range(3)]
        wide = [tile(f"wide{i}", [P, FB], F32, moe) for i in range(2)]
        silu = [tile(f"silu{i}", [P, QB], F32, moe) for i in range(2)]
        inter = [tile(f"inter{i}", [P, QB], F32, moe) for i in range(2)]
        i_hi = [tile(f"i_hi{i}", [P, QB], F32R, moe) for i in range(2)]
        i_lo = [tile(f"i_lo{i}", [P, QB], F32R, moe) for i in range(2)]
        moe_out = tile("moe_out", [P, KC, FB], F32, moe)
        moe.close()
        outer.close()

        core = ExitStack()
        Qp, Kp = [None, None], [None, None]
        Qp[1] = tile("Qp1", [P, 2, S], F32R, core)
        context = tile("context", [P, T, E], F32, core)
        Qp[0] = tile("Qp0", [P, 2, S], F32R, core)
        Kp[0] = tile("Kp0", [P, 2, 2, S], F32R, core)
        Kp[1] = tile("Kp1", [P, 2, 2, S], F32R, core)
        contextT = Kp[0]
        probs = tile("probs", [P, NP, GH, QB], F32, core)
        masked = [tile(f"masked{i}", [P, QB], BF16, core) for i in range(2)]
        chunk_max = tile("chunk_max", [P, 2, GH, TPB, NB], F32, core)
        neg_max = tile("neg_max", [P, 2, GH, TPB], F32, core)
        neg_hi = tile("neg_hi", [GH * TPB, 2, P], F32R, core)
        neg_lo = tile("neg_lo", [GH * TPB, 2, P], F32R, core)
        sums = tile("sums", [P, 2, QB], F32, core)
        inv_den = tile("inv_den", [P, 2, TPB * GH], F32, core)
        core.close()

        q_parts = nc.dram_tensor("q_parts", [2, E, S], F32).ap()
        k_parts = nc.dram_tensor("k_parts", [2, E, S], F32).ap()
        slope_parts = nc.dram_tensor("slope_parts", [2, H, S], F32).ap()
        zero_rows = nc.dram_tensor("zero_rows", [D, 2 * S], F32).ap()
        one_rows = nc.dram_tensor("one_rows", [2, S], F32).ap()
        max_rows = nc.dram_tensor("max_rows", [4, 2, S], F32).ap()
        route_rows = [nc.dram_tensor(f"route_rows{f}", [GC, S], F32).ap() for f in range(2)]

        x_in = [sem(f"x_in{b}") for b in range(NB)]
        consts_in = sem("consts_in")
        w_in = sem("w_in")
        wpost_in = sem("wpost_in")
        set_zero = sem("set_zero")
        ident_ready = sem("ident_ready")
        fill_ready = sem("fill_ready")
        latent_set = sem("latent_set")
        w_high = sem("w_high")
        w_split = sem("w_split")
        wpost_split = sem("wpost_split")
        const_out = sem("const_out")
        slopes_ready = sem("slopes_ready")
        stats_done = sem("stats_done")
        aggr_done = sem("aggr_done")
        eps_done = sem("eps_done")
        rstd_done = sem("rstd_done")
        xn_done = sem("xn_done")
        product = sem("product")
        hi_done = sem("hi_done")
        bank_free = sem("bank_free")
        part_out = [sem(f"part_out{i}") for i in range(NSTAGE)]
        ops_in = [sem(f"ops_in{i}") for i in range(2)]
        first_in = [sem(f"first_in{i}") for i in range(2)]
        max_product = sem("max_product")
        max_free = sem("max_free")
        neg_done = sem("neg_done")
        neg_high = sem("neg_high")
        neg_in = sem("neg_in")
        qk_product = sem("qk_product")
        exp_done = sem("exp_done")
        pv_done = sem("pv_done")
        sums_out = sem("sums_out")
        inv_done = sem("inv_done")
        ctx_high = sem("ctx_high")
        bias_added = sem("bias_added")
        g_in = sem("g_in")
        g_split = sem("g_split")
        top_done = sem("top_done")
        route_step = sem("route_step")
        route_exp = sem("route_exp")
        rows_out = sem("rows_out")
        raw_in = [sem(f"raw_in{i}") for i in range(3)]
        wide_in = [sem(f"wide_in{i}") for i in range(2)]
        gu_high = sem("gu_high")
        gu_split = sem("gu_split")
        dn_high = sem("dn_high")
        dn_split = sem("dn_split")
        gu_product = sem("gu_product")
        silu_done = sem("silu_done")
        gated = sem("gated")
        weighted = sem("weighted")
        i_high = sem("i_high")
        i_split = sem("i_split")
        down_done = sem("down_done")
        moe_sums = sem("moe_sums")
        x_out = sem("x_out")

        STAGES = {("a", 0): [("T", 8), ("Q0", 4), ("K0", 4), ("V0", 4), ("Q1", 4), ("V1", 4), ("K1", 4),
                              ("core", 0)],
                  ("b", 1): [("T", 8), ("KM", 8), ("Q0", 4), ("KL", 4), ("VM", 8), ("K0", 4), ("VL", 4), ("Q1", 4),
                             ("V0", 4), ("V1", 4), ("K1", 4), ("core", 0)],
                  "f": [("T", 8), ("R", 4), ("RT", 4), ("W0", 2), ("W1", 2), ("F0", 4), ("F1", 4)]}
        WITH_HI = {"T", "Q0", "Q1", "K0", "K1", "VM", "VL", "KM", "KL"}
        first_unit, first_hi, norm_of, phases = {}, {}, {}, []
        u = hi = 0
        for i, kind in enumerate(parts):
            n = parts[:i].count("f") if kind == "f" else "ab".index(kind)
            phases.append((kind, n))
            norm_of[kind, n] = i
            for name, count in STAGES["f"] if kind == "f" else STAGES[kind, n]:
                first_unit[kind, n, name], first_hi[kind, n, name] = u, hi
                u += count
                hi += count * (name in WITH_HI)
        total_units = u
        order_of = {phase: DOWN if i and phases[i - 1][0] != "f" else UP for i, phase in enumerate(phases)}
        bias_of_col = {"q": 0, "k": 2, "v": 4, "upk": 6, "kl": 8, "vl": 9}

        def w_ready(layer, name):
            return sum(len(W_ORDER[i]) for i in range(layer)) + W_ORDER[layer].index(name) + 1

        def weight(part, name, k, cols):
            at = W_OFF[name] + k * W_COLS[name]
            return part[:, at + cols.start:at + cols.stop]

        e_of = {}
        n = 0
        for layer in range(2):
            for g, b in BLOCKS:
                for j in range(TPB * (b + 1)):
                    e_of[layer, g, b, j] = n
                    n += 1
        mu_of = {}
        for item in plan:
            if item[0] in ("max", "turn", "ctx", "turn_ctx", "project"):
                mu_of[item] = len(mu_of)
        MU = len(mu_of)

        def block_no(layer, g, b):
            return layer * G * NB + BLOCKS.index((g, b))

        FRESH_LOADS, LOADS = 9, 10
        SHARED = 2
        HU = 2 * (PAIRS + 1)

        def split_base(f, fb):
            return f * (1 + NFB * PAIRS) + 1 + fb * PAIRS

        W_BANK, F_BANK = (NBANK - 2, 2), 4

        def split_no(f, fb, pair):
            return split_base(f, fb) + pair + (fb > 0)

        def unit_base(f, fb):
            return (f * NFB + fb) * HU

        def turned(t, part, order=UP):
            return lambda i: t[:, part, i % KC, order[i // KC] * QB:(order[i // KC] + 1) * QB]

        def in_block(t, part):
            return lambda i: t[:, part, i // NB, (i % NB) * QB:(i % NB + 1) * QB]

        PROJECTIONS = [[name for name, _ in STAGES[phase] if name not in ("T", "core")]
                       for phase in (("a", 0), ("b", 1))]
        LAT_OF = {"VL": slice(0, DL), "KL": slice(DL, 2 * DL)}

        def in_lat(name, part):
            return lambda i: lat[LAT_OF[name], part, i * QB:(i + 1) * QB]

        def staged_no(layer, name, i):
            return (layer * 4 + STAGED.index(name)) * NB + i

        def staged(layer, name, tiles):
            return lambda i: tiles[staged_no(layer, name, i) % NSTAGE][:, :]

        def bias_col(name, half=0, rows=slice(0, P)):
            return lambda i: bias_cols[rows, bias_of_col[name] + half + i // NB:bias_of_col[name] + half + i // NB + 1]

        block = ctx.enter_context(nc.Block())

        def experts_dma(sp, f, last, store):
            sp.wait_ge(max_free, (f + 1) * MU)

            def load_raw(fb, q, k, first=False):
                if not first:
                    sp.wait_ge(dn_split, split_base(f, fb) + q - 1)
                sp.dma_start(e_raw[k][:, :], A["experts"][q]).then_inc(raw_in[k], 16)

            def load_wide(fb, q, k, value):
                if value is not None:
                    sp.wait_ge(weighted, value)
                rows = route_rows[f][bass.ds(2 * q, 2), fb * FB:(fb + 1) * FB]
                sp.dma_start(wide[k][:, :],
                             rows.rearrange("e (o c) -> e o c", o=1).broadcast_to([2, EI, FB])).then_inc(wide_in[k], 16)

            for fb in range(NFB):
                at = unit_base(f, fb)
                for k in range(2):
                    load_raw(fb, k, k, first=(f == 0 and fb == 0))
                if fb == 0:
                    sp.dma_start(e_raw[2][:, :], A["experts"][PAIRS]).then_inc(raw_in[2], 16)
                sp.wait_ge(bank_free, first_unit["f", f, f"W{fb}"] + 2)
                tokens = slice(fb * FB, (fb + 1) * FB)
                sp.dma_start(route_rows[f][:, tokens], route_rows_sb[:, tokens]).then_inc(rows_out, 16)
                sp.wait_ge(rows_out, 16 * (2 * f + fb + 1))
                for k in range(2):
                    load_wide(fb, k, k, at - 2 * k if at else None)
                if fb and last:
                    for i in range(FB // QB):
                        sp.wait_ge(bank_free, first_unit["f", f, "F0"] + 2 * (i + 1))
                        store(i)
                with sp.Fori(1, PAIRS // 2) as i:
                    for k in range(2):
                        load_raw(fb, 2 * i + k, k)
                        load_wide(fb, 2 * i + k, k, at + 4 * i + 2 * k - 2)
                load_wide(fb, PAIRS, 0, at + 2 * PAIRS - 2)

        @block.sync
        def _(sp):
            def block_of(a, b):
                return a[b * QB:(b + 1) * QB, :].rearrange("(t p) e -> p t e", p=P)

            def store(b):
                sp.dma_start(block_of(A["out"], b), x[:, b * TPB:(b + 1) * TPB, :]).then_inc(x_out, 16)

            for b in range(NB):
                sp.dma_start(x[:, b * TPB:(b + 1) * TPB, :], block_of(A["x"], b)).then_inc(x_in[b], 16)
                if b == 0:
                    sp.dma_start(w_raw[:, 0:NWA], A["w_a"]).then_inc(w_in, 16)
            sp.dma_start(bias_cols[:, :], A["bias_cols"]).then_inc(consts_in, 16)
            sp.dma_start(bias_rows[:, :, :], A["bias_rows"].rearrange("(a r) e -> a r e", a=1)
                         .broadcast_to([P, 3, E])).then_inc(consts_in, 16)
            sp.dma_start(slope_raw[:, :], A["slopes"]).then_inc(consts_in, 16)
            sp.dma_start(w_post_raw[:, :], A["w_a_post"]).then_inc(wpost_in, 16)
            sp.dma_start(g_raw[:, :], A["router"]).then_inc(g_in, 16)
            sp.wait_ge(fill_ready, 4)
            for c in range(2 * S // FILL):
                sp.dma_start(zero_rows[:, c * FILL:(c + 1) * FILL], fill[:, 0, :].bitcast(F32)).then_inc(const_out, 16)
            for row in range(2):
                sp.dma_start(one_rows[row, :].rearrange("(r c) -> r c", c=FILL),
                             fill[0:S // FILL, 1, :].bitcast(F32)).then_inc(const_out, 16)
            for part in range(2):
                for h in range(2):
                    for row in range(2):
                        sp.dma_start(max_rows[2 * part + row, h, :].rearrange("(r c) -> r c", c=FILL),
                                     fill[0:S // FILL, int(row == h), :].bitcast(F32)).then_inc(const_out, 16)
            sp.wait_ge(slopes_ready, 2)
            for i, part in enumerate((slope_hi, slope_lo)):
                sp.dma_start(slope_parts[i, :, :].rearrange("h (k c) -> h k c", k=P // H),
                             part[:, :].bitcast(F32)).then_inc(const_out, 16)

            def attention(kind, layer):
                if layer == 1:
                    sp.wait_ge(product, first_unit[kind, layer, "T"])
                    sp.dma_start(w_raw[:, :], A["w_b"]).then_inc(w_in, 16)
                    sp.dma_start(w_post_raw[:, :], A["w_b_post"]).then_inc(wpost_in, 16)
                def load_fresh(s):
                    for r in range(len(K_PARTS)):
                        for hh in range(2):
                            other = r * PAIR + (1 - hh) * D
                            sp.dma_start(Kp[s][other:other + D, hh, :, :].bitcast(F32), zero_rows[:, :]).then_inc(ops_in[s], 16)
                    sp.dma_start(Qp[s][ROW_BIAS:ROW_MAX, :, :].bitcast(F32),
                                 one_rows.rearrange("r (o s) -> r o s", o=1).broadcast_to([2, 2, S])).then_inc(ops_in[s], 16)
                    for p in range(2):
                        sp.dma_start(Kp[s][ROW_MAX:ROWS, :, p, :].bitcast(F32), max_rows[:, :, :]).then_inc(ops_in[s], 16)

                def load_group(g, cols, done):
                    s, features, n = g % 2, slice(GH * D * g, GH * D * (g + 1)), cols.stop - cols.start
                    for r, part in enumerate(Q_PARTS):
                        sp.dma_start(Qp[s][r * PAIR:(r + 1) * PAIR, :, cols].bitcast(F32),
                                     q_parts[part, features, cols].rearrange("(p f) s -> f p s", p=2)).then_inc(done, 16)
                    for r, part in enumerate(K_PARTS):
                        for hh in range(2):
                            own = r * PAIR + hh * D
                            sp.dma_start(Kp[s][own:own + D, hh, :, cols].bitcast(F32),
                                         k_parts[part, features, cols].rearrange("(p h d) s -> h d p s", p=2, h=2)[hh])\
                                .then_inc(done, 16)
                    if layer == 0:
                        bias = slope_parts[:, GH * g:GH * (g + 1), cols]
                    else:
                        bias = zero_rows[0:2, cols].rearrange("r (o s) -> r o s", o=1).broadcast_to([2, GH, n])
                    sp.dma_start(Kp[s][ROW_BIAS:ROW_MAX, :, :, cols].bitcast(F32).rearrange("r h p s -> r (h p) s"), bias)\
                        .then_inc(done, 16)

                for name in STAGED:
                    for i in range(NB):
                        n = staged_no(layer, name, i)
                        sp.wait_ge(bank_free, first_unit[kind, layer, name] + i + 1)
                        dst, m = q_parts if name[0] == "Q" else k_parts, int(name[1])
                        for a, part in enumerate((part_hi, part_lo)):
                            sp.dma_start(dst[a, m * P:(m + 1) * P, i * QB:(i + 1) * QB],
                                         part[n % NSTAGE][:, :].bitcast(F32)).then_inc(part_out[n % NSTAGE], 16)
                    if name in LOADS_AFTER:
                        what = LOADS_AFTER[name]
                        if what == "fresh":
                            sp.wait_ge(product, first_unit[kind, layer, "T"] + KC * NB if layer == 0 else
                                       first_unit[kind, layer, "VL"] + NB)
                            if layer == 0:
                                sp.wait_ge(const_out, 16 * (2 + 2 * S // FILL + 2 + 8))
                            load_fresh(0)
                        else:
                            for b in range(what * NB // 2, (what + 1) * NB // 2):
                                for first in ("Q0", "K0"):
                                    n = staged_no(layer, first, b)
                                    sp.wait_ge(part_out[n % NSTAGE], 32 * (n // NSTAGE + 1))
                            load_group(0, slice(what * S // 2, (what + 1) * S // 2), first_in[what])

                sp.wait_ge(product, first_unit[kind, layer, "core"])
                sp.wait_ge(bank_free, first_unit[kind, layer, "core"])
                for n in range(staged_no(layer, "K1", NB), staged_no(layer, "K1", NB) - NSTAGE, -1):
                    sp.wait_ge(part_out[(n - 1) % NSTAGE], 32 * ((n - 1) // NSTAGE + 1))
                for g, b in BLOCKS:
                    n = block_no(layer, g, b)
                    s = g % 2
                    sp.wait_ge(max_free, layer * MU + mu_of["turn", g, b] + 1)
                    for p in range(2):
                        for r, rows in ((ROW_MAX, neg_hi), (ROW_MAX + 2, neg_lo)):
                            sp.dma_start(Qp[s][r:r + 2, p, b * QB:(b + 1) * QB].bitcast(F32),
                                         rows[8 * p:8 * p + 8, n % 2, :].bitcast(F32)).then_inc(neg_in, 16)
                    sp.wait_ge(neg_in, 64 * (n + 1))
                    if (g, b) == (0, 1):
                        load_fresh(1)
                        load_group(1, slice(0, S), ops_in[1])
                    if b == NB - 2 and 1 <= g < G - 1:
                        sp.wait_ge(qk_product, 2 * (e_of[layer, g - 1, NB - 1, T - 1] + 1))
                        load_group(g + 1, slice(0, S), ops_in[s ^ 1])

            for kind, n in phases:
                if kind != "f":
                    attention(kind, n)
                else:
                    experts_dma(sp, n, (kind, n) == phases[-1], store)
            done = FB // QB if phases[-1][0] == "f" else 0
            sp.wait_ge(max_free, MU * sum(kind != "f" for kind, _ in phases))
            for b in range(done, NB):
                sp.wait_ge(bank_free, total_units - 2 * (NB - 1 - b) if done else total_units)
                store(b)
            sp.wait_ge(x_out, 16 * NB)

        def inverse_std(pool, n, place):
            if n < len(phases):
                b = order_of[phases[n]][place]
                tiles = slice(b * TPB, (b + 1) * TPB)
                pool.wait_ge(aggr_done, n * T + (place + 1) * TPB)
                pool.tensor_scalar(var_eps[:, tiles], mean_var[:, tiles, 1], EPS, None, ALU.add).then_inc(eps_done, 1)
                pool.wait_ge(eps_done, n * NB + place + 1)
                pool.tensor_tensor(rstd[:, tiles], var_eps[:, tiles], minus_half[:, :].broadcast_to([P, TPB]), ALU.pow)\
                    .then_inc(rstd_done, 1)

        def experts_pool(pool, f):
            def split(k, cols, high, low, value):
                pool.tensor_tensor(e_hi[k][:, cols], e_raw[k][:, cols], ones[:, :].broadcast_to([P, cols.stop - cols.start]),
                                   ALU.mult).then_inc(high, 1)
                pool.wait_ge(high, value)
                pool.tensor_tensor(e_lo[k][:, cols], e_raw[k][:, cols], e_hi[k][:, cols].bitcast(F32), ALU.subtract)\
                    .then_inc(low, 1)

            GU, DN = slice(0, EW - E), slice(EW - E, EW)
            for fb in range(NFB):
                at, sb = unit_base(f, fb), split_base(f, fb)
                loads = (f * NFB + fb) * PAIRS // 2

                def pair(i, k, used, sb=sb):
                    pool.wait_ge(raw_in[k], 16 * (loads + 1 + i))
                    if used is not None:
                        pool.wait_ge(gu_product, used)
                    split(k, GU, gu_high, gu_split, sb + 2 * i + k + 1)
                    if used is not None:
                        pool.wait_ge(down_done, used)
                    split(k, DN, dn_high, dn_split, sb + 2 * i + k + 1)

                for k in range(2):
                    pair(0, k, at - 4 + 2 * k if at else None, split_no(f, fb, k) - k - 1)
                if fb == 0:
                    pool.wait_ge(raw_in[2], 16 * (f + 1))
                    split(2, GU, gu_high, gu_split, sb + 2)
                    split(2, DN, dn_high, dn_split, sb + 2)
                if fb == 1:
                    for b in range(FB // QB):
                        inverse_std(pool, norm_of["f", f] + 1, b)
                with pool.Fori(1, PAIRS // 2) as i:
                    for k in range(2):
                        pair(i, k, at + 4 * i + 2 * k - 2)
            for b in range(FB // QB, NB):
                inverse_std(pool, norm_of["f", f] + 1, b)

        @block.gpsimd
        def _(pool):
            pool.memset(ident[:, :], 0.0).then_inc(set_zero, 1)
            pool.memset(diag_mask[:, :], 0.0).then_inc(set_zero, 1)
            pool.memset(cut16[:, :], 0.0).then_inc(set_zero, 1)
            pool.wait_ge(set_zero, 3)
            pool.affine_select(out=ident[:, :], in_=ident[:, :], compare_op=ALU.not_equal, fill=1.0, base=0,
                               pattern=[[-1, P]], channel_multiplier=1).then_inc(ident_ready, 1)
            pool.affine_select(out=diag_mask[:, QB - P:QB], in_=diag_mask[:, QB - P:QB], compare_op=ALU.is_ge,
                               fill=NEG, base=0, pattern=[[-1, P]], channel_multiplier=1).then_inc(ident_ready, 1)
            pool.affine_select(out=cut16[:, :], in_=cut16[:, :], compare_op=ALU.is_ge, fill=NEG, base=0,
                               pattern=[[1, P]], channel_multiplier=-1).then_inc(ident_ready, 1)
            pool.wait_ge(ident_ready, 1)
            pool.tensor_copy(ident16[:, :], ident[:, :]).then_inc(ident_ready, 1)
            pool.memset(ones[:, :], 1.0).then_inc(fill_ready, 1)
            pool.memset(minus_half[:, :], -0.5).then_inc(fill_ready, 1)
            pool.memset(fill[:, 0, :].bitcast(F32), 0.0).then_inc(fill_ready, 1)
            pool.memset(fill[:, 1, :].bitcast(F32), 1.0).then_inc(fill_ready, 1)

            def attention(kind, layer):
                pool.wait_ge(fill_ready, 2)
                for b in range(2 if norm_of[kind, layer] == 0 else 0):
                    inverse_std(pool, 0, b)
                pool.wait_ge(w_in, 16 * (layer + 1))
                for name in W_ORDER[layer]:
                    cols = slice(W_OFF[name], W_OFF[name] + W_CHUNKS[name] * W_COLS[name])
                    pool.tensor_tensor(w_hi[:, cols], w_raw[:, cols], ones[:, :].broadcast_to([P, cols.stop - cols.start]),
                                       ALU.mult).then_inc(w_high, 1)
                    pool.wait_ge(w_high, w_ready(layer, name))
                    pool.tensor_tensor(w_lo[:, cols], w_raw[:, cols], w_hi[:, cols].bitcast(F32), ALU.subtract)\
                        .then_inc(w_split, 1)
                    if name == "kl":
                        pool.memset(lat[0:DL, :, :].bitcast(F32), 0.0).then_inc(latent_set, 1)
                    if norm_of[kind, layer] == 0 and name == W_ORDER[layer][0]:
                        for b in range(2, NB):
                            inverse_std(pool, 0, b)
                if layer == 0:
                    pool.memset(values[:, :, :, D:2 * D], 0.0).then_inc(set_zero, 1)
                    pool.wait_ge(set_zero, 4)
                    pool.memset(values[:, :, :, D:D + 1], 1.0).then_inc(ident_ready, 1)
                if layer == 0:
                    pool.wait_ge(g_in, 16)
                    pool.tensor_copy(g_hi[:, :], g_raw[:, :]).then_inc(g_split, 1)
                    pool.wait_ge(g_split, 1)
                    pool.tensor_tensor(g_lo[:, :], g_raw[:, :], g_hi[:, :].bitcast(F32), ALU.subtract).then_inc(g_split, 1)
                pool.wait_ge(wpost_in, 16 * (layer + 1))
                wp = w_post_raw[:, :].rearrange("p (k e) -> p k e", k=KC)
                pool.tensor_copy(w_post[:, 0, :, :], wp).then_inc(wpost_split, 1)
                pool.wait_ge(wpost_split, 2 * layer + 1)
                pool.tensor_tensor(w_post[:, 1, :, :], wp, w_post[:, 0, :, :].bitcast(F32), ALU.subtract)\
                    .then_inc(wpost_split, 1)
                pool.wait_ge(consts_in, 48)
                pool.wait_ge(xn_done, T * (norm_of[kind, layer] + 1))
                pool.tensor_tensor(x[:, :, :], x[:, :, :], bias_rows[:, layer:layer + 1, :].broadcast_to([P, T, E]),
                                   ALU.add).then_inc(bias_added, 1)
                for b in range(NB):
                    inverse_std(pool, norm_of[kind, layer] + 1, b)

            for kind, n in phases:
                if kind != "f":
                    attention(kind, n)
                else:
                    experts_pool(pool, n)

        def experts_act(act, f, high_parts):
            phase = ("f", f)
            high_parts(phase, "T", KC * NB, turned(xT, 0, order_of[phase]))

            def route_exps(half):
                tiles = slice(half * RT, (half + 1) * RT)
                act.wait_ge(route_step, ROUTE_STEPS * (2 * f + half) + 2)
                act.activation(route[:, tiles, :], route[:, tiles, :], ACT.Exp).then_inc(route_exp, 1)

            route_exps(0)
            for fb in range(NFB):
                at = unit_base(f, fb)

                def unit(v, s, first=False, rows=slice(0, P)):
                    act.wait_ge(gu_product, at + v + 1)
                    if not first:
                        act.wait_ge(gated, at + v - 1)
                    act.activation(silu[s][rows, :], BANK[2 * s][rows, :], ACT.Silu).then_inc(silu_done, 1)
                    act.wait_ge(weighted, at + v + 1)
                    if not first:
                        act.wait_ge(down_done, at + v - 1)
                    act.activation(i_hi[s][rows, :], inter[s][rows, :], ACT.Copy).then_inc(i_high, 1)

                for v in range(4):
                    unit(v, v % 2, first=(at == 0 and v < 2))
                    if fb == 0 and v == 1:
                        route_exps(1)
                with act.Fori(1, PAIRS // 2) as i:
                    for r in range(4):
                        unit(4 * i + r, r % 2)
                for v in range(2 * PAIRS, HU):
                    unit(v, v % 2, rows=slice(0, EI))
                act.wait_ge(down_done, at + HU)
                if fb:
                    act.wait_ge(product, first_unit["f", f, "F0"] + 4)
                for n in range(2 * KC):
                    act.activation(moe_out[:, n // 2, (n % 2) * QB:(n % 2 + 1) * QB], BANK[4 + n], ACT.Copy)\
                        .then_inc(moe_sums, 1)

        @block.scalar
        def _(act):
            def high_parts(phase, name, count, dst, bias=None, rows=slice(0, P)):
                for i in range(count):
                    u = first_unit[(*phase, name)] + i
                    act.wait_ge(product, u + 1)
                    if phase[0] != "f" and name in STAGED:
                        n = staged_no(phase[1], name, i)
                        if n >= NSTAGE:
                            act.wait_ge(part_out[n % NSTAGE], 32 * (n // NSTAGE))
                    bank = BANK[u % NBANK][rows, :]
                    if bias is None:
                        act.activation(dst(i), bank, ACT.Copy).then_inc(hi_done, 1)
                    else:
                        act.activation(dst(i), bank, ACT.Identity, bias=bias(i)).then_inc(hi_done, 1)

            def attention(kind, layer):
                phase = (kind, layer)
                high_parts(phase, "T", KC * NB, turned(xT, 0, order_of[phase]))
                if layer == 0:
                    act.wait_ge(consts_in, 48)
                    act.activation(slope_hi[:, :], slope_raw[:, :], ACT.Copy).then_inc(slopes_ready, 1)
                for name in PROJECTIONS[layer]:
                    if name in STAGED:
                        bias = None if layer == 0 else bias_col("q" if name[0] == "Q" else "upk", int(name[1]))
                        high_parts(phase, name, NB, staged(layer, name, part_hi), bias)
                    elif name in ("V0", "V1"):
                        pass
                    elif name in ("VM", "KM"):
                        high_parts(phase, name, 2 * NB, in_block(mid, 0), bias_col(name[0].lower()))
                    else:
                        rows = LAT_OF[name]
                        high_parts(phase, name, NB, in_lat(name, 0), bias_col(name[0].lower() + "l", 0, rows), rows)
                act.wait_ge(product, first_unit[kind, layer, "core"])
                act.wait_ge(bank_free, first_unit[kind, layer, "core"])
                for item in plan:
                    if item[0] == "qk":
                        _, g, b, j, p, _ = item
                        e = e_of[layer, g, b, j]
                        off = P * max(0, j - TPB * b)
                        act.wait_ge(qk_product, 2 * e + p + 1)
                        if e >= NP:
                            act.wait_ge(pv_done, e - NP + 1)
                        act.activation(probs[:, e % NP, 2 * p:2 * p + 2, off:QB], exp_banks[p][:, :, off:QB],
                                       ACT.Exp, scale=D ** -0.5).then_inc(exp_done, 1)
                    elif item[0] == "out":
                        _, g, b = item
                        n = block_no(layer, g, b)
                        act.wait_ge(pv_done, e_of[layer, g, b, TPB * (b + 1) - 1] + 1)
                        if n % (G * NB) >= 2:
                            before = BLOCKS[BLOCKS.index((g, b)) - 2]
                            act.wait_ge(max_product, layer * MU + mu_of["ctx", before[0], before[1]] + 1)
                        act.activation(sums[:, n % 2, :], pv_banks[n % NPV][:, :], ACT.Copy).then_inc(sums_out, 1)
                    elif item[0] == "turn_ctx":
                        mu = layer * MU + mu_of[item]
                        act.wait_ge(max_product, mu + 1)
                        act.activation(turned(contextT, 0)(item[1] * KC + item[2]), max_banks[mu % NMAX][:, :], ACT.Copy)\
                            .then_inc(ctx_high, 1)

            for kind, n in phases:
                if kind != "f":
                    attention(kind, n)
                else:
                    experts_act(act, n, high_parts)

        def experts_pe(pe, f, turn, bank_of, three_passes):
            phase = ("f", f)
            turn(phase)
            pe.wait_ge(g_split, 2)
            for i in range(NB):
                bank = bank_of(first_unit["f", f, "R"] + i)
                pe.wait_ge(bank_free, first_unit["f", f, "T"] + KC * (order_of[phase].index(i) + 1))
                three_passes(bank[0:GC, :], lambda a, k: (g_hi, g_lo)[a][:, k * GC:(k + 1) * GC],
                             lambda c, k: xT[:, c, k, i * QB:(i + 1) * QB], KC).then_inc(product, 1)
            for i in range(NB):
                bank = bank_of(first_unit["f", f, "RT"] + i)
                pe.wait_ge(bank_free, first_unit["f", f, "R"] + i + 1)
                for t in range(TPB):
                    last = pe.transpose(bank[:, t * P:t * P + GC], route_rows_sb[:, (i * TPB + t) * P:(i * TPB + t + 1) * P],
                                        ident[0:GC, 0:GC])
                last.then_inc(product, 1)

            def turn_routes(half):
                if half == 0:
                    pe.wait_ge(bank_free, first_unit["f", f, "W0"])
                pe.wait_ge(route_step, ROUTE_STEPS * (2 * f + half + 1))
                for i in range(NB // 2):
                    bank = BANK[W_BANK[half] + i]
                    for t in range(TPB):
                        last = pe.transpose(bank[0:GC, t * P:(t + 1) * P], route[:, half * RT + i * TPB + t, :], ident[:, :])
                    last.then_inc(product, 1)

            def gate_up(fb, v, k, s, new_pair, split_value, first=False):
                if new_pair:
                    pe.wait_ge(gu_split, split_value)
                if not first:
                    pe.wait_ge(gated, unit_base(f, fb) + v - 1)
                tokens = slice(fb * FB + s * QB, fb * FB + (s + 1) * QB)
                for n in range(1 if k == SHARED else 2):
                    last = three_passes(BANK[2 * s + n],
                                        lambda a, c: (e_hi, e_lo)[a][k][:, (2 * c + n) * P:(2 * c + n + 1) * P],
                                        lambda a, c: xT[:, a, c, tokens], KC)
                last.then_inc(gu_product, 1)

            pe.wait_ge(bank_free, first_unit["f", f, "W0"])
            for v in range(2):
                gate_up(0, v, 0, v, v == 0, split_no(f, 0, 0), first=True)
            turn_routes(0)
            for fb in range(NFB):
                at, sb = unit_base(f, fb), split_base(f, fb)

                def down(v, k, s, new_pair, split_value, start=False, stop=False):
                    if new_pair:
                        pe.wait_ge(dn_split, split_value)
                    pe.wait_ge(i_split, at + v + 1)
                    for m in range(KC):
                        cols = slice(EW - E + m * P, EW - E + (m + 1) * P)
                        last = three_passes(BANK[4 + 2 * m + s], lambda a, c: (e_hi, e_lo)[a][k][:, cols],
                                            lambda a, c: (i_hi, i_lo)[a][s][:, :], 1, start, stop)
                    last.then_inc(down_done, 1)

                def four(i, first=False, last=False):
                    for r in range(4):
                        k, pair = (1, 2 * i + 1) if r < 2 else (0, 2 * i + 2)
                        if last and r >= 2:
                            gate_up(fb, 4 * i + r + 2, SHARED, r % 2, False, None)
                        else:
                            gate_up(fb, 4 * i + r + 2, k, r % 2, r % 2 == 0,
                                    split_no(f, fb, 1) if first and r < 2 else sb + pair + 1)
                        down(4 * i + r, r // 2, r % 2, r % 2 == 0,
                             split_no(f, fb, r // 2) if first else sb + 2 * i + r // 2 + 1, start=first and r < 2)

                four(0, first=True)
                with pe.Fori(1, PAIRS // 2 - 1) as i:
                    four(i)
                four(PAIRS // 2 - 1, last=True)
                for v in range(2 * PAIRS, HU):
                    down(v, SHARED, v % 2, False, None, stop=True)
                if fb == 0:
                    turn_routes(1)
                    for v in range(2):
                        if v == 1:
                            pe.wait_ge(bank_free, first_unit["f", f, "W1"] + 2)
                        gate_up(1, v, 0, v, v == 0, split_no(f, 1, 0))
                pe.wait_ge(moe_sums, 4 * (f * NFB + fb + 1))
                for i in range(FB // P // 2):
                    bank = BANK[F_BANK + i]
                    for n in range(2 * KC):
                        t, m = 2 * i + n // 2, n % 2
                        last = pe.transpose(bank[:, n * P:(n + 1) * P], moe_out[:, m, t * P:(t + 1) * P], ident[:, :])
                    last.then_inc(product, 1)
            pe.wait_ge(bank_free, first_unit["f", f, "F1"] + 4)

        @block.tensor
        def _(pe):
            def bank_of(u):
                if u >= NBANK:
                    pe.wait_ge(bank_free, u - NBANK + 1)
                return BANK[u % NBANK]

            def three_passes(out, stationary, moving, chunks, start=True, stop=True):
                order = [(k, a, c) for k in range(chunks) for a, c in ((0, 0), (0, 1), (1, 0))]
                for n, (k, a, c) in enumerate(order):
                    last = pe.matmul(out, stationary(a, k), moving(c, k), start=start and n == 0,
                                     stop=stop and n == len(order) - 1, skip_group_check=not (start and stop))
                return last

            def turn(phase):
                for i in range(KC * NB):
                    b, k = order_of[phase][i // KC], i % KC
                    pe.wait_ge(xn_done, T * norm_of[phase] + (i // KC + 1) * TPB)
                    bank = bank_of(first_unit[(*phase, "T")] + i)
                    for t in range(TPB):
                        last = pe.transpose(bank[:, t * P:(t + 1) * P], xn[:, b * TPB + t, k * P:(k + 1) * P], ident[:, :])
                    last.then_inc(product, 1)

            def features(phase, name, w, src, halves, chunks=KC, first=False):
                pe.wait_ge(w_split, w_ready(phase[1], w))
                for i in range(len(halves) * NB):
                    m, b = halves[i // NB], i % NB
                    bank = bank_of(first_unit[(*phase, name)] + i)
                    if first and i < NB:
                        pe.wait_ge(bank_free, first_unit[(*phase, "T")] + KC * (order_of[phase].index(b) + 1))
                    three_passes(bank, lambda a, k: weight((w_hi, w_lo)[a], w, k, slice(m * P, (m + 1) * P)),
                                 lambda c, k: src(c, k, slice(b * QB, (b + 1) * QB)), chunks).then_inc(product, 1)

            def latent(phase, name, w, since):
                pe.wait_ge(w_split, w_ready(phase[1], w))
                pe.wait_ge(bank_free, first_unit[(*phase, since)] + 2 * NB)
                for b in range(NB):
                    bank = bank_of(first_unit[(*phase, name)] + b)
                    three_passes(bank[0:W_COLS[w], :], lambda a, k: weight((w_hi, w_lo)[a], w, k, slice(0, W_COLS[w])),
                                 lambda c, k: mid[:, c, k, b * QB:(b + 1) * QB], KC).then_inc(product, 1)

            def token_pair(bank, pair, stationary, moving, chunks):
                for t in range(2):
                    last = three_passes(bank[:, t * E:(t + 1) * E], lambda a, k: stationary(a, k, 2 * pair + t),
                                        moving, chunks)
                return last

            def tokens_out(phase, name, stationary, moving, chunks, pairs):
                for i, pair in enumerate(pairs):
                    token_pair(bank_of(first_unit[(*phase, name)] + i), pair, stationary, moving, chunks).then_inc(product, 1)

            def from_xT(c, k, cols):
                return xT[:, c, k, cols]

            def max_bank(n):
                if n >= NMAX:
                    pe.wait_ge(max_free, n - NMAX + 1)
                return max_banks[n % NMAX]

            def attention(kind, layer):
                phase = (kind, layer)
                turn(phase)
                for name in PROJECTIONS[layer]:
                    if name in ("VM", "KM"):
                        features(phase, name, name[0].lower(), from_xT, (0, 1), first=name == "KM")
                    elif name in ("VL", "KL"):
                        latent(phase, name, name[0].lower() + "l", name[0] + "M")
                    elif name in ("V0", "V1"):
                        pairs = range(int(name[1]) * NB, (int(name[1]) + 1) * NB)
                        pe.wait_ge(w_split, w_ready(layer, "v" if layer == 0 else "upv"))
                        if layer == 0:
                            tokens_out(phase, name, lambda a, k, t: xT[:, a, k, t * P:(t + 1) * P],
                                       lambda c, k: weight((w_hi, w_lo)[c], "v", k, slice(0, E)), KC, pairs)
                        else:
                            pe.wait_ge(bank_free, first_unit[kind, layer, "VL"] + NB)
                            tokens_out(phase, name, lambda a, k, t: lat[:, a, t * P:(t + 1) * P],
                                       lambda c, k: weight((w_hi, w_lo)[c], "upv", 0, slice(0, E)), 1, pairs)
                    elif layer == 1 and name[0] == "K":
                        pe.wait_ge(bank_free, first_unit[kind, layer, "KL"] + NB)
                        pe.wait_ge(latent_set, 1)
                        if name == "K1":
                            pe.wait_ge(bank_free, first_unit[kind, layer, "VL"] + NB)
                        features(phase, name, "upk", lambda c, k, cols: lat[:, c, cols], (int(name[1]),), 1)
                    else:
                        features(phase, name, name[0].lower(), from_xT, (int(name[1]),), first=layer == 0 and name == "Q0")
                pe.wait_ge(bank_free, first_unit[kind, layer, "core"])
                pe.wait_ge(ident_ready, 5)
                begun = set()
                per_layer = (FRESH_LOADS + LOADS, FRESH_LOADS + 2 * LOADS)
                for item in plan:
                    if item[0] == "max":
                        _, g, h, t, c = item
                        s, p, hh = g % 2, h // 2, h % 2
                        if g not in begun:
                            begun.add(g)
                            count = FRESH_LOADS + LOADS * (g // 2 + s)
                            pe.wait_ge(ops_in[s], 16 * (layer * per_layer[s] + count))
                        half = t // (T // 2)
                        if g == 0 and (g, half) not in begun:
                            begun.add((g, half))
                            pe.wait_ge(first_in[half], 16 * LOADS * (layer + 1))
                        n = min(QB, P * (t + 1) - QB * c)
                        bank = max_bank(layer * MU + mu_of[item])
                        pe.matmul(bank[:, 0:n], Qp[s][0:ROW_MAX, p, t * P:(t + 1) * P],
                                  Kp[s][0:ROW_MAX, hh, p, c * QB:c * QB + n], start=True, stop=True)\
                            .then_inc(max_product, 1)
                    elif item[0] == "turn":
                        _, g, b = item
                        n = block_no(layer, g, b)
                        bank = max_bank(layer * MU + mu_of[item])
                        pe.wait_ge(neg_done, n + 1)
                        pe.transpose(bank[0:GH * TPB, 0:P], neg_max[:, n % 2, :, :].rearrange("p h t -> p (h t)"),
                                     ident[:, :]).then_inc(max_product, 1)
                    elif item[0] == "qk":
                        _, g, b, j, p, _ = item
                        e = e_of[layer, g, b, j]
                        s = g % 2
                        off = P * max(0, j - TPB * b)
                        if j == 0 and p == 0:
                            pe.wait_ge(neg_in, 64 * (block_no(layer, g, b) + 1))
                        if e >= 1:
                            pe.wait_ge(exp_done, 2 * (e - 1) + p + 1)
                        for hh in range(2):
                            last = pe.matmul(exp_banks[p][:, hh, off:QB], Kp[s][0:ROWS, hh, p, j * P:(j + 1) * P],
                                             Qp[s][0:ROWS, p, b * QB + off:(b + 1) * QB], start=True,
                                             stop=j < TPB * b)
                            if j >= TPB * b:
                                last = pe.matmul(exp_banks[p][:, hh, off:off + P], ident16[:, :], cut16[:, :],
                                                 start=False, stop=True)
                        last.then_inc(qk_product, 1)
                    elif item[0] == "pv":
                        _, g, b, j, _ = item
                        e = e_of[layer, g, b, j]
                        off = P * max(0, j - TPB * b)
                        n = block_no(layer, g, b)
                        if j == 0 and n >= NPV:
                            pe.wait_ge(sums_out, n - NPV + 1)
                        pe.wait_ge(exp_done, 2 * (e + 1))
                        for h in range(GH):
                            last = pe.matmul(pv_banks[n % NPV][32 * h:32 * h + 32, off:QB],
                                             values[:, j, GH * g + h, :], probs[:, e % NP, h, off:QB],
                                             start=(j == 0), stop=(j == TPB * (b + 1) - 1))
                        last.then_inc(pv_done, 1)
                    elif item[0] == "ctx":
                        _, g, b = item
                        n = block_no(layer, g, b)
                        bank = max_bank(layer * MU + mu_of[item])
                        pe.wait_ge(sums_out, n + 1)
                        for t in range(TPB):
                            last = pe.transpose(bank[:, t * P:(t + 1) * P], sums[:, n % 2, t * P:(t + 1) * P], ident[:, :])
                        last.then_inc(max_product, 1)
                    elif item[0] == "turn_ctx":
                        _, b, k = item
                        bank = max_bank(layer * MU + mu_of[item])
                        pe.wait_ge(max_free, layer * MU + mu_of["ctx", G - 1, b] + 1)
                        for t in range(TPB):
                            last = pe.transpose(bank[:, t * P:(t + 1) * P], context[:, b * TPB + t, k * P:(k + 1) * P],
                                                ident[:, :])
                        last.then_inc(max_product, 1)
                    elif item[0] == "project":
                        i = item[1]
                        bank = max_bank(layer * MU + mu_of[item])
                        pe.wait_ge(max_free, layer * MU + mu_of["turn_ctx", 2 * i // TPB, KC - 1] + 1)
                        pe.wait_ge(wpost_split, 2 * (layer + 1))
                        token_pair(bank, i, lambda a, k, t: contextT[:, a, k, t * P:(t + 1) * P],
                                   lambda c, k: w_post[:, c, k, :], KC).then_inc(max_product, 1)
                pe.wait_ge(max_free, (layer + 1) * MU)

            pe.wait_ge(ident_ready, 1)
            for kind, n in phases:
                if kind != "f":
                    attention(kind, n)
                else:
                    experts_pe(pe, n, turn, bank_of, three_passes)

        def experts_dve(dve, f, statistics, normalise, low_parts):
            phase = ("f", f)
            low_parts(phase, "T", KC * NB, turned(xT, 0, order_of[phase]), turned(xT, 1, order_of[phase]))
            for i in range(NB):
                u = first_unit["f", f, "R"] + i
                dve.wait_ge(product, u + 1)
                dve.tensor_copy(route_rows_sb[:, i * QB:(i + 1) * QB], BANK[u % NBANK][0:GC, :]).then_inc(bank_free, 1)
            for i in range(NB):
                u = first_unit["f", f, "RT"] + i
                dve.wait_ge(product, u + 1)
                dve.tensor_copy(logits[:, i * TPB:(i + 1) * TPB, :],
                                BANK[u % NBANK].rearrange("p (t c) -> p t c", t=TPB)[:, :, 0:GC]).then_inc(bank_free, 1)
            dve.wait_ge(bank_free, first_unit["f", f, "RT"] + NB)

            def routing_parts(half):
                tiles = slice(half * RT, (half + 1) * RT)
                return (tiles, ROUTE_STEPS * (2 * f + half), logits[:, tiles, 0:NEXP], route[:, tiles, 0:NEXP],
                        chosen[:, tiles, :])

            def top_experts(half):
                tiles, step, logit, weight, picked = routing_parts(half)
                for t in range(tiles.start, tiles.stop):
                    dve.max(top[:, t, :], logits[:, t, 0:NEXP]).then_inc(top_done, 1)
                dve.wait_ge(top_done, RT * (2 * f + half + 1))
                dve.tensor_tensor(weight, logit, top[:, tiles, 0:1].broadcast_to([P, RT, NEXP]), ALU.subtract)\
                    .then_inc(route_step, 1)
                dve.tensor_scalar(route[:, tiles, NEXP:GC], logits[:, tiles, NEXP:GC], -1.0, None, ALU.mult)\
                    .then_inc(route_step, 1)
                for t in range(tiles.start, tiles.stop):
                    dve.match_replace(out=chosen[:, t, :], in_to_replace=top[:, t, :], in_values=logits[:, t, 0:NEXP],
                                      imm_value=VLOW).then_inc(route_step, 1)

            def routing(half):
                tiles, step, logit, weight, picked = routing_parts(half)
                dve.wait_ge(route_step, step + 2 + RT)
                dve.tensor_tensor(picked, picked, logit, ALU.not_equal).then_inc(route_step, 1)
                dve.wait_ge(route_exp, 2 * f + half + 1)
                dve.wait_ge(route_step, step + 3 + RT)
                dve.tensor_tensor(weight, weight, picked, ALU.mult).then_inc(route_step, 1)
                dve.wait_ge(route_step, step + 4 + RT)
                dve.tensor_reduce(route_sum[:, tiles], weight, AX.X, ALU.add).then_inc(route_step, 1)
                dve.wait_ge(route_step, step + 5 + RT)
                dve.reciprocal(route_inv[:, tiles], route_sum[:, tiles]).then_inc(route_step, 1)
                gate = route[:, tiles, NEXP:NEXP + 1]
                dve.tensor_scalar(gate, gate, 1.0, None, ALU.add).then_inc(route_step, 1)
                dve.wait_ge(route_step, step + 7 + RT)
                inv = route_inv[:, tiles].rearrange("p (t o) -> p t o", o=1).broadcast_to([P, RT, NEXP])
                dve.tensor_tensor(weight, weight, inv, ALU.mult).then_inc(route_step, 1)
                dve.reciprocal(gate, gate).then_inc(route_step, 1)
                dve.memset(route[:, tiles, NEXP + 1:GC], 0.0).then_inc(route_step, 1)

            def rows_out_of_psum(half):
                for i in range(NB // 2):
                    u = first_unit["f", f, f"W{half}"] + i
                    dve.wait_ge(product, u + 1)
                    cols = slice(half * FB + i * QB, half * FB + (i + 1) * QB)
                    dve.tensor_copy(route_rows_sb[:, cols], BANK[W_BANK[half] + i][0:GC, :]).then_inc(bank_free, 1)

            top_experts(0)
            routing(0)
            rows_out_of_psum(0)
            for fb in range(NFB):
                at = unit_base(f, fb)
                loads = [(f * NFB + fb) * (PAIRS // 2 + 1), (f * NFB + fb) * PAIRS // 2]

                def unit(v, s, k, load, first=False, shared=False):
                    rows = slice(0, EI) if shared else slice(0, P)
                    up = BANK[2 * s][EI:P, :] if shared else BANK[2 * s + 1]
                    dve.wait_ge(silu_done, at + v + 1)
                    if not first:
                        dve.wait_ge(i_split, at + v - 1)
                    dve.tensor_tensor(inter[s][rows, :], up, silu[s][rows, :], ALU.mult).then_inc(gated, 1)
                    if s == 0:
                        dve.wait_ge(wide_in[k], 16 * load)
                    dve.wait_ge(gated, at + v + 1)
                    dve.tensor_tensor(inter[s][rows, :], inter[s][rows, :], wide[k][rows, s * QB:(s + 1) * QB], ALU.mult)\
                        .then_inc(weighted, 1)
                    dve.wait_ge(i_high, at + v + 1)
                    if not first:
                        dve.wait_ge(down_done, at + v - 1)
                    dve.tensor_tensor(i_lo[s][rows, :], inter[s][rows, :], i_hi[s][rows, :].bitcast(F32), ALU.subtract)\
                        .then_inc(i_split, 1)

                for v in range(4):
                    unit(v, v % 2, v // 2, loads[v // 2] + 1, first=(at == 0 and v < 2))
                    if fb == 0 and v == 1:
                        top_experts(1)
                    elif fb == 0 and v == 3:
                        routing(1)
                    elif fb == 1 and v % 2:
                        normalise(phase, v // 2)
                with dve.Fori(1, PAIRS // 2) as i:
                    for r in range(4):
                        unit(4 * i + r, r % 2, r // 2, loads[r // 2] + 1 + i)
                for v in range(2 * PAIRS, HU):
                    unit(v, v % 2, 0, loads[0] + PAIRS // 2 + 1, shared=True)
                if fb == 0:
                    rows_out_of_psum(1)
                for i in range(FB // P // 2):
                    u = first_unit["f", f, f"F{fb}"] + i
                    dve.wait_ge(product, u + 1)
                    t = fb * FB // P + 2 * i
                    dve.tensor_tensor(x[:, t:t + 2, :], BANK[F_BANK + i].rearrange("p (t e) -> p t e", t=2),
                                      x[:, t:t + 2, :], ALU.add).then_inc(bank_free, 1)
                for b in range(fb * FB // QB, (fb + 1) * FB // QB):
                    dve.wait_ge(bank_free, first_unit["f", f, f"F{fb}"] + 2 * (b - fb * FB // QB) + 2)
                    statistics(phase, b)
                    if fb == 1:
                        normalise(phase, b)

        @block.vector
        def _(dve):
            def statistics(phase, b):
                n = norm_of.get(phase, -1) + 1
                if n < len(phases):
                    place = order_of[phases[n]].index(b)
                    for t in range(b * TPB, (b + 1) * TPB):
                        dve.bn_stats(stats[:, t, :], x[:, t, :]).then_inc(stats_done, 1)
                    for i in range(TPB):
                        dve.wait_ge(stats_done, n * T + place * TPB + i + 1)
                        dve.bn_aggr(mean_var[:, b * TPB + i, :], stats[:, b * TPB + i, :]).then_inc(aggr_done, 1)

            def normalise(phase, b):
                n = norm_of.get(phase, -1) + 1
                if n < len(phases):
                    dve.wait_ge(rstd_done, n * NB + order_of[phases[n]].index(b) + 1)
                    for t in range(b * TPB, (b + 1) * TPB):
                        dve.tensor_scalar(xn[:, t, :], x[:, t, :], mean_var[:, t, 0:1], rstd[:, t:t + 1],
                                          ALU.subtract, ALU.mult).then_inc(xn_done, 1)

            def low_parts(phase, name, count, hi, lo, bias=None, rows=slice(0, P)):
                for i in range(count):
                    u = first_unit[(*phase, name)] + i
                    dve.wait_ge(hi_done, first_hi[(*phase, name)] + i + 1)
                    bank = BANK[u % NBANK][rows, :]
                    if bias is None:
                        dve.tensor_tensor(lo(i), bank, hi(i).bitcast(F32), ALU.subtract).then_inc(bank_free, 1)
                    else:
                        dve.scalar_tensor_tensor(out=lo(i), in0=bank, scalar=bias(i), in1=hi(i).bitcast(F32),
                                                 op0=ALU.add, op1=ALU.subtract).then_inc(bank_free, 1)

            def attention(kind, layer):
                phase = (kind, layer)

                def values_out(first, at):
                    for i in range(NB):
                        dve.wait_ge(product, first + i + 1)
                        for t in range(2):
                            bank = BANK[(first + i) % NBANK][:, t * E:(t + 1) * E].rearrange("p (h d) -> p h d", h=H)
                            dst = values[:, 2 * (at + i) + t, :, 0:D]
                            if layer == 0:
                                op = dve.tensor_copy(dst, bank)
                            else:
                                op = dve.tensor_tensor(dst, bank, bias_rows[:, 2, :].rearrange("p (h d) -> p h d", h=H), ALU.add)
                        op.then_inc(bank_free, 1)

                low_parts(phase, "T", KC * NB, turned(xT, 0, order_of[phase]), turned(xT, 1, order_of[phase]))
                if layer == 0:
                    dve.wait_ge(slopes_ready, 1)
                    dve.tensor_tensor(slope_lo[:, :], slope_raw[:, :], slope_hi[:, :].bitcast(F32), ALU.subtract)\
                        .then_inc(slopes_ready, 1)
                for name in PROJECTIONS[layer]:
                    if name in STAGED:
                        bias = None if layer == 0 else bias_col("q" if name[0] == "Q" else "upk", int(name[1]))
                        low_parts(phase, name, NB, staged(layer, name, part_hi), staged(layer, name, part_lo), bias)
                    elif name in ("V0", "V1"):
                        values_out(first_unit[kind, layer, name], int(name[1]) * NB)
                    elif name in ("VM", "KM"):
                        low_parts(phase, name, 2 * NB, in_block(mid, 0), in_block(mid, 1), bias_col(name[0].lower()))
                    else:
                        rows = LAT_OF[name]
                        low_parts(phase, name, NB, in_lat(name, 0), in_lat(name, 1),
                                  bias_col(name[0].lower() + "l", 0, rows), rows)
                dve.wait_ge(product, first_unit[kind, layer, "core"])
                dve.wait_ge(bank_free, first_unit[kind, layer, "core"])
                dve.wait_ge(g_split, 2)
                if layer == 0:
                    dve.wait_ge(ident_ready, 2)
                masked_at = []
                begun = set()
                for item in plan:
                    if item[0] == "max":
                        _, g, h, t, c = item
                        b, n = t // TPB, min(QB, P * (t + 1) - QB * c)
                        bn = block_no(layer, g, b)
                        mu = layer * MU + mu_of[item]
                        slot = bn % 2
                        if bn not in begun:
                            begun.add(bn)
                            if bn >= 2:
                                dve.wait_ge(neg_done, bn - 1)
                        bank = max_banks[mu % NMAX]
                        dve.wait_ge(max_product, mu + 1)
                        to = chunk_max[:, slot, h, t % TPB, c:c + 1]
                        if c == b:
                            k = len(masked_at)
                            if k >= 2:
                                dve.wait_ge(max_free, masked_at[k - 2] + 1)
                            dve.tensor_tensor_reduce(masked[k % 2][:, 0:n], bank[:, 0:n], diag_mask[:, QB - n:QB],
                                                     1.0, VLOW, ALU.add, ALU.max, to).then_inc(max_free, 1)
                            masked_at.append(mu)
                        else:
                            dve.tensor_reduce(to, bank[:, 0:n], AX.X, ALU.max).then_inc(max_free, 1)
                        if t % TPB == TPB - 1 and h == GH - 1 and c == b:
                            dve.wait_ge(max_free, mu + 1)
                            if bn >= 2:
                                last = BLOCKS[(bn - 2) % len(BLOCKS)]
                                base = (bn - 2) // len(BLOCKS) * MU
                                dve.wait_ge(max_product, base + mu_of[("turn", *last)] + 1)
                            dve.tensor_reduce(neg_max[:, slot, :, :], chunk_max[:, slot, :, :, 0:b + 1], AX.X, ALU.max,
                                              negate=True).then_inc(neg_done, 1)
                    elif item[0] == "turn":
                        _, g, b = item
                        n = block_no(layer, g, b)
                        mu = layer * MU + mu_of[item]
                        bank = max_banks[mu % NMAX][0:GH * TPB, 0:P]
                        dve.wait_ge(max_product, mu + 1)
                        if n >= 2:
                            dve.wait_ge(neg_in, 64 * (n - 1))
                        dve.tensor_copy(neg_hi[:, n % 2, :], bank).then_inc(neg_high, 1)
                        dve.wait_ge(neg_high, n + 1)
                        dve.tensor_tensor(neg_lo[:, n % 2, :], bank, neg_hi[:, n % 2, :].bitcast(F32), ALU.subtract)\
                            .then_inc(max_free, 1)
                    elif item[0] == "ctx":
                        _, g, b = item
                        n = block_no(layer, g, b)
                        mu = layer * MU + mu_of[item]
                        dve.wait_ge(max_product, mu + 1)
                        if n >= 2:
                            dve.wait_ge(inv_done, n - 1)
                        bank = max_banks[mu % NMAX][:, :].rearrange("p (t r) -> p t r", r=2 * D)
                        dve.reciprocal(inv_den[:, n % 2, :], bank[:, :, D]).then_inc(inv_done, 1)
                        dve.wait_ge(inv_done, n + 1)
                        out = context[:, b * TPB:(b + 1) * TPB, g * GH * D:(g + 1) * GH * D]
                        inv = inv_den[:, n % 2, :].rearrange("p (t h o) -> p t h o", h=GH, o=1)
                        dve.tensor_tensor(out.rearrange("p t (h d) -> p t h d", h=GH),
                                          bank[:, :, 0:D].rearrange("p (t h) d -> p t h d", h=GH),
                                          inv.broadcast_to([P, TPB, GH, D]), ALU.mult).then_inc(max_free, 1)
                    elif item[0] == "turn_ctx":
                        _, b, k = item
                        i = b * KC + k
                        mu = layer * MU + mu_of[item]
                        dve.wait_ge(ctx_high, layer * KC * NB + DOWN.index(b) * KC + k + 1)
                        dve.tensor_tensor(turned(contextT, 1)(i), max_banks[mu % NMAX][:, :],
                                          turned(contextT, 0)(i).bitcast(F32), ALU.subtract).then_inc(max_free, 1)
                    elif item[0] == "project":
                        i = item[1]
                        mu = layer * MU + mu_of[item]
                        dve.wait_ge(max_product, mu + 1)
                        dve.wait_ge(bias_added, layer + 1)
                        pair = x[:, 2 * i:2 * i + 2, :]
                        dve.tensor_tensor(pair, max_banks[mu % NMAX][:, :].rearrange("p (t e) -> p t e", t=2), pair, ALU.add)\
                            .then_inc(max_free, 1)
                        if i % 2:
                            dve.wait_ge(max_free, mu + 1)
                            statistics(phase, i // 2)
                            normalise(phase, i // 2)

            for b in range(NB):
                dve.wait_ge(x_in[b], 16)
                statistics(None, b)
                normalise(None, b)
            for kind, n in phases:
                if kind != "f":
                    attention(kind, n)
                else:
                    experts_dve(dve, n, statistics, normalise, low_parts)


_INPUTS = ("x", "w_a", "w_a_post", "w_b", "w_b_post", "bias_cols", "bias_rows", "slopes", "router", "experts")


def lay_out(L):
    def chunks(w):
        return w.reshape(KC, P, -1).transpose(1, 0, 2).reshape(P, -1)

    def top(w):
        return np.concatenate([w, np.zeros_like(w)], 0)

    def bottom(w):
        return np.concatenate([np.zeros_like(w), w], 0)

    a = {k[len("L0_attn_a_"):]: np.asarray(v) for k, v in L.items() if k.startswith("L0_attn_a_")}
    b = {k[len("L0_attn_b_"):]: np.asarray(v) for k, v in L.items() if k.startswith("L0_attn_b_")}
    f = {k[len("L0_ffn_"):]: np.asarray(v) for k, v in L.items() if k.startswith("L0_ffn_")}
    up = {n: b[f"up{n}_w"].transpose(1, 0, 2).reshape(DL, E) for n in "kv"}
    w_a = np.concatenate([chunks(a["Wq"]), chunks(a["Wk"]), chunks(a["Wv"])], 1)
    w_b = np.concatenate([chunks(b["wq_w"]), chunks(b["wk_w"]), chunks(b["wv_w"]), chunks(bottom(b["wkl_w"].T).T),
                          chunks(b["wvl_w"]), bottom(up["k"]), top(up["v"])], 1)
    bias_cols = np.stack([b["wq_b"][0:P], b["wq_b"][P:E], b["wk_b"][0:P], b["wk_b"][P:E], b["wv_b"][0:P], b["wv_b"][P:E],
                          b["upk_b"].reshape(E)[0:P], b["upk_b"].reshape(E)[P:E], bottom(b["wkl_b"]), top(b["wvl_b"])], 1)
    bias_rows = np.stack([a["bo"], b["wo_b"], b["upv_b"].reshape(E)])
    slope = (2.0 ** (-8.0 * np.arange(1, H + 1) / H)).astype(np.float32)
    slope = slope.reshape(G, GH // 2, 2).transpose(0, 2, 1).reshape(H)
    slopes = slope[:, None] * (np.arange(S) - S // 2).astype(np.float32)[None, :]
    router = chunks(np.concatenate([f["gate_w"], f["sh_gate1_w"], np.zeros_like(f["sh_gate1_w"])], 0).T)
    pad = np.zeros((1, EI, E), np.float32)
    gate = np.concatenate([f["gu_w"][:, 0:EI], f["sh_gate_w"][None], f["sh_up_w"][None]], 0)
    upw = np.concatenate([f["gu_w"][:, EI:], pad, pad], 0)
    down = np.concatenate([f["dp_w"].transpose(0, 2, 1), f["sh_down_w"].T[None], pad], 0)
    gu = np.stack([gate.reshape(PAIRS + 1, P, KC, P), upw.reshape(PAIRS + 1, P, KC, P)], 0)
    gu = gu.transpose(1, 4, 3, 0, 2).reshape(PAIRS + 1, P, KC * 2 * P)
    experts = np.concatenate([gu, down.reshape(PAIRS + 1, P, E)], 2)
    return {"x": a["x"].reshape(S, E), "w_a": w_a, "w_a_post": chunks(a["Wo"]), "w_b": w_b, "w_b_post": chunks(b["wo_w"]),
            "bias_cols": bias_cols, "bias_rows": bias_rows, "slopes": slopes.reshape(P, -1), "router": router,
            "experts": experts}


def kernel(**inputs):
    import concourse.bacc as bacc
    from concourse.bass_utils import run_bass_kernel_spmd

    nc = bacc.Bacc("TRN2", target_bir_lowering=False, num_devices=1)
    laid = lay_out(inputs)
    arrays, aps = {}, {}
    for name in _INPUTS:
        array = np.ascontiguousarray(laid[name])
        arrays[f"in_{name}"] = array
        aps[name] = nc.dram_tensor(f"in_{name}", array.shape, mybir.dt.from_np(array.dtype), kind="ExternalInput").ap()
    aps["out"] = nc.dram_tensor("result", (S, E), F32, kind="ExternalOutput").ap()
    build(nc, aps)
    got = run_bass_kernel_spmd(nc, [arrays], core_ids=[0])
    return got.results[0]["result"].reshape(1, S, E)
```
